# Optimizing a Trainium2 kernel written in Bass

```python
import numpy as np
import jax
import jax.numpy as jnp

def _softmax(x, axis=-1):
    return jax.nn.softmax(x, axis=axis)

def _gelu(x):
    return jax.nn.gelu(x, approximate=True)

def _silu(x):
    return jax.nn.silu(x)

def _sigmoid(x):
    return jax.nn.sigmoid(x)

def _layernorm(x, axis=-1, eps=1e-05):
    m = jnp.mean(x, axis=axis, keepdims=True)
    v = jnp.var(x, axis=axis, keepdims=True)
    return (x - m) / jnp.sqrt(v + eps)

def _scatter_add(tgt, idx, src, axis=0):
    return tgt.at[idx].add(src)

def _segment_sum(src, seg, n):
    return jax.ops.segment_sum(src, seg, n)
kernel_name = 'mk_xattn_ffn_d2_seqx_r8_6ba799'

def setup_inputs(seed: int=0):
    np.random.seed(seed)
    _w = jnp.asarray

    def _rec_inputs():
        import jax
        import jax.numpy as jnp
        _rk = jax.random.key(seed)
        x = 4.136e-05 + 0.9999 * jax.random.normal(jax.random.fold_in(_rk, 1), (4, 256, 256), jnp.float32)
        _lenS = 256 - jax.random.randint(jax.random.fold_in(_rk, 7), (4,), 0, max(1, 256 // 4) + 1, jnp.int32)
        _lenS2 = 256 - jax.random.randint(jax.random.fold_in(_rk, 8), (4,), 0, max(1, 256 // 4) + 1, jnp.int32)
        _ctx_1024P = jax.random.normal(jax.random.fold_in(_rk, 11), (4, 16, 128), jnp.float32)
        _ctx_1024c = jax.random.dirichlet(jax.random.fold_in(_rk, 511), 0.3 * jnp.ones((16,), jnp.float32), (4, 256))
        _ctx_1024t = jnp.einsum('bsk,bkd->bsd', _ctx_1024c, _ctx_1024P)
        _ctx_1024t = _ctx_1024t * jax.lax.rsqrt(jnp.mean(jnp.square(_ctx_1024t)) + 1e-12) * 0.953939
        ctx_1024 = -0.000292821 + 1.00034 * (_ctx_1024t + 0.3 * jax.random.normal(jax.random.fold_in(_rk, 611), (4, 256, 128), jnp.float32))
        fside_BxSx2_0 = jax.random.uniform(jax.random.fold_in(_rk, 12), (4, 256, 2), jnp.float32, 0.0, 0.999707)
        return (x, ctx_1024, fside_BxSx2_0)
    x, ctx_1024, fside_BxSx2_0 = _rec_inputs()

    def _L0_xattn_setup():
        import jax, jax.numpy as jnp
        import numpy as np
        import math
        B, L, DM = (2, 256, 128)
        DS, DC, EXP = (16, 4, 2)
        DI = EXP * DM
        DR = math.ceil(DM / 16)
        DT_MIN, DT_MAX, DT_FLOOR = (0.001, 0.1, 0.0001)

        def _ssm_forward(hidden_states, z, in_proj_w, conv_w, conv_b, x_proj_w, dt_proj_w, dt_proj_b, A_log, D):
            b = hidden_states.shape[0]
            x = jnp.einsum('ed,bld->bel', in_proj_w, hidden_states)
            xp = jnp.pad(x, ((0, 0), (0, 0), (DC - 1, 0)))
            xc = jax.lax.conv_general_dilated(xp, conv_w[:, None, :], window_strides=(1,), padding='VALID', dimension_numbers=('NCH', 'OIH', 'NCH'), feature_group_count=DI)
            u = jax.nn.silu(xc + conv_b[None, :, None])
            x_dbl = jnp.einsum('ke,bel->bkl', x_proj_w, u)
            dt_lo = x_dbl[:, :DR]
            Bm = x_dbl[:, DR:DR + DS]
            Cm = x_dbl[:, DR + DS:]
            delta = jax.nn.softplus(jnp.einsum('er,brl->bel', dt_proj_w, dt_lo) + dt_proj_b[None, :, None])
            A = -jnp.exp(A_log)

            def step(state, xs):
                d_t, B_t, C_t, u_t = xs
                dA = jnp.exp(d_t[..., None] * A)
                state = state * dA + (d_t * u_t)[..., None] * B_t[:, None, :]
                y_t = jnp.einsum('ben,bn->be', state, C_t)
                return (state, y_t)
            xs = (jnp.moveaxis(delta, -1, 0), jnp.moveaxis(Bm, -1, 0), jnp.moveaxis(Cm, -1, 0), jnp.moveaxis(u, -1, 0))
            state0 = jnp.zeros((b, DI, DS), delta.dtype)
            _, ys = jax.lax.scan(step, state0, xs)
            y = jnp.moveaxis(ys, 0, -1)
            y = y + D[None, :, None] * u
            y = y * jax.nn.silu(z)
            return jnp.swapaxes(y, 1, 2)
        key = jax.random.key(seed)
        ks = jax.random.split(key, 8)
        hidden_states = jax.random.normal(ks[0], (B, L, DM), jnp.float32)
        z = jax.random.normal(ks[1], (B, DI, L), jnp.float32)
        in_proj_w = jax.random.normal(ks[2], (DI, DM), jnp.float32) * DM ** (-0.5)
        conv_w = jax.random.normal(ks[3], (DI, DC), jnp.float32) * DC ** (-0.5)
        conv_b = jnp.zeros((DI,), jnp.float32)
        x_proj_w = jax.random.normal(ks[4], (DR + 2 * DS, DI), jnp.float32) * DI ** (-0.5)
        dt_std = DR ** (-0.5)
        dt_proj_w = jax.random.uniform(ks[5], (DI, DR), jnp.float32, -dt_std, dt_std)
        dt = jnp.exp(jax.random.uniform(ks[6], (DI,), jnp.float32) * (math.log(DT_MAX) - math.log(DT_MIN)) + math.log(DT_MIN))
        dt = jnp.clip(dt, DT_FLOOR)
        dt_proj_b = dt + jnp.log(-jnp.expm1(-dt))
        A_log = jnp.log(jnp.broadcast_to(jnp.arange(1, DS + 1, dtype=jnp.float32), (DI, DS)))
        D = jnp.ones((DI,), jnp.float32)
        return dict(hidden_states=hidden_states, z=z, in_proj_w=in_proj_w, conv_w=conv_w, conv_b=conv_b, x_proj_w=x_proj_w, dt_proj_w=dt_proj_w, dt_proj_b=dt_proj_b, A_log=A_log, D=D)
    _L0_xattn_all = _L0_xattn_setup()
    _L0_xattn_in = {k: v for k, v in _L0_xattn_all.items() if k in ('in_proj_w', 'conv_w', 'conv_b', 'x_proj_w', 'dt_proj_w', 'dt_proj_b', 'A_log', 'D')}
    del _L0_xattn_all

    def _L0_ffn_setup():
        import jax, jax.numpy as jnp
        import numpy as np
        SEQ, BS, D, F, E = (128, 2, 256, 256, 8)
        key = jax.random.key(seed)
        ks = jax.random.split(key, 8)
        s = 0.02
        return {'hidden_states': jax.random.normal(ks[0], (SEQ, BS, D), jnp.float32), 'router_w': jax.random.normal(ks[1], (D, E), jnp.float32) * s, 'gate_w': jax.random.normal(ks[2], (E, D, F), jnp.float32) * s, 'up_w': jax.random.normal(ks[3], (E, D, F), jnp.float32) * s, 'down_w': jax.random.normal(ks[4], (E, F, D), jnp.float32) * s, 'shared_gate_w': jax.random.normal(ks[5], (D, F), jnp.float32) * s, 'shared_up_w': jax.random.normal(ks[6], (D, F), jnp.float32) * s, 'shared_down_w': jax.random.normal(ks[7], (F, D), jnp.float32) * s}
    _L0_ffn_all = _L0_ffn_setup()
    _L0_ffn_in = {k: v for k, v in _L0_ffn_all.items() if k in ('router_w', 'gate_w', 'up_w', 'down_w', 'shared_gate_w', 'shared_up_w', 'shared_down_w')}
    del _L0_ffn_all

    def _L1_xattn_setup():
        import jax, jax.numpy as jnp
        import numpy as np
        DIM = 256
        CTX_DIM = 128
        N_HEADS = 32
        HEAD_DIM = DIM // N_HEADS
        POS_DIM = 2
        B, N, CTXN = (2, 256, 256)
        ROPE_BASE = 10000.0

        def apply_axial_rope(x, pos):
            b, n, h, d = x.shape
            p = pos.shape[-1]
            dpa = d // p
            half = dpa // 2
            freqs = ROPE_BASE ** (-jnp.arange(half, dtype=x.dtype) / half)
            ang = pos[..., :, None] * freqs
            cos = jnp.cos(ang)[:, :, None, :, :]
            sin = jnp.sin(ang)[:, :, None, :, :]
            xr = x.reshape(b, n, h, p, half, 2)
            x1, x2 = (xr[..., 0], xr[..., 1])
            out = jnp.stack([x1 * cos - x2 * sin, x1 * sin + x2 * cos], axis=-1)
            return out.reshape(b, n, h, d)
        key = jax.random.key(seed)
        ks = jax.random.split(key, 8)
        x = jax.random.normal(ks[0], (B, N, DIM), jnp.float32)
        ctx = jax.random.normal(ks[1], (B, CTXN, CTX_DIM), jnp.float32)
        pos_map = jax.random.uniform(ks[2], (B, N, POS_DIM), jnp.float32)
        ctx_pos_map = jax.random.uniform(ks[3], (B, CTXN, POS_DIM), jnp.float32)
        Wq = jax.random.normal(ks[4], (DIM, DIM), jnp.float32) / np.sqrt(DIM)
        Wkv = jax.random.normal(ks[5], (CTX_DIM, 2 * DIM), jnp.float32) / np.sqrt(CTX_DIM)
        Wout = jax.random.normal(ks[6], (DIM, DIM), jnp.float32) / np.sqrt(DIM)
        bout = jnp.zeros((DIM,), jnp.float32)
        return {'x': x, 'ctx': ctx, 'pos_map': pos_map, 'ctx_pos_map': ctx_pos_map, 'Wq': Wq, 'Wkv': Wkv, 'Wout': Wout, 'bout': bout}
    _L1_xattn_all = _L1_xattn_setup()
    _L1_xattn_in = {k: v for k, v in _L1_xattn_all.items() if k in ('Wq', 'Wkv', 'Wout', 'bout')}
    del _L1_xattn_all

    def _L1_ffn_setup():
        import jax, jax.numpy as jnp
        import numpy as np
        RANK = 64
        SCALING = 1.0 / RANK
        TEMPERATURE = 1.0
        key = jax.random.key(seed)
        k_x, k_a, k_b, k_w = jax.random.split(key, 4)
        B_, S, D = (4, 256, 256)
        E, R, O = (8, RANK, 256)
        x = jax.random.normal(k_x, (B_, S, D), dtype=jnp.float32)
        A = jax.random.normal(k_a, (E, R, D), dtype=jnp.float32) * (1.0 / np.sqrt(D))
        Bw = jax.random.normal(k_b, (E, O, R), dtype=jnp.float32) * 0.02
        Wr = jax.random.normal(k_w, (E, D), dtype=jnp.float32) * (1.0 / np.sqrt(D))
        br = jnp.zeros((E,), dtype=jnp.float32)
        return {'x': x, 'A': A, 'B': Bw, 'Wr': Wr, 'br': br}
    _L1_ffn_all = _L1_ffn_setup()
    _L1_ffn_in = {k: v for k, v in _L1_ffn_all.items() if k in ('A', 'B', 'Wr', 'br')}
    del _L1_ffn_all
    return {'x': x, 'ctx_1024': ctx_1024, 'fside_BxSx2_0': fside_BxSx2_0, 'L0_xattn_in_proj_w': _L0_xattn_in['in_proj_w'], 'L0_xattn_conv_w': _L0_xattn_in['conv_w'], 'L0_xattn_conv_b': _L0_xattn_in['conv_b'], 'L0_xattn_x_proj_w': _L0_xattn_in['x_proj_w'], 'L0_xattn_dt_proj_w': _L0_xattn_in['dt_proj_w'], 'L0_xattn_dt_proj_b': _L0_xattn_in['dt_proj_b'], 'L0_xattn_A_log': _L0_xattn_in['A_log'], 'L0_xattn_D': _L0_xattn_in['D'], 'L0_ffn_router_w': _L0_ffn_in['router_w'], 'L0_ffn_gate_w': _L0_ffn_in['gate_w'], 'L0_ffn_up_w': _L0_ffn_in['up_w'], 'L0_ffn_down_w': _L0_ffn_in['down_w'], 'L0_ffn_shared_gate_w': _L0_ffn_in['shared_gate_w'], 'L0_ffn_shared_up_w': _L0_ffn_in['shared_up_w'], 'L0_ffn_shared_down_w': _L0_ffn_in['shared_down_w'], 'L1_xattn_Wq': _L1_xattn_in['Wq'], 'L1_xattn_Wkv': _L1_xattn_in['Wkv'], 'L1_xattn_Wout': _L1_xattn_in['Wout'], 'L1_xattn_bout': _L1_xattn_in['bout'], 'L1_ffn_A': _L1_ffn_in['A'], 'L1_ffn_B': _L1_ffn_in['B'], 'L1_ffn_Wr': _L1_ffn_in['Wr'], 'L1_ffn_br': _L1_ffn_in['br']}

def reference(x, ctx_1024, fside_BxSx2_0, L0_xattn_in_proj_w, L0_xattn_conv_w, L0_xattn_conv_b, L0_xattn_x_proj_w, L0_xattn_dt_proj_w, L0_xattn_dt_proj_b, L0_xattn_A_log, L0_xattn_D, L0_ffn_router_w, L0_ffn_gate_w, L0_ffn_up_w, L0_ffn_down_w, L0_ffn_shared_gate_w, L0_ffn_shared_up_w, L0_ffn_shared_down_w, L1_xattn_Wq, L1_xattn_Wkv, L1_xattn_Wout, L1_xattn_bout, L1_ffn_A, L1_ffn_B, L1_ffn_Wr, L1_ffn_br):
    import jax
    import jax.numpy as jnp

    def _L0_xattn_ref(hidden_states, z, in_proj_w, conv_w, conv_b, x_proj_w, dt_proj_w, dt_proj_b, A_log, D):
        import jax, jax.numpy as jnp
        import numpy as np
        import math
        B, L, DM = (2, 256, 128)
        DS, DC, EXP = (16, 4, 2)
        DI = EXP * DM
        DR = math.ceil(DM / 16)
        DT_MIN, DT_MAX, DT_FLOOR = (0.001, 0.1, 0.0001)

        def _ssm_forward(hidden_states, z, in_proj_w, conv_w, conv_b, x_proj_w, dt_proj_w, dt_proj_b, A_log, D):
            b = hidden_states.shape[0]
            x = jnp.einsum('ed,bld->bel', in_proj_w, hidden_states)
            xp = jnp.pad(x, ((0, 0), (0, 0), (DC - 1, 0)))
            xc = jax.lax.conv_general_dilated(xp, conv_w[:, None, :], window_strides=(1,), padding='VALID', dimension_numbers=('NCH', 'OIH', 'NCH'), feature_group_count=DI)
            u = jax.nn.silu(xc + conv_b[None, :, None])
            x_dbl = jnp.einsum('ke,bel->bkl', x_proj_w, u)
            dt_lo = x_dbl[:, :DR]
            Bm = x_dbl[:, DR:DR + DS]
            Cm = x_dbl[:, DR + DS:]
            delta = jax.nn.softplus(jnp.einsum('er,brl->bel', dt_proj_w, dt_lo) + dt_proj_b[None, :, None])
            A = -jnp.exp(A_log)

            def step(state, xs):
                d_t, B_t, C_t, u_t = xs
                dA = jnp.exp(d_t[..., None] * A)
                state = state * dA + (d_t * u_t)[..., None] * B_t[:, None, :]
                y_t = jnp.einsum('ben,bn->be', state, C_t)
                return (state, y_t)
            xs = (jnp.moveaxis(delta, -1, 0), jnp.moveaxis(Bm, -1, 0), jnp.moveaxis(Cm, -1, 0), jnp.moveaxis(u, -1, 0))
            state0 = jnp.zeros((b, DI, DS), delta.dtype)
            _, ys = jax.lax.scan(step, state0, xs)
            y = jnp.moveaxis(ys, 0, -1)
            y = y + D[None, :, None] * u
            y = y * jax.nn.silu(z)
            return jnp.swapaxes(y, 1, 2)
        return _ssm_forward(hidden_states, z, in_proj_w, conv_w, conv_b, x_proj_w, dt_proj_w, dt_proj_b, A_log, D)

    def _L0_ffn_ref(hidden_states, router_w, gate_w, up_w, down_w, shared_gate_w, shared_up_w, shared_down_w):
        import jax, jax.numpy as jnp
        import numpy as np
        SEQ, BS, D, F, E = (128, 2, 256, 256, 8)
        S, B, Dm = hidden_states.shape
        x = hidden_states.reshape(-1, Dm)
        logits = x @ router_w
        expert_idx = jnp.argmax(logits, axis=-1)
        score = jax.nn.sigmoid(jnp.max(logits, axis=-1))
        xs = x * score[:, None]
        n_experts = router_w.shape[1]
        out = jnp.zeros_like(x)
        for e in range(n_experts):
            m = (expert_idx == e)[:, None]
            xe = jnp.where(m, xs, 0.0)
            h = jax.nn.silu(xe @ gate_w[e]) * (xe @ up_w[e])
            out = out + jnp.where(m, h @ down_w[e], 0.0)
        shared = jax.nn.silu(x @ shared_gate_w) * (x @ shared_up_w) @ shared_down_w
        return (out + shared).reshape(S, B, Dm)

    def _L1_xattn_ref(x, ctx, pos_map, ctx_pos_map, Wq, Wkv, Wout, bout):
        import jax, jax.numpy as jnp
        import numpy as np
        DIM = 256
        CTX_DIM = 128
        N_HEADS = 32
        HEAD_DIM = DIM // N_HEADS
        POS_DIM = 2
        B, N, CTXN = (2, 256, 256)
        ROPE_BASE = 10000.0

        def apply_axial_rope(x, pos):
            b, n, h, d = x.shape
            p = pos.shape[-1]
            dpa = d // p
            half = dpa // 2
            freqs = ROPE_BASE ** (-jnp.arange(half, dtype=x.dtype) / half)
            ang = pos[..., :, None] * freqs
            cos = jnp.cos(ang)[:, :, None, :, :]
            sin = jnp.sin(ang)[:, :, None, :, :]
            xr = x.reshape(b, n, h, p, half, 2)
            x1, x2 = (xr[..., 0], xr[..., 1])
            out = jnp.stack([x1 * cos - x2 * sin, x1 * sin + x2 * cos], axis=-1)
            return out.reshape(b, n, h, d)
        b, n, _ = x.shape
        ctx_n = ctx.shape[1]
        q = (x @ Wq).reshape(b, n, N_HEADS, HEAD_DIM)
        k, v = jnp.split(ctx @ Wkv, 2, axis=-1)
        k = k.reshape(b, ctx_n, N_HEADS, HEAD_DIM)
        v = v.reshape(b, ctx_n, N_HEADS, HEAD_DIM)
        q = apply_axial_rope(q, pos_map)
        k = apply_axial_rope(k, ctx_pos_map)
        scale = 1.0 / np.sqrt(HEAD_DIM).astype(np.float32)
        logits = jnp.einsum('bqhd,bkhd->bhqk', q, k) * scale
        w = jax.nn.softmax(logits, axis=-1)
        attn = jnp.einsum('bhqk,bkhd->bqhd', w, v)
        attn = attn.reshape(b, n, N_HEADS * HEAD_DIM)
        return attn @ Wout + bout

    def _L1_ffn_ref(x, A, B, Wr, br):
        import jax, jax.numpy as jnp
        import numpy as np
        RANK = 64
        SCALING = 1.0 / RANK
        TEMPERATURE = 1.0
        batch, seq, d = x.shape
        E, out_dim = (B.shape[0], B.shape[1])
        x_flat = x.reshape(-1, d)
        logits = (x_flat @ Wr.T + br) / TEMPERATURE
        probs = jax.nn.softmax(logits, axis=-1)
        expert_idx = jnp.argmax(probs, axis=-1)
        expert_weight = jnp.max(probs, axis=-1)
        h = jnp.einsum('nd,erd->ner', x_flat, A)
        y = jnp.einsum('ner,eor->neo', h, B) * SCALING
        sel = jnp.take_along_axis(y, expert_idx[:, None, None], axis=1)[:, 0, :]
        out_flat = sel * expert_weight[:, None]
        return out_flat.reshape(batch, seq, out_dim)
    x = x + _L0_xattn_ref(ctx_1024, _layernorm(x, axis=-1), L0_xattn_in_proj_w, L0_xattn_conv_w, L0_xattn_conv_b, L0_xattn_x_proj_w, L0_xattn_dt_proj_w, L0_xattn_dt_proj_b, L0_xattn_A_log, L0_xattn_D)
    x = x + _L0_ffn_ref(_layernorm(x, axis=-1), L0_ffn_router_w, L0_ffn_gate_w, L0_ffn_up_w, L0_ffn_down_w, L0_ffn_shared_gate_w, L0_ffn_shared_up_w, L0_ffn_shared_down_w)
    x = x + _L1_xattn_ref(_layernorm(x, axis=-1), ctx_1024, fside_BxSx2_0, fside_BxSx2_0, L1_xattn_Wq, L1_xattn_Wkv, L1_xattn_Wout, L1_xattn_bout)
    x = x + _L1_ffn_ref(_layernorm(x, axis=-1), L1_ffn_A, L1_ffn_B, L1_ffn_Wr, L1_ffn_br)
    return x

_drawn_inputs = setup_inputs


def setup_inputs(seed=0):
    import zlib

    import numpy as np

    out = dict(_drawn_inputs(seed))
    spreads = {'L0_xattn_conv_b': (0.0, 0.1),
     'L0_xattn_D': (1.0, 0.2),
     'L1_xattn_bout': (0.0, 0.8),
     'L1_ffn_br': (0.0, 2.0)}
    factors = {'L0_xattn_dt_proj_w': 6.925,
     'L0_xattn_dt_proj_b': 2.87,
     'L0_ffn_router_w': 8.0,
     'L0_ffn_gate_w': 8.0,
     'L0_ffn_up_w': 8.0,
     'L0_ffn_down_w': 8.0,
     'L0_ffn_shared_gate_w': 4.014,
     'L0_ffn_shared_up_w': 3.953,
     'L0_ffn_shared_down_w': 3.955,
     'L1_ffn_A': 33.821,
     'L1_ffn_B': 33.944,
     'L1_ffn_Wr': 36.407,
     'fside_BxSx2_0': 8.0,
     'L1_xattn_Wq': 2.783}
    for name, (base, spread) in spreads.items():
        noise = np.random.default_rng([zlib.crc32(name.encode()), seed]).standard_normal(out[name].shape)
        drawn = base * np.exp(spread * noise) if base else spread * noise
        out[name] = jnp.asarray(drawn.astype(out[name].dtype))
    for name, factor in factors.items():
        out[name] = (out[name] * factor).astype(out[name].dtype)
    return out
```

```python
import math
from contextlib import ExitStack

import concourse.bass as bass
from concourse import mybir

F32 = mybir.dt.float32
F32R = mybir.dt.float32r
BF16 = mybir.dt.bfloat16
I32 = mybir.dt.int32
ALU = mybir.AluOpType
ACT = mybir.ActivationFunctionType
AX = mybir.AxisListType

P = 128
NB, L, DM = 4, 256, 256
DC = 128
TOK = NB * L
NT = TOK // P
KT = DM // P
DS, TAPS, DR = 16, 4, 8
LN_EPS = 1e-5
HALF = 512
NE, F = 8, 256
NS = TOK // P + NE


NH, HD = 32, 8
G = 4
NG = NB * NH // G
ROWS = 32
SLOTS = 4
SPLIT = 3 * HD
RANK = 64
TWO_PI_HI = 6.28125
TWO_PI_LO = 2 * math.pi - TWO_PI_HI
PI_BELOW = 3.1415925
ROUND = 1.5 * 2.0 ** 23


def wait_from_one(eng, sem, value):
    if not isinstance(value, int) or value > 0:
        eng.wait_ge(sem, value)


class Chain:

    def __init__(self, eng, sem):
        self.eng, self.sem, self.n = eng, sem, 0

    def then_wait(self, ins):
        self.n += 1
        ins.then_inc(self.sem, 1)
        self.eng.wait_ge(self.sem, self.n)


def build(nc, h, out):
    ctx = ExitStack()
    with ctx:
        def sb(name, shape, dt=F32):
            return ctx.enter_context(nc.sbuf_tensor(name, shape, dt))

        def sem(name):
            return ctx.enter_context(nc.semaphore(name))

        ps = ctx.enter_context(nc.psum_tensor("ps", [P, 8, HALF], F32))

        def banks(a, n):
            return ps[:, a:a + n, :].rearrange("p b c -> p (b c)")

        x_tok = sb("x_tok", [P, NT, DM])
        ctxT = sb("ctxT", [P, TOK])
        consts = sb("consts", [P, 2 * P + 64 + G])
        ident, upper = consts[:, 0:P], consts[:, P:2 * P]
        head_rows = consts[:, 2 * P + 64:]
        ident3f = consts[:, 2 * P:2 * P + 32]
        in_w = sb("in_w", [P, DM])
        xp_w = sb("xp_w", [P, KT, 104])
        dt_w = sb("dt_w", [104, DM])
        chan = sb("chan", [P, KT, TAPS + 3 + DS])
        tap_w, conv_b = chan[:, :, 0:TAPS], chan[:, :, TAPS:TAPS + 1]
        dt_b, d_skip = chan[:, :, TAPS + 1:TAPS + 2], chan[:, :, TAPS + 2:TAPS + 3]
        a_log = chan[:, :, TAPS + 3:]
        neg_a = sb("neg_a", [P, KT, DS])
        ident3 = sb("ident3", [96, 32], BF16)
        diag_d = sb("diag_d", [P, KT, P])
        u = sb("u", [P, KT, TOK])
        delta = sb("delta", [P, KT, TOK])
        du = sb("du", [P, KT, TOK])
        gate_z = sb("gate_z", [P, KT, TOK])
        xdbl_all = sb("xdbl", [P, TOK])
        xdbl = xdbl_all[0:104, :]
        bc3 = sb("bc3", [96, TOK], BF16)
        decay = sb("decay", [P, 2, TOK])
        drive = sb("drive", [P, 2, TOK])
        state = sb("state", [P, 2, TOK])
        read = sb("read", [P, 2, TOK])
        c_rows = sb("c_rows", [P, 2, TOK])
        stats = sb("stats", [P, NT, 6])
        mean_var = sb("mean_var", [P, NT, 2])
        ln_var = sb("ln_var", [P, NT])
        rstd = sb("rstd", [P, NT])
        shift = sb("shift", [P, NT])
        eps_col, one_col = sb("eps_col", [P, 1]), sb("one_col", [P, 1])

        col = consts[:, 2 * P + 32:]
        e_minus_8, j_times_128, tile_no = col[:, 0:NE], col[:, NE:2 * NE], col[:, 2 * NE:2 * NE + NS]
        router_w = sb("router_w", [P, KT, NE])
        gu_w = sb("gu_w", [P, NE + 1, KT, 2 * F])
        down_w = sb("down_w", [P, NE + 1, KT, DM])
        upper_bf, ones_bf = sb("upper_bf", [P, P], BF16), sb("ones_bf", [P, P], BF16)
        xn = delta[:].rearrange("p k (t d) -> p (k t) d", d=DM)
        xnT = du
        hidT = drive
        scaled = decay[:].rearrange("p k (t d) -> p (k t) d", d=DM)
        routed = read[:].rearrange("p k (t d) -> p (k t) d", d=DM)
        silu_g = state[:].rearrange("p k (b c) -> p (k b) c", c=HALF)
        zero_rows = c_rows[:].rearrange("p k c -> p (k c)")
        logitT = sb("logitT", [NE, TOK])
        logit = sb("logit", [P, NT, NE])
        top = sb("top", [P, NT])
        pick = sb("pick", [P, NT, NE])
        first_e = sb("first_e", [P, NT])
        onehot = sb("onehot", [P, NT, NE], BF16)
        score = sb("score", [P, NT])
        full_tile = sb("full_tile", [P, NE, NE])
        tiles_e, tiles_upto, zeros8 = sb("tiles_e", [P, NE]), sb("tiles_upto", [P, NE]), sb("zeros8", [P, NE])
        slot_f, slot = sb("slot_f", [P, NT]), sb("slot", [P, NT], I32)
        tile_e, tile_ei = sb("tile_e", [1, NS]), sb("tile_ei", [1, NS], I32)
        tile_cmp = sb("tile_cmp", [1, NS, NE])
        xg = xdbl_all[:, 0:2 * DM].rearrange("p (k d) -> p k d", k=2)
        xgT = xdbl_all[:, 2 * DM:].rearrange("p (k c t) -> p k c t", k=2, c=KT)
        sg = ctxT[:, 0:2 * F].rearrange("p (k f) -> p k f", k=2)
        hid = ctxT[:, 2 * F:].rearrange("p (k f) -> p k f", k=2)
        hT = sb("hT", [P, 2, KT, P])
        yo = sb("yo", [P, 2, DM])
        pos = sb("pos", [P, NT, 2])
        angle, turns = sb("angle", [P, 2, NT, 4]), sb("turns", [P, 2, NT, 4])
        cos8 = sb("cos8", [P, NT, HD])
        sin_pos, sin_neg = sb("sin_pos", [P, NT, 4]), sb("sin_neg", [P, NT, 4])
        q_w, kv_w, out_w = sb("q_w", [P, KT, DM]), sb("kv_w", [P, 2 * DM]), sb("out_w", [P, KT, DM])
        out_b = sb("out_b", [P, DM])
        k_tok = gate_z[:].rearrange("p k (t d) -> p (k t) d", d=DM)
        v_tok = c_rows[:].rearrange("p k (g c) -> p (k g) c", c=2 * G * HD)
        swapped = u[:].rearrange("p k (t d) -> p (k t) d", d=DM)
        q_cos = drive[:].rearrange("p k (t d) -> p (k t) d", d=DM)
        rot = sb("rot", [P, NG, 2, 2 * G * HD])
        stack = gu_w[:, 2:4].rearrange("p e c (m g r) -> p (e c) m g r", g=G, r=ROWS)
        rowsT = [sb(f"rowsT{k}", [P, L], F32R) for k in range(2)]
        keysT = [sb(f"keysT{k}", [P, G, L], F32R) for k in range(SLOTS)]
        queryT = [sb(f"queryT{k}", [P, L], F32R) for k in range(2)]
        current = gu_w[:, 0].rearrange("p c (k n) -> p (c k) n", n=4 * G * HD)
        row_max = sb("row_max", [P, 2, 2, G])
        v_ones = gu_w[:, 4, 0].rearrange("p (k j g r) -> p k j g r", k=2, j=2, g=G)
        prob = [b[:].rearrange("p k (c n) -> p (k c) n", n=HALF) for b in (drive, state)]
        o_sb = gu_w[:, 1].rearrange("p c (k n) -> p (c k) n", n=L)
        inv_sum = sb("inv_sum", [P, 2, G])
        attn = delta
        attnT = decay
        wr_w, br_row = sb("wr_w", [P, KT, NE]), sb("br_row", [P, NE])
        a_w = gate_z[:, 0, :].rearrange("p (k c) -> p k c", k=KT)
        b_w = gate_z[:, 1, :].rearrange("p (k c) -> p k c", k=4)
        weight, pick_w = sb("weight", [P, NT]), sb("pick_w", [P, NT, NE])
        low = drive[:].rearrange("p k (c n) -> p (k c) n", n=HALF)
        lowT = state[:].rearrange("p k (c n) -> p (k c) n", n=HALF)
        sorted_x = nc.dram_tensor("sorted_x", (NS * P, DM), F32, kind="Internal").ap()
        sorted_y = nc.dram_tensor("sorted_y", (NS * P, DM), F32, kind="Internal").ap()

        x_loaded = sem("x_loaded")
        ctx_loaded = sem("ctx_loaded")
        ssm_w_loaded = sem("ssm_w_loaded")
        consts_loaded = sem("consts_loaded")
        out_stored = sem("out_stored")
        dve_own, act_own, pool_own = sem("dve_own"), sem("act_own"), sem("pool_own")
        xin_done = sem("xin_done")
        tap0_done = sem("tap0_done")
        conv_done = sem("conv_done")
        cols_set = sem("cols_set")
        ln0_stats = sem("ln0_stats")
        ln0_rstd = sem("ln0_rstd")
        ln0_shift = sem("ln0_shift")
        u_done = sem("u_done")
        xdbl_done = sem("xdbl_done")
        xdbl_copied = sem("xdbl_copied")
        dt_done = sem("dt_done")
        expa_done = sem("expa_done")
        setup_done = sem("setup_done")
        log_done = sem("log_done")
        delta_done = sem("delta_done")
        bc3_done = sem("bc3_done")
        b_ready, c_ready = sem("b_ready"), sem("c_ready")
        decay_ready = [sem(f"decay_ready{e}") for e in range(KT)]
        drive_done = sem("drive_done")
        scan_done = [sem(f"scan_done{e}") for e in range(KT)]
        c_copied = sem("c_copied")
        read_done = [sem(f"read_done{e}") for e in range(KT)]
        y_added = [sem(f"y_added{e}") for e in range(KT)]
        y_gated = sem("y_gated")
        y_turned = sem("y_turned")
        x1_done = sem("x1_done")
        ffn_w_loaded = sem("ffn_w_loaded")
        zeros_set, sorted_cleared = sem("zeros_set"), sem("sorted_cleared")
        ln_stats, ln_rstd, xn_done = sem("ln_stats"), sem("ln_rstd"), sem("xn_done")
        xn_turned, xnT_even, xnT_odd = sem("xn_turned"), sem("xnT_even"), sem("xnT_odd")
        bf_consts = sem("bf_consts")
        logitT_done, logitT_copied = sem("logitT_done"), sem("logitT_copied")
        logit_turned = sem("logit_turned")
        onehot_done, top_done, exp_top_done = sem("onehot_done"), sem("top_done"), sem("exp_top_done")
        rank_done = sem("rank_done")
        tile_e_done, slot_done, scaled_done = sem("tile_e_done"), sem("slot_done"), sem("scaled_done")
        scattered = sem("scattered")
        shared_gu, shared_silu, shared_hid = sem("shared_gu"), sem("shared_silu"), sem("shared_hid")
        shared_down, shared_added = sem("shared_down"), sem("shared_added")
        xg_loaded = [sem(f"xg_loaded{k}") for k in range(2)]
        xg_turned, xgT_ready = sem("xg_turned"), sem("xgT_ready")
        gu_done, sg_done, hid_done = sem("gu_done"), sem("sg_done"), sem("hid_done")
        hid_turned, hT_ready, down_done = sem("hid_turned"), sem("hT_ready"), sem("down_done")
        yo_ready = sem("yo_ready")
        yo_stored = [sem(f"yo_stored{k}") for k in range(2)]
        gathered = sem("gathered")
        x2_done = sem("x2_done")
        pos_loaded, att_w_loaded, last_w_loaded = sem("pos_loaded"), sem("att_w_loaded"), sem("last_w_loaded")
        angle_done, trig_done, trig_ready = sem("angle_done"), sem("trig_done"), sem("trig_ready")
        kv_done, kv_copied = sem("kv_done"), sem("kv_copied")
        k_rotated, q_done, q_rotated = sem("k_rotated"), sem("q_done"), sem("q_rotated")
        pads_set, built = sem("pads_set"), sem("built")
        stack_turned, rowsT_ready, keysT_ready = sem("stack_turned"), sem("rowsT_ready"), sem("keysT_ready")
        rows_done, max_done, shift_done = sem("rows_done"), sem("max_done"), sem("shift_done")
        query_turned, queryT_ready = sem("query_turned"), sem("queryT_ready")
        cols_done, exp_done, pv_done = sem("cols_done"), sem("exp_done"), sem("pv_done")
        o_copied, o_turned, attn_done = sem("o_copied"), sem("o_turned"), sem("attn_done")
        v_copied = sem("v_copied")
        current_ready = sem("current_ready")
        hi_built = sem("hi_built")
        shift_hi, inv_done = sem("shift_hi"), sem("inv_done")
        bias_added = sem("bias_added")
        attn_turned, attnT_ready, proj_done, x3_done = (sem("attn_turned"), sem("attnT_ready"), sem("proj_done"),
                                                        sem("x3_done"))
        shifted_done, exp_logit_done, pick_w_done = sem("shifted_done"), sem("exp_logit_done"), sem("pick_w_done")
        onehot2_done = sem("onehot2_done")
        low_done, low_masked, low_turned, lowT_ready = (sem("low_done"), sem("low_masked"), sem("low_turned"),
                                                        sem("lowT_ready"))
        last_done, tile_done = sem("last_done"), sem("tile_done")

        xin_ps = [banks(0, 2), banks(2, 2)]
        xdbl_ps = banks(4, 2)[0:104, :]
        dt_ps = xin_ps
        b_ps, c_ps = banks(0, 2), banks(2, 2)
        y_ps = [banks(4, 2), banks(6, 2)]
        turned = banks(0, 4).rearrange("p (t d) -> p t d", t=NT)

        logitT_ps = banks(4, 2)[0:NE, :]
        logit_ps = banks(6, 1)[:, 0:NT * NE].rearrange("p (t e) -> p t e", e=NE)
        rank_ps = banks(7, 1)[:, 0:NT * NE].rearrange("p (t e) -> p t e", e=NE)
        count_ps = banks(7, 1)[:, NT * NE:NT * NE + NE]

        def rotate(eng, x, swap, tiles):
            n = tiles.stop - tiles.start
            pairs = x.rearrange("p t (h c two) -> p t h c two", two=2, c=4)
            outs = swap.rearrange("p t (h c two) -> p t h c two", two=2, c=4)
            for m, sine in ((0, sin_neg), (1, sin_pos)):
                ins = eng.tensor_tensor(outs[:, :, :, :, m], pairs[:, :, :, :, 1 - m],
                                  sine[:, tiles].unsqueeze(2).to_broadcast([P, n, NH, 4]), ALU.mult)
            return ins

        def add_rotated(eng, x_cos, swap, which, c, j):
            def view(x):
                return x.rearrange("p (b j) (g c) -> p b j g c", j=2, c=G * HD)[:, 2 * c:2 * c + 2, j]
            groups = rot[:].rearrange("p (b g) w (j c) -> p b g w j c", b=NB, j=2)
            return eng.tensor_tensor(groups[:, 2 * c:2 * c + 2, :, which, j, :], view(x_cos), view(swap), ALU.add)

        def run_turns(eng, turn):
            lead, tail = 8, NG - SLOTS
            for i in range(-1, lead):
                turn(i, i % SLOTS, lambda n, i=i: 0 <= i + n < NG)
            with eng.Fori(lead // SLOTS, tail // SLOTS) as m:
                for k in range(SLOTS):
                    turn(SLOTS * m + k, k, lambda n: True)
            for i in range(tail, NG + 3):
                turn(i, i % SLOTS, lambda n, i=i: 0 <= i + n < NG)

        block = ctx.enter_context(nc.Block())

        @block.sync
        def _(sp):
            sp.dma_start(pos[:], h["pos"].rearrange("b (l p) c -> p (b l) c", p=P)).then_inc(pos_loaded, 16)
            sp.dma_start(ctxT[:], h["ctxT"]).then_inc(ctx_loaded, 16)
            sp.dma_start(in_w[:], h["in_w"]).then_inc(ctx_loaded, 16)
            sp.dma_start(chan[:], h["chan"].rearrange("(k p) c -> p k c", p=P)).then_inc(ssm_w_loaded, 16)
            sp.dma_start(x_tok[:], h["x"].rearrange("b (l p) d -> p (b l) d", p=P)).then_inc(x_loaded, 16)
            sp.dma_start(consts[:], h["consts"]).then_inc(consts_loaded, 16)
            sp.dma_start(xp_w[:], h["xp_w"].rearrange("(k p) c -> p k c", p=P)).then_inc(ssm_w_loaded, 16)
            sp.dma_start(dt_w[:], h["dt_w"]).then_inc(ssm_w_loaded, 16)
            sp.wait_ge(zeros_set, 1)
            sp.dma_start(sorted_x.rearrange("(p r) d -> p (r d)", p=P)[:, 0:NS // 2 * DM], zero_rows).then_inc(sorted_cleared, 16)
            sp.dma_start(sorted_x.rearrange("(p r) d -> p (r d)", p=P)[:, NS // 2 * DM:], zero_rows).then_inc(sorted_cleared, 16)
            sp.dma_start(router_w[:], h["router_w"].rearrange("(k p) e -> p k e", p=P)).then_inc(ffn_w_loaded, 16)
            sp.dma_start(gu_w[:, NE], h["gu_w"][NE].rearrange("(k p) f -> p k f", p=P)).then_inc(ffn_w_loaded, 16)
            sp.dma_start(down_w[:, NE], h["down_w"][NE].rearrange("(k p) f -> p k f", p=P)).then_inc(ffn_w_loaded, 16)
            for e in range(NE):
                sp.dma_start(gu_w[:, e], h["gu_w"][e].rearrange("(k p) f -> p k f", p=P)).then_inc(ffn_w_loaded, 16)
                sp.dma_start(down_w[:, e], h["down_w"][e].rearrange("(k p) f -> p k f", p=P)).then_inc(ffn_w_loaded, 16)

            sp.dma_start(q_w[:], h["q_w"].rearrange("(k p) c -> p k c", p=P)).then_inc(att_w_loaded, 16)
            sp.dma_start(kv_w[:], h["kv_w"]).then_inc(att_w_loaded, 16)
            sp.dma_start(out_w[:], h["out_w"].rearrange("(k p) c -> p k c", p=P)).then_inc(att_w_loaded, 16)
            sp.dma_start(out_b[:], h["out_b"].to_broadcast([P, DM])).then_inc(att_w_loaded, 16)
            sp.dma_start(wr_w[:], h["wr_w"].rearrange("(k p) c -> p k c", p=P)).then_inc(last_w_loaded, 16)
            sp.dma_start(br_row[:], h["br"].to_broadcast([P, NE])).then_inc(last_w_loaded, 16)

            def load_tile(s, k, first):
                if not first:
                    sp.wait_ge(xg_turned, s - 1)
                sp.dma_start(xg[:, k, :], sorted_x[bass.ds(s * P, P), :]).then_inc(xg_loaded[k], 16)

            sp.wait_ge(scattered, 16 * NT)
            for s in range(2):
                load_tile(s, s, first=True)
            with nc.sync.Fori(1, NS // 2) as i:
                for k in range(2):
                    load_tile(2 * i + k, k, first=False)

            sp.wait_ge(k_rotated, 1)
            sp.dma_start(a_w, h["a_w"].rearrange("(k p) c -> p k c", p=P)).then_inc(last_w_loaded, 16)
            sp.dma_start(b_w, h["b_w"].rearrange("(k p) c -> p k c", p=P)).then_inc(last_w_loaded, 16)
            for t in range(NT):
                sp.wait_ge(tile_done, t + 1)
                sp.dma_start(out.rearrange("b (l p) d -> p (b l) d", p=P)[:, t, :], x_tok[:, t, :]) \
                  .then_inc(out_stored, 16)
            sp.wait_ge(out_stored, 16 * NT)

        @block.tensor
        def _(pe):
            mm = nc.tensor.matmul

            pe.wait_ge(ctx_loaded, 32)
            for et in range(KT):
                for c in range(2):
                    ins = mm(xin_ps[et][:, c * HALF:(c + 1) * HALF], in_w[:, et * P:(et + 1) * P],
                             ctxT[:, c * HALF:(c + 1) * HALF], start=True, stop=True)
                ins.then_inc(xin_done, 1)
            pe.wait_ge(ssm_w_loaded, 48)
            for et in range(KT):
                pe.wait_ge(u_done, et + 1)
                for c in range(2):
                    ins = mm(xdbl_ps[:, c * HALF:(c + 1) * HALF], xp_w[:, et, :],
                             u[:, et, c * HALF:(c + 1) * HALF], start=(et == 0), stop=(et == 1))
            ins.then_inc(xdbl_done, 1)
            pe.wait_ge(xdbl_copied, 1)
            pe.wait_ge(conv_done, 2)
            for et in range(KT):
                for c in range(2):
                    ins = mm(dt_ps[et][:, c * HALF:(c + 1) * HALF], dt_w[:, et * P:(et + 1) * P],
                             xdbl[:, c * HALF:(c + 1) * HALF], start=True, stop=True)
                ins.then_inc(dt_done, 1)
            pe.wait_ge(setup_done, 1)
            pe.wait_ge(bc3_done, 1)
            for et in range(KT):
                for c in range(2):
                    mm(y_ps[et][:, c * HALF:(c + 1) * HALF], diag_d[:, et, :],
                       u[:, et, c * HALF:(c + 1) * HALF], start=True, stop=False, skip_group_check=True)

            def spread_b(n):
                for c in range(2):
                    ins = mm(b_ps[:, c * HALF:(c + 1) * HALF], ident3[:, bass.ds(n, 1)].to_broadcast([96, P]),
                             bc3[:, c * HALF:(c + 1) * HALF], start=True, stop=True)
                ins.then_inc(b_ready, 1)

            def spread_c(n):
                for c in range(2):
                    ins = mm(c_ps[:, c * HALF:(c + 1) * HALF],
                             ident3[:, bass.ds(n + DS, 1)].to_broadcast([96, P]),
                             bc3[:, c * HALF:(c + 1) * HALF], start=True, stop=True)
                ins.then_inc(c_ready, 1)

            def add_y(n, last=False):
                for et in range(KT):
                    pe.wait_ge(read_done[et], n + 1)
                    for c in range(2):
                        ins = mm(y_ps[et][:, c * HALF:(c + 1) * HALF], ident,
                                 read[:, et, c * HALF:(c + 1) * HALF], start=False, stop=last,
                                 skip_group_check=True)
                    ins.then_inc(y_added[et], 1)

            pe.wait_ge(delta_done, 2)
            spread_b(0)
            spread_c(0)
            with nc.tensor.Fori(0, DS - 1) as n:
                pe.wait_ge(drive_done, 2 * n + 2)
                spread_b(n + 1)
                pe.wait_ge(c_copied, n + 1)
                spread_c(n + 1)
                add_y(n)
            add_y(DS - 1, last=True)

            for b in range(NB):
                for et in range(KT):
                    pe.wait_ge(y_gated, et + 1)
                    for lt in range(2):
                        ins = nc.tensor.transpose(turned[:, 2 * b + lt, et * P:(et + 1) * P],
                                                  u[:, et, b * L + lt * P:b * L + (lt + 1) * P], ident)
                if b % 2 == 1:
                    ins.then_inc(y_turned, 1)

            def turn_xn(r):
                for c in range(2):
                    pe.wait_ge(xn_done, 2 * r + c + 1)
                    for k in range(KT):
                        for t in range(4 * c, 4 * c + 4):
                            ins = nc.tensor.transpose(ps[:, 2 * c + k, (t % 4) * P:(t % 4 + 1) * P],
                                                      xn[:, t, k * P:(k + 1) * P], ident)
                        ins.then_inc(xn_turned, 1)

            def router(r, weights):
                pe.wait_ge(xnT_even, 2 * r + 2)
                pe.wait_ge(xnT_odd, 2 * r + 2)
                for k in range(KT):
                    for c in range(2):
                        ins = mm(logitT_ps[:, c * HALF:(c + 1) * HALF], weights[:, k, :],
                                 xnT[:, k, c * HALF:(c + 1) * HALF], start=(k == 0), stop=(k == 1))
                ins.then_inc(logitT_done, 1)

            def turn_logits(n):
                pe.wait_ge(logitT_copied, n)
                for t in range(NT):
                    ins = nc.tensor.transpose(logit_ps[:, t, :], logitT[:, t * P:(t + 1) * P], ident[0:NE, 0:NE])
                ins.then_inc(logit_turned, 1)

            pe.wait_ge(att_w_loaded, 64)
            for t in range(NT):
                if t >= 4:
                    pe.wait_ge(kv_copied, t - 3)
                mm(ps[:, 4 + t % 4, :], ctxT[:, t * P:(t + 1) * P], kv_w[:], start=True, stop=True) \
                    .then_inc(kv_done, 1)

            pe.wait_ge(x1_done, 2)
            turn_xn(0)
            pe.wait_ge(ffn_w_loaded, 16 * (3 + 2 * NE))
            pe.wait_ge(kv_copied, NT)
            router(0, router_w)

            def shared_gate_up(j):
                c, ft = j // 2, j % 2
                if j >= 2:
                    pe.wait_ge(shared_hid, j - 1)
                for g in range(2):
                    for k in range(KT):
                        ins = mm(ps[:, 2 * (j % 2) + g, :], gu_w[:, NE, k, g * F + ft * P:g * F + (ft + 1) * P],
                                 xnT[:, k, c * HALF:(c + 1) * HALF], start=(k == 0), stop=(k == 1))
                    ins.then_inc(shared_gu, 1)

            shared_gate_up(0)
            turn_logits(1)
            shared_gate_up(1)
            pe.wait_ge(onehot_done, 1)
            pe.wait_ge(bf_consts, 1)
            mm(rank_ps, upper_bf[:], onehot[:], start=True, stop=False, skip_group_check=True)
            for t in range(NT - 1):
                mm(rank_ps[:, t + 1:, :], ones_bf[:], onehot[:, t:t + 1, :].to_broadcast([P, NT - 1 - t, NE]),
                   start=False, stop=True, skip_group_check=True)
            for t in range(NT):
                ins = mm(count_ps, ones_bf[:], onehot[:, t, :], start=False, stop=(t == NT - 1),
                         skip_group_check=True)
            ins.then_inc(rank_done, 1)
            shared_gate_up(2)
            shared_gate_up(3)
            for j in range(4):
                pe.wait_ge(shared_hid, 2 * (j // 2) + 2)
                if j >= 2:
                    pe.wait_ge(shared_added, j - 1)
                for t in (2 * j, 2 * j + 1):
                    for ft in range(KT):
                        ins = mm(ps[:, 4 + j % 2, (t % 2) * DM:(t % 2 + 1) * DM], hidT[:, ft, t * P:(t + 1) * P],
                                 down_w[:, NE, ft, :], start=(ft == 0 and t % 2 == 0), stop=(ft == 1),
                                 skip_group_check=True)
                ins.then_inc(shared_down, 1)

            pe.wait_ge(shared_added, 4)
            pe.wait_ge(tile_e_done, 1)

            def turn_x(s, k, first, pair=None):
                pe.wait_ge(xg_loaded[k], 16 * ((s // 2 if pair is None else pair) + 1))
                if not first:
                    pe.wait_ge(xgT_ready, s - 1)
                for c in range(KT):
                    ins = nc.tensor.transpose(ps[:, k, c * P:(c + 1) * P], xg[:, k, c * P:(c + 1) * P], ident)
                ins.then_inc(xg_turned, 1)

            def expert(s):
                return pe.value_load(tile_ei[0:1, bass.ds(s, 1)], min_val=0, max_val=NE - 1)

            def gate_up(s, k, first):
                e = expert(s)
                pe.wait_ge(xgT_ready, s + 1)
                if not first:
                    pe.wait_ge(hid_done, s - 1)
                for c in range(KT):
                    ins = mm(ps[:, 2 + k, :], xgT[:, k, c, :],
                             gu_w[:, bass.ds(e, 1), c, :].rearrange("p e f -> p (e f)"),
                             start=(c == 0), stop=(c == 1))
                ins.then_inc(gu_done, 1)

            def down(s, k, first):
                e = expert(s)
                pe.wait_ge(hid_done, s + 1)
                if not first:
                    pe.wait_ge(hT_ready, s - 1)
                for c in range(KT):
                    ins = nc.tensor.transpose(ps[:, 4 + k, c * P:(c + 1) * P], hid[:, k, c * P:(c + 1) * P], ident)
                ins.then_inc(hid_turned, 1)
                pe.wait_ge(hT_ready, s + 1)
                if not first:
                    pe.wait_ge(yo_ready, s - 1)
                for c in range(KT):
                    ins = mm(ps[:, 6 + k, 0:DM], hT[:, k, c, :],
                             down_w[:, bass.ds(e, 1), c, :].rearrange("p e f -> p (e f)"),
                             start=(c == 0), stop=(c == 1))
                ins.then_inc(down_done, 1)

            turn_x(0, 0, True)
            turn_x(1, 1, True)
            gate_up(0, 0, True)
            for s in (1, 2):
                turn_x(s + 1, (s + 1) % 2, False)
                gate_up(s, s % 2, s < 2)
                down(s - 1, (s - 1) % 2, True)
            with nc.tensor.Fori(1, NS // 2 - 1) as i:
                for k in range(2):
                    s = 2 * i + k + 1
                    turn_x(s + 1, k, False, pair=i + 1)
                    gate_up(s, 1 - k, False)
                    down(s - 1, k, False)
            gate_up(NS - 1, 1, False)
            down(NS - 2, 0, False)
            down(NS - 1, 1, False)

            pe.wait_ge(yo_ready, NS)
            turn_xn(1)
            pe.wait_ge(xnT_even, 4)
            pe.wait_ge(xnT_odd, 4)
            for j in range(4):
                for t in (2 * j, 2 * j + 1):
                    for k in range(KT):
                        ins = mm(ps[:, 4 + j, (t % 2) * DM:(t % 2 + 1) * DM], xnT[:, k, t * P:(t + 1) * P],
                                 q_w[:, k, :], start=(k == 0 and t % 2 == 0), stop=(k == 1),
                                 skip_group_check=True)
                ins.then_inc(q_done, 1)

            def rows_of(g, n):
                return slice(g * ROWS, g * ROWS + n)

            def turn_stack(i, k):
                pe.wait_ge(built, i + 1)
                wait_from_one(pe, keysT_ready, i)
                for n in range(4):
                    ins = nc.tensor.transpose(ps[:, 0, n * P:(n + 1) * P],
                                              stack[:, k, n].rearrange("p g r -> p (g r)"), ident)
                ins.then_inc(stack_turned, 1)

            def logit_rows(i, k, n):
                if n == 0:
                    pe.wait_ge(keysT_ready, i + 1)
                wait_from_one(pe, max_done, G * i + n - 1)
                heads, j = n // 2, n % 2
                mm(ps[:, 2 + n % 2, :], rowsT[k % 2][:, j * P:(j + 1) * P],
                   keysT[k][:, 2 * heads:2 * heads + 2, :].rearrange("p g n -> p (g n)")).then_inc(rows_done, 1)

            def turn_queries(i, k):
                pe.wait_ge(shift_done, i + 1)
                wait_from_one(pe, queryT_ready, i)
                for n in range(2):
                    ins = nc.tensor.transpose(ps[:, 1, n * P:(n + 1) * P],
                                              stack[:, k, n].rearrange("p g r -> p (g r)"), ident)
                ins.then_inc(query_turned, 1)

            def logit_cols(i, k, g):
                if g == 0:
                    pe.wait_ge(queryT_ready, i + 1)
                wait_from_one(pe, exp_done, G * i + g - 1)
                for j in range(2):
                    ins = mm(ps[:, 4 + g % 2, j * L:(j + 1) * L], keysT[k][:, g, j * P:(j + 1) * P],
                             queryT[k % 2][:], start=(j == 0), stop=True,
                             skip_group_check=True)
                ins.then_inc(cols_done, 1)

            def values(i, k, g):
                pe.wait_ge(exp_done, G * i + g + 1)
                if g == 0:
                    pe.wait_ge(v_copied, i + 1)
                    wait_from_one(pe, o_copied, i)
                for j in range(2):
                    ins = mm(ps[rows_of(g, ROWS), 6, 0:L], v_ones[:, k % 2, j, g, :],
                             prob[k % 2][:, g, j * L:(j + 1) * L], start=(j == 0), stop=(j == 1),
                             tile_position=(0, g * ROWS))
                ins.then_inc(pv_done, 1)

            def turn_values(i, k):
                pe.wait_ge(o_copied, i + 1)
                wait_from_one(pe, attn_done, i)
                for n in range(2):
                    ins = nc.tensor.transpose(ps[:, 7, n * P:(n + 1) * P], o_sb[:, k % 2, n * P:(n + 1) * P], ident)
                ins.then_inc(o_turned, 1)

            def attention_turn(i, k, live):
                if live(-3):
                    turn_values(i - 3, (k + 1) % SLOTS)
                if live(0):
                    logit_rows(i, k, 0)
                if live(-2):
                    values(i - 2, (k + 2) % SLOTS, 0)
                if live(1):
                    turn_stack(i + 1, (k + 1) % SLOTS)
                if live(-1):
                    turn_queries(i - 1, (k + 3) % SLOTS)
                if live(0):
                    logit_rows(i, k, 1)
                if live(-2):
                    values(i - 2, (k + 2) % SLOTS, 1)
                    values(i - 2, (k + 2) % SLOTS, 2)
                if live(0):
                    logit_rows(i, k, 2)
                if live(-2):
                    values(i - 2, (k + 2) % SLOTS, 3)
                if live(-1):
                    logit_cols(i - 1, (k + 3) % SLOTS, 0)
                    logit_cols(i - 1, (k + 3) % SLOTS, 1)
                if live(0):
                    logit_rows(i, k, 3)
                if live(-1):
                    logit_cols(i - 1, (k + 3) % SLOTS, 2)
                    logit_cols(i - 1, (k + 3) % SLOTS, 3)

            pe.wait_ge(xnT_even, 4)
            run_turns(nc.tensor, attention_turn)

            for c in range(2):
                for f in range(KT):
                    for t in range(4 * c, 4 * c + 4):
                        pe.wait_ge(attn_done, NG)
                        b, j = t // 2, t % 2
                        heads = attn[:, j, b * DM + f * P:b * DM + (f + 1) * P]
                        ins = nc.tensor.transpose(ps[:, 2 * c + f, (t % 4) * P:(t % 4 + 1) * P], heads, ident)
                    ins.then_inc(attn_turned, 1)
            for j in range(4):
                pe.wait_ge(attnT_ready, 2 * (j // 2) + 2)
                for t in (2 * j, 2 * j + 1):
                    for k in range(KT):
                        ins = mm(ps[:, 4 + j, (t % 2) * DM:(t % 2 + 1) * DM], attnT[:, k, t * P:(t + 1) * P],
                                 out_w[:, k, :], start=(k == 0 and t % 2 == 0), stop=(k == 1),
                                 skip_group_check=True)
                ins.then_inc(proj_done, 1)

            pe.wait_ge(x3_done, 4)
            turn_xn(2)
            pe.wait_ge(last_w_loaded, 64)
            router(2, wr_w)

            def low_rank(t):
                if t >= 2:
                    pe.wait_ge(low_masked, t - 1)
                for k in range(KT):
                    ins = mm(ps[:, t % 2, :], xnT[:, k, t * P:(t + 1) * P], a_w[:, k, :], start=(k == 0), stop=(k == 1))
                ins.then_inc(low_done, 1)

            def turn_low(t):
                pe.wait_ge(low_masked, t + 1)
                if t >= 2:
                    pe.wait_ge(lowT_ready, t - 1)
                for c in range(4):
                    ins = nc.tensor.transpose(ps[:, 2 + t % 2, c * P:(c + 1) * P], low[:, t % 2, c * P:(c + 1) * P],
                                              ident)
                ins.then_inc(low_turned, 1)

            def high(t):
                pe.wait_ge(lowT_ready, t + 1)
                if t >= 2:
                    pe.wait_ge(tile_done, t - 1)
                elif t == 0:
                    pe.wait_ge(logitT_copied, 2)
                for c in range(4):
                    ins = mm(ps[:, 4 + t % 2, 0:DM], lowT[:, t % 2, c * P:(c + 1) * P], b_w[:, c, :],
                             start=(c == 0), stop=(c == 3))
                ins.then_inc(last_done, 1)

            low_rank(0)
            turn_logits(2)
            for t in range(NT + 1):
                if t + 1 < NT:
                    low_rank(t + 1)
                if t < NT:
                    turn_low(t)
                if t >= 1:
                    high(t - 1)

        @block.scalar
        def _(act):
            own = Chain(act, act_own)
            nc.scalar.preload_act_table_set("natural_log_exp_and_others")
            act.wait_ge(ssm_w_loaded, 48)
            nc.scalar.activation(neg_a[:], a_log, ACT.Exp).then_inc(expa_done, 1)
            act.wait_ge(ln0_stats, 1)
            act.wait_ge(cols_set, 1)
            own.then_wait(nc.scalar.activation(ln_var[:], mean_var[:, :, 1], ACT.Ln, bias=eps_col[:]))
            nc.scalar.activation(rstd[:], ln_var[:], ACT.Exp, scale=-0.5).then_inc(ln0_rstd, 1)
            for et in range(KT):
                act.wait_ge(xin_done, et + 1)
                nc.scalar.activation(delta[:, et, :], xin_ps[et], ACT.Identity, bias=conv_b[:, et, :],
                                     scale=tap_w[:, et, TAPS - 1:TAPS]).then_inc(tap0_done, 1)
            nc.scalar.preload_act_table_set("silu_and_others")
            act.wait_ge(ln0_shift, 1)
            for b in range(NB):
                for et in range(KT):
                    t = 2 * b + et
                    nc.scalar.activation(gate_z[:, et, b * L:(b + 1) * L], x_tok[:, t, :], ACT.Silu,
                                         bias=shift[:, t:t + 1], scale=rstd[:, t:t + 1])
            act.wait_ge(angle_done, 1)
            nc.scalar.activation(angle[:], angle[:], ACT.Sin).then_inc(trig_done, 1)
            for et in range(KT):
                act.wait_ge(conv_done, et + 1)
                nc.scalar.activation(u[:, et, :], delta[:, et, :], ACT.Silu).then_inc(u_done, 1)
            nc.scalar.preload_act_table_set("natural_log_exp_and_others")
            act.wait_ge(xdbl_done, 1)
            nc.scalar.copy(xdbl[:], xdbl_ps).then_inc(xdbl_copied, 1)
            for et in range(KT):
                act.wait_ge(dt_done, et + 1)
                own.then_wait(nc.scalar.activation(state[:, et, :], dt_ps[et], ACT.Identity, bias=dt_b[:, et, :]))
                own.then_wait(nc.scalar.activation(read[:, et, :], state[:, et, :], ACT.Abs))
                own.then_wait(nc.scalar.activation(read[:, et, :], read[:, et, :], ACT.Exp, scale=-1.0))
                nc.scalar.activation(read[:, et, :], read[:, et, :], ACT.Ln, bias=one_col[:]).then_inc(log_done, 1)

            def decay_and_c(n, k, first):
                act.wait_ge(c_ready, n + 1)
                if not first:
                    act.wait_ge(read_done[1], n - 1)
                elif k == 0:
                    act.wait_ge(sorted_cleared, 32)
                nc.scalar.copy(c_rows[:, k, :], c_ps).then_inc(c_copied, 1)
                for et in range(KT):
                    act.wait_ge(delta_done, et + 1)
                    if not first or k > 0:
                        act.wait_ge(scan_done[et], n)
                    nc.scalar.activation(
                        decay[:, et, :].rearrange("p (b l) -> p b l", b=NB)[:, :, 1:],
                        delta[:, et, :].rearrange("p (b l) -> p b l", b=NB)[:, :, 1:],
                        ACT.Exp, scale=neg_a[:, et, bass.ds(n, 1)]).then_inc(decay_ready[et], 1)

            act.wait_ge(setup_done, 1)
            for k in range(2):
                decay_and_c(k, k, first=True)
            with nc.scalar.Fori(1, DS // 2) as i:
                for k in range(2):
                    decay_and_c(2 * i + k, k, first=False)

            def norm_rstd(r):
                act.wait_ge(ln_stats, r + 1)
                own.then_wait(nc.scalar.activation(ln_var[:], mean_var[:, :, 1], ACT.Ln, bias=eps_col[:]))
                nc.scalar.activation(rstd[:], ln_var[:], ACT.Exp, scale=-0.5).then_inc(ln_rstd, 1)

            def copy_xnT_even(r):
                for c in range(2):
                    act.wait_ge(xn_turned, 4 * r + 2 * c + 1)
                    nc.scalar.copy(xnT[:, 0, c * HALF:(c + 1) * HALF], ps[:, 2 * c, :]).then_inc(xnT_even, 1)

            def copy_kv(t):
                b, j = t // 2, t % 2
                act.wait_ge(kv_done, t + 1)
                nc.scalar.copy(k_tok[:, t, :], ps[:, 4 + t % 4, 0:DM])
                nc.scalar.copy(v_tok[:, 8 * b:8 * b + 8, j * G * HD:(j + 1) * G * HD],
                               ps[:, 4 + t % 4, DM:2 * DM].rearrange("p (g c) -> p g c", c=G * HD)).then_inc(kv_copied, 1)

            for t in range(4):
                copy_kv(t)
            norm_rstd(0)
            for t in range(4, NT):
                copy_kv(t)
            copy_xnT_even(0)
            act.wait_ge(logitT_done, 1)
            nc.scalar.copy(logitT[:], logitT_ps).then_inc(logitT_copied, 1)
            act.wait_ge(top_done, 1)
            nc.scalar.activation(score[:], top[:], ACT.Exp, scale=-1.0).then_inc(exp_top_done, 1)
            nc.scalar.preload_act_table_set("silu_and_others")
            for j in range(4):
                act.wait_ge(shared_gu, 2 * j + 1)
                nc.scalar.activation(silu_g[:, j, :], ps[:, 2 * (j % 2), :], ACT.Silu).then_inc(shared_silu, 1)

            def silu_tile(s, k, first):
                act.wait_ge(gu_done, s + 1)
                if not first:
                    act.wait_ge(hid_done, s - 1)
                nc.scalar.activation(sg[:, k, :], ps[:, 2 + k, 0:F], ACT.Silu).then_inc(sg_done, 1)

            def copy_hT(s, k, first):
                act.wait_ge(hid_turned, s + 1)
                if not first:
                    act.wait_ge(down_done, s - 1)
                nc.scalar.copy(hT[:, k].rearrange("p c t -> p (c t)"), ps[:, 4 + k, 0:F]).then_inc(hT_ready, 1)

            silu_tile(0, 0, True)
            for s in (1, 2):
                silu_tile(s, s % 2, s < 2)
                copy_hT(s - 1, (s - 1) % 2, True)
            with nc.scalar.Fori(1, NS // 2 - 1) as i:
                for k in range(2):
                    s = 2 * i + k + 1
                    silu_tile(s, 1 - k, False)
                    copy_hT(s - 1, k, False)
            silu_tile(NS - 1, 1, False)
            copy_hT(NS - 2, 0, False)
            copy_hT(NS - 1, 1, False)

            nc.scalar.preload_act_table_set("natural_log_exp_and_others")
            norm_rstd(1)
            copy_xnT_even(1)

            def copy_rowsT(i, k):
                act.wait_ge(stack_turned, i + 1)
                wait_from_one(act, rows_done, G * (i - 1))
                nc.scalar.copy(rowsT[k % 2][:], ps[:, 0, 0:L]).then_inc(rowsT_ready, 1)

            def copy_queryT(i, k):
                act.wait_ge(query_turned, i + 1)
                wait_from_one(act, cols_done, G * (i - 1))
                nc.scalar.copy(queryT[k % 2][:], ps[:, 1, 0:L]).then_inc(queryT_ready, 1)

            def exponential(i, k, g):
                act.wait_ge(cols_done, G * i + g + 1)
                wait_from_one(act, pv_done, G * (i - 2) + g + 1)
                nc.scalar.activation(prob[k % 2][:, g, :], ps[:, 4 + g % 2, :], ACT.Exp, scale=HD ** -0.5) \
                    .then_inc(exp_done, 1)

            def copy_o(i, k):
                act.wait_ge(pv_done, G * i + G)
                wait_from_one(act, o_turned, i - 1)
                nc.scalar.copy(o_sb[:, k % 2, :], ps[:, 6, 0:L]).then_inc(o_copied, 1)

            def attention_turn(i, k, live):
                if live(-1):
                    copy_queryT(i - 1, (k + 3) % SLOTS)
                if live(1):
                    copy_rowsT(i + 1, (k + 1) % SLOTS)
                if live(-2):
                    copy_o(i - 2, (k + 2) % SLOTS)
                if live(-1):
                    exponential(i - 1, (k + 3) % SLOTS, 0)
                    exponential(i - 1, (k + 3) % SLOTS, 1)
                    exponential(i - 1, (k + 3) % SLOTS, 2)
                    exponential(i - 1, (k + 3) % SLOTS, 3)

            run_turns(nc.scalar, attention_turn)

            for n in range(4):
                act.wait_ge(attn_turned, n + 1)
                nc.scalar.copy(attnT[:, n % 2, (n // 2) * HALF:(n // 2 + 1) * HALF], ps[:, n, :]) \
                    .then_inc(attnT_ready, 1)
            norm_rstd(2)
            copy_xnT_even(2)
            act.wait_ge(logitT_done, 2)
            nc.scalar.copy(logitT[:], logitT_ps).then_inc(logitT_copied, 1)
            act.wait_ge(shifted_done, 1)
            nc.scalar.activation(pick_w[:], pick_w[:], ACT.Exp).then_inc(exp_logit_done, 1)
            for t in range(NT):
                act.wait_ge(low_turned, t + 1)
                if t >= 2:
                    act.wait_ge(last_done, t - 1)
                nc.scalar.copy(lowT[:, t % 2, :], ps[:, 2 + t % 2, :]).then_inc(lowT_ready, 1)

        @block.vector
        def _(dve):
            own = Chain(dve, dve_own)
            vec = nc.vector

            def layer_norm_stats(done):
                for t in range(NT):
                    ins = vec.bn_stats(stats[:, t, :], x_tok[:, t, :])
                own.then_wait(ins)
                for t in range(NT):
                    ins = vec.bn_aggr(mean_var[:, t, :], stats[:, t, :])
                ins.then_inc(done, 1)

            dve.wait_ge(pos_loaded, 16)
            pos2 = pos[:].rearrange("p t c -> p (t c)")
            flat = [angle[:, c].rearrange("p t (c h) -> p (t c) h", h=2) for c in range(2)]
            for half in range(2):
                freq = 10000.0 ** (-half / 2)
                vec.tensor_scalar(flat[0][:, :, half], pos2, freq, None, ALU.mult)
                ins = vec.tensor_scalar(flat[1][:, :, half], pos2, freq, math.pi / 2, ALU.mult, ALU.add)
            own.then_wait(ins)
            own.then_wait(vec.tensor_scalar(turns[:], angle[:], 1 / (2 * math.pi), ROUND, ALU.mult, ALU.add))
            own.then_wait(vec.tensor_scalar(turns[:], turns[:], ROUND, None, ALU.subtract))
            for part in (TWO_PI_HI, TWO_PI_LO):
                own.then_wait(vec.scalar_tensor_tensor(out=angle[:], in0=turns[:], scalar=-part, in1=angle[:],
                                                       op0=ALU.mult, op1=ALU.add))
            vec.tensor_scalar(angle[:], angle[:], PI_BELOW, -PI_BELOW, ALU.min, ALU.max).then_inc(angle_done, 1)

            dve.wait_ge(x_loaded, 16)
            layer_norm_stats(ln0_stats)
            dve.wait_ge(ln0_rstd, 1)
            vec.scalar_tensor_tensor(out=shift[:], in0=mean_var[:, :, 0], scalar=-1.0, in1=rstd[:],
                                     op0=ALU.mult, op1=ALU.mult).then_inc(ln0_shift, 1)
            for j in range(TAPS - 1):
                back = TAPS - 1 - j
                for et in range(KT):
                    if j == 0:
                        dve.wait_ge(tap0_done, et + 1)
                    acc = delta[:, et, :].rearrange("p (b l) -> p b l", b=NB)[:, :, back:]
                    xin = xin_ps[et].rearrange("p (b l) -> p b l", b=NB)[:, :, 0:L - back]
                    ins = vec.scalar_tensor_tensor(out=acc, in0=xin, scalar=tap_w[:, et, j:j + 1], in1=acc,
                                                   op0=ALU.mult, op1=ALU.add)
                    if j == TAPS - 2:
                        ins.then_inc(conv_done, 1)
                if j < TAPS - 2:
                    own.then_wait(ins)

            dve.wait_ge(xdbl_copied, 1)
            rest = drive[0:96, 0, :]
            own.then_wait(vec.tensor_copy(bc3[:], xdbl[0:96, :]))
            own.then_wait(vec.tensor_tensor(rest, xdbl[0:96, :], bc3[:], ALU.subtract))
            vec.tensor_copy(bc3[32:64, :], rest[32:64, :])
            own.then_wait(vec.tensor_copy(bc3[64:96, :], rest[64:96, :]))
            vec.tensor_tensor(bc3[64:96, :], rest[64:96, :], bc3[64:96, :], ALU.subtract).then_inc(bc3_done, 1)

            for et in range(KT):
                dve.wait_ge(log_done, et + 1)
                vec.scalar_tensor_tensor(out=delta[:, et, :], in0=state[:, et, :], scalar=0.0, in1=read[:, et, :],
                                         op0=ALU.max, op1=ALU.add).then_inc(delta_done, 1)
                dve.wait_ge(delta_done, et + 1)
                ins = vec.tensor_tensor(du[:, et, :], delta[:, et, :], u[:, et, :], ALU.mult)
            own.then_wait(ins)

            def scan_state(n, first):
                dve.wait_ge(b_ready, n + 1)
                for et in range(KT):
                    if not first:
                        dve.wait_ge(scan_done[et], n)
                    vec.tensor_tensor(drive[:, et, :], du[:, et, :], b_ps, ALU.mult).then_inc(drive_done, 1)
                for et in range(KT):
                    dve.wait_ge(decay_ready[et], n + 1)
                    dve.wait_ge(drive_done, 2 * n + et + 1)
                    if not first:
                        dve.wait_ge(read_done[et], n)
                    vec.tensor_tensor_scan(state[:, et, :], decay[:, et, :], drive[:, et, :], 0.0,
                                           ALU.mult, ALU.add).then_inc(scan_done[et], 1)

            scan_state(0, True)
            with nc.vector.Fori(1, DS) as n:
                scan_state(n, False)

            for et in range(KT):
                dve.wait_ge(y_added[et], DS)
                vec.tensor_tensor(u[:, et, :], y_ps[et], gate_z[:, et, :], ALU.mult).then_inc(y_gated, 1)
            for c in range(2):
                dve.wait_ge(y_turned, c + 1)
                vec.tensor_tensor(x_tok[:, 4 * c:4 * c + 4, :], x_tok[:, 4 * c:4 * c + 4, :],
                                  turned[:, 4 * c:4 * c + 4, :], ALU.add).then_inc(x1_done, 1)

            def normalise(r):
                for c in range(2):
                    for t in range(4 * c, 4 * c + 4):
                        if t == 0:
                            dve.wait_ge(ln_rstd, r + 1)
                        ins = vec.tensor_scalar(xn[:, t, :], x_tok[:, t, :], mean_var[:, t, 0:1], rstd[:, t:t + 1],
                                                ALU.subtract, ALU.mult)
                    ins.then_inc(xn_done, 1)

            def copy_xnT_odd(r):
                for c in range(2):
                    dve.wait_ge(xn_turned, 4 * r + 2 * c + 2)
                    vec.tensor_copy(xnT[:, 1, c * HALF:(c + 1) * HALF], ps[:, 2 * c + 1, :]).then_inc(xnT_odd, 1)

            def first_of_top(done):
                vec.tensor_reduce(top[:], logit[:], AX.X, ALU.max).then_inc(top_done, 1)
                dve.wait_ge(top_done, 1 if done is onehot_done else 2)
                own.then_wait(vec.tensor_tensor(pick[:], logit[:], top[:].unsqueeze(2).to_broadcast([P, NT, NE]),
                                                ALU.is_equal))
                own.then_wait(vec.tensor_tensor(pick[:], pick[:], e_minus_8.unsqueeze(1).to_broadcast([P, NT, NE]),
                                                ALU.mult))
                own.then_wait(vec.tensor_reduce(first_e[:], pick[:], AX.X, ALU.min))
                vec.tensor_tensor(onehot[:], e_minus_8.unsqueeze(1).to_broadcast([P, NT, NE]),
                                  first_e[:].unsqueeze(2).to_broadcast([P, NT, NE]), ALU.is_equal) \
                   .then_inc(done, 1)

            dve.wait_ge(trig_done, 1)
            vec.tensor_copy(cos8[:].rearrange("p t (c h) -> p (t c) h", h=2),
                            angle[:, 1].rearrange("p t c -> p (t c)").unsqueeze(2).to_broadcast([P, NT * 4, 2]))
            vec.tensor_copy(sin_pos[:], angle[:, 0])
            vec.tensor_scalar(sin_neg[:], angle[:, 0], -1.0, None, ALU.mult).then_inc(trig_ready, 1)
            dve.wait_ge(x1_done, 2)
            layer_norm_stats(ln_stats)
            normalise(0)
            vec.memset(ones_bf[:], 1.0)
            vec.memset(zeros8[:], 0.0)
            vec.tensor_copy(upper_bf[:], upper).then_inc(bf_consts, 1)
            copy_xnT_odd(0)
            dve.wait_ge(logit_turned, 1)
            own.then_wait(vec.tensor_copy(logit[:], logit_ps))
            first_of_top(onehot_done)
            dve.wait_ge(onehot_done, 1)
            dve.wait_ge(rank_done, 1)
            own.then_wait(vec.tensor_copy(tiles_e[:], count_ps))
            own.then_wait(vec.tensor_tensor(full_tile[:], tiles_e[:].unsqueeze(2).to_broadcast([P, NE, NE]),
                                            j_times_128.unsqueeze(1).to_broadcast([P, NE, NE]), ALU.is_gt))
            own.then_wait(vec.tensor_reduce(tiles_e[:], full_tile[:], AX.X, ALU.add))
            own.then_wait(vec.tensor_tensor_scan(tiles_upto[:], tiles_e[:], zeros8[:], 0.0, ALU.add, ALU.add))
            own.then_wait(vec.tensor_tensor(tiles_e[:], tiles_upto[:], tiles_e[:], ALU.subtract))
            own.then_wait(vec.scalar_tensor_tensor(
                out=pick[:], in0=tiles_e[:].unsqueeze(1).to_broadcast([P, NT, NE]), scalar=float(P), in1=rank_ps,
                op0=ALU.mult, op1=ALU.add))
            own.then_wait(vec.tensor_tensor(pick[:], pick[:], onehot[:], ALU.mult))
            own.then_wait(vec.tensor_reduce(slot_f[:], pick[:], AX.X, ALU.add))
            vec.tensor_copy(slot[:], slot_f[:]).then_inc(slot_done, 1)
            own.then_wait(vec.tensor_tensor(tile_cmp[:], tiles_upto[0:1, :].unsqueeze(1).to_broadcast([1, NS, NE]),
                                            tile_no[0:1, :].unsqueeze(2).to_broadcast([1, NS, NE]), ALU.is_le))
            own.then_wait(vec.tensor_reduce(tile_e[:], tile_cmp[:], AX.X, ALU.add))
            vec.tensor_scalar(tile_ei[:], tile_e[:], float(NE - 1), None, ALU.min).then_inc(tile_e_done, 1)
            dve.wait_ge(exp_top_done, 1)
            own.then_wait(vec.tensor_scalar(score[:], score[:], 1.0, None, ALU.add))
            own.then_wait(vec.reciprocal(score[:], score[:]))
            for t in range(NT):
                vec.tensor_scalar(scaled[:, t, :], xn[:, t, :], score[:, t:t + 1], None, ALU.mult) \
                   .then_inc(scaled_done, 1)

            for j in range(4):
                dve.wait_ge(shared_gu, 2 * j + 2)
                dve.wait_ge(shared_silu, j + 1)
                vec.tensor_tensor(hidT[:, j % 2, (j // 2) * HALF:(j // 2 + 1) * HALF], ps[:, 2 * (j % 2) + 1, :],
                                  silu_g[:, j, :], ALU.mult).then_inc(shared_hid, 1)
            for j in range(4):
                dve.wait_ge(shared_down, j + 1)
                pair = x_tok[:, 2 * j:2 * j + 2, :].rearrange("p t d -> p (t d)")
                vec.tensor_tensor(pair, pair, ps[:, 4 + j % 2, :], ALU.add).then_inc(shared_added, 1)

            def copy_xgT(s, k, first):
                dve.wait_ge(xg_turned, s + 1)
                if not first:
                    dve.wait_ge(gu_done, s - 1)
                vec.tensor_copy(xgT[:, k].rearrange("p c t -> p (c t)"), ps[:, k, 0:DM]).then_inc(xgT_ready, 1)

            def multiply(s, k, first):
                dve.wait_ge(sg_done, s + 1)
                if not first:
                    dve.wait_ge(hid_turned, s - 1)
                vec.tensor_tensor(hid[:, k, :], ps[:, 2 + k, F:2 * F], sg[:, k, :], ALU.mult).then_inc(hid_done, 1)

            def copy_yo(s, k, first, pair=None):
                dve.wait_ge(down_done, s + 1)
                if not first:
                    dve.wait_ge(yo_stored[k], 16 * (s // 2 if pair is None else pair))
                vec.tensor_copy(yo[:, k, :], ps[:, 6 + k, 0:DM]).then_inc(yo_ready, 1)

            copy_xgT(0, 0, True)
            copy_xgT(1, 1, True)
            multiply(0, 0, True)
            for s in (1, 2):
                copy_xgT(s + 1, (s + 1) % 2, False)
                multiply(s, s % 2, s < 2)
                copy_yo(s - 1, (s - 1) % 2, True)
            with nc.vector.Fori(1, NS // 2 - 1) as i:
                for k in range(2):
                    s = 2 * i + k + 1
                    copy_xgT(s + 1, k, False)
                    multiply(s, 1 - k, False)
                    copy_yo(s - 1, k, False, pair=i)
            multiply(NS - 1, 1, False)
            copy_yo(NS - 2, 0, False)
            copy_yo(NS - 1, 1, False)
            for c in range(2):
                dve.wait_ge(gathered, 16 * NT)
                vec.tensor_tensor(x_tok[:, 4 * c:4 * c + 4, :], x_tok[:, 4 * c:4 * c + 4, :],
                                  routed[:, 4 * c:4 * c + 4, :], ALU.add).then_inc(x2_done, 1)

            dve.wait_ge(x2_done, 2)
            layer_norm_stats(ln_stats)
            normalise(1)
            copy_xnT_odd(1)
            dve.wait_ge(k_rotated, 1)
            q_ps = banks(4, 4).rearrange("p (t d) -> p t d", d=DM)
            for c in range(2):
                dve.wait_ge(q_done, 2 * c + 2)
                tiles = slice(4 * c, 4 * c + 4)
                rotate(vec, q_ps[:, tiles], swapped[:, tiles], tiles)
                ins = vec.tensor_tensor(q_cos[:, tiles].rearrange("p t (h c) -> p t h c", c=HD),
                                        q_ps[:, tiles].rearrange("p t (h c) -> p t h c", c=HD),
                                        cos8[:, tiles].unsqueeze(2).to_broadcast([P, 4, NH, HD]), ALU.mult)
                own.then_wait(ins)
                for j in range(2):
                    ins = add_rotated(vec, q_cos, swapped, 0, c, j)
            ins.then_inc(q_rotated, 1)

            def spread_keys(i, k):
                dve.wait_ge(rowsT_ready, i + 1)
                wait_from_one(dve, cols_done, G * (i + 1 - SLOTS))
                vec.tensor_tensor(keysT[k][:], ps[:, 0, L:2 * L].unsqueeze(1).to_broadcast([P, G, L]),
                                  head_rows.unsqueeze(2).to_broadcast([P, G, L]), ALU.mult).then_inc(keysT_ready, 1)

            def row_maximum(i, k, n):
                dve.wait_ge(rows_done, G * i + n + 1)
                heads = slice(n // 2 * 2, n // 2 * 2 + 2)
                vec.tensor_reduce(row_max[:, k % 2, n % 2, heads], ps[:, 2 + n % 2, :].rearrange("p (g n) -> p g n", n=L),
                                  AX.X, ALU.max).then_inc(max_done, 1)

            def write_shift(i, k):
                dve.wait_ge(max_done, G * i + G)
                dve.wait_ge(stack_turned, i + 1)
                wait_from_one(dve, query_turned, i + 1 - SLOTS)
                hi, lo = stack[:, k, 0:2, :, SPLIT], stack[:, k, 0:2, :, SPLIT + 1]
                vec.tensor_scalar(hi.bitcast(F32R), row_max[:, k % 2], -1.0, None, ALU.mult).then_inc(shift_hi, 1)
                dve.wait_ge(shift_hi, i + 1)
                vec.scalar_tensor_tensor(out=lo.bitcast(F32R), in0=row_max[:, k % 2], scalar=-1.0, in1=hi,
                                         op0=ALU.mult, op1=ALU.subtract).then_inc(shift_done, 1)

            def divide(i, k):
                dve.wait_ge(o_turned, i + 1)
                heads = ps[:, 7, 0:2 * P].rearrange("p (j g r) -> p j g r", j=2, g=G)
                wait_from_one(dve, attn_done, i)
                vec.reciprocal(inv_sum[:], heads[:, :, :, HD]).then_inc(inv_done, 1)
                dve.wait_ge(inv_done, i + 1)
                vec.tensor_tensor(attn[:, :, bass.ds(i * (G * HD), G * HD)].rearrange("p j (g c) -> p j g c", g=G),
                                  heads[:, :, :, 0:HD], inv_sum[:].unsqueeze(3).to_broadcast([P, 2, G, HD]),
                                  ALU.mult).then_inc(attn_done, 1)

            def attention_turn(i, k, live):
                if live(-3):
                    divide(i - 3, (k + 1) % SLOTS)
                if live(0):
                    row_maximum(i, k, 0)
                    row_maximum(i, k, 1)
                if live(1):
                    spread_keys(i + 1, (k + 1) % SLOTS)
                if live(0):
                    row_maximum(i, k, 2)
                    row_maximum(i, k, 3)
                    write_shift(i, k)

            run_turns(nc.vector, attention_turn)

            dve.wait_ge(bias_added, 1)
            for j in range(4):
                dve.wait_ge(proj_done, j + 1)
                pair = x_tok[:, 2 * j:2 * j + 2, :].rearrange("p t d -> p (t d)")
                vec.tensor_tensor(pair, pair, ps[:, 4 + j, :], ALU.add).then_inc(x3_done, 1)
            dve.wait_ge(x3_done, 4)
            layer_norm_stats(ln_stats)
            normalise(2)
            copy_xnT_odd(2)
            dve.wait_ge(logit_turned, 2)
            own.then_wait(vec.tensor_tensor(logit[:], logit_ps, br_row[:].unsqueeze(1).to_broadcast([P, NT, NE]), ALU.add))
            first_of_top(onehot2_done)
            vec.tensor_tensor(pick_w[:], logit[:], top[:].unsqueeze(2).to_broadcast([P, NT, NE]), ALU.subtract) \
               .then_inc(shifted_done, 1)
            dve.wait_ge(exp_logit_done, 1)
            own.then_wait(vec.tensor_reduce(weight[:], pick_w[:], AX.X, ALU.add))
            own.then_wait(vec.reciprocal(weight[:], weight[:]))
            own.then_wait(vec.tensor_scalar(weight[:], weight[:], 1.0 / RANK, None, ALU.mult))
            dve.wait_ge(onehot2_done, 1)
            own.then_wait(vec.tensor_tensor(pick_w[:], onehot[:], weight[:].unsqueeze(2).to_broadcast([P, NT, NE]),
                                            ALU.mult))
            for t in range(NT + 2):
                if t < NT:
                    dve.wait_ge(low_done, t + 1)
                    if t >= 2:
                        dve.wait_ge(low_turned, t - 1)
                    vec.tensor_tensor(low[:, t % 2, :].rearrange("p (e r) -> p e r", r=RANK),
                                      ps[:, t % 2, :].rearrange("p (e r) -> p e r", r=RANK),
                                      pick_w[:, t, :].unsqueeze(2).to_broadcast([P, NE, RANK]), ALU.mult) \
                       .then_inc(low_masked, 1)
                if t >= 2:
                    dve.wait_ge(last_done, t - 1)
                    vec.tensor_tensor(x_tok[:, t - 2, :], x_tok[:, t - 2, :], ps[:, 4 + t % 2, 0:DM], ALU.add) \
                       .then_inc(tile_done, 1)

        @block.gpsimd
        def _(pool):
            own = Chain(pool, pool_own)
            pl = nc.gpsimd
            pl.memset(eps_col[:], LN_EPS)
            pl.memset(one_col[:], 1.0)
            pl.memset(zero_rows, 0.0).then_inc(zeros_set, 1)
            pl.memset(decay[:].rearrange("p e (b l) -> p e b l", b=NB)[:, :, :, 0:1], 0.0).then_inc(cols_set, 1)
            pool.wait_ge(consts_loaded, 16)
            pool.wait_ge(ssm_w_loaded, 48)
            pl.tensor_copy(ident3[:], ident3f[0:96, :])
            for et in range(KT):
                pl.tensor_scalar(diag_d[:, et, :], ident, d_skip[:, et, :], 1.0, ALU.mult, ALU.mult)
            pool.wait_ge(expa_done, 1)
            pl.tensor_scalar(neg_a[:], neg_a[:], -1.0, 1.0, ALU.mult, ALU.mult).then_inc(setup_done, 1)

            def read_state(n, k, first):
                for et in range(KT):
                    pool.wait_ge(scan_done[et], n + 1)
                    pool.wait_ge(c_copied, n + 1)
                    if not first:
                        pool.wait_ge(y_added[et], n)
                    pl.tensor_tensor(read[:, et, :], state[:, et, :], c_rows[:, k, :], ALU.mult) \
                      .then_inc(read_done[et], 1)

            for k in range(2):
                read_state(k, k, first=(k == 0))
            with nc.gpsimd.Fori(1, DS // 2) as i:
                for k in range(2):
                    read_state(2 * i + k, k, first=False)

            for t in range(NT):
                pool.wait_ge(scaled_done, t + 1)
                if t == 0:
                    pool.wait_ge(slot_done, 1)
                    pool.wait_ge(sorted_cleared, 32)
                pl.indirect_dma_start(sorted_x, bass.IndirectOffsetOnAxis(ap=slot[:, t:t + 1], axis=0),
                                      scaled[:, t, :], None).then_inc(scattered, 16)
            pool.wait_ge(trig_ready, 1)
            pool.wait_ge(kv_copied, NT)
            pool.wait_ge(y_turned, 2)
            own.then_wait(rotate(pl, k_tok, swapped, slice(0, NT)))
            own.then_wait(pl.tensor_tensor(k_tok.rearrange("p t (h c) -> p t h c", c=HD),
                                           k_tok.rearrange("p t (h c) -> p t h c", c=HD),
                                           cos8[:].unsqueeze(2).to_broadcast([P, NT, NH, HD]), ALU.mult))
            for c in range(2):
                for j in range(2):
                    ins = add_rotated(pl, k_tok, swapped, 1, c, j)
            ins.then_inc(k_rotated, 1)

            with nc.gpsimd.Fori(0, NS // 2) as i:
                for k in range(2):
                    pool.wait_ge(yo_ready, 2 * i + k + 1)
                    pl.dma_start(sorted_y[bass.ds((2 * i + k) * P, P), :], yo[:, k, :]).then_inc(yo_stored[k], 16)
            pool.wait_ge(yo_stored[0], 8 * NS)
            pool.wait_ge(yo_stored[1], 8 * NS)
            for t in range(NT):
                pl.indirect_dma_start(routed[:, t, :], None, sorted_y,
                                      bass.IndirectOffsetOnAxis(ap=slot[:, t:t + 1], axis=0)) \
                  .then_inc(gathered, 16)

            pl.memset(stack[:], 0.0)
            pl.memset(v_ones[:], 0.0).then_inc(pads_set, 1)
            pool.wait_ge(pads_set, 1)
            pl.memset(stack[:, :, 2:4, :, SPLIT:SPLIT + 2], 1.0)
            pl.memset(v_ones[:, :, :, :, HD:HD + 1], 1.0)

            def build_group(i, k):
                pool.wait_ge(q_rotated, 1)
                wait_from_one(pool, query_turned, i + 1 - SLOTS)
                wait_from_one(pool, built, i - 1)
                pl.tensor_copy(current[:, k % 2:k % 2 + 1], rot[:, bass.ds(i, 1)].rearrange("p i w c -> p i (w c)")) \
                  .then_inc(current_ready, 1)
                pool.wait_ge(current_ready, i + 1)
                both = current[:, k % 2].rearrange("p (n g c) -> p n g c", n=4, g=G)
                q, key = both[:, 0:2], both[:, 2:4]
                part = [stack[:, k, :, :, n * HD:(n + 1) * HD] for n in range(3)]
                pl.tensor_tensor(part[0].bitcast(F32R), both, one_col[:].unsqueeze(1).unsqueeze(2).to_broadcast([P, 4, G, HD]),
                                 ALU.mult)
                pl.tensor_scalar(part[1][:, 0:2].bitcast(F32R), q, 1.0, 1.0, ALU.mult, ALU.mult)
                pl.tensor_scalar(part[2][:, 2:4].bitcast(F32R), key, 1.0, 1.0, ALU.mult, ALU.mult).then_inc(hi_built, 1)
                pool.wait_ge(hi_built, i + 1)
                pl.tensor_tensor(part[2][:, 0:2].bitcast(F32R), q, part[0][:, 0:2], ALU.subtract)
                pl.tensor_tensor(part[1][:, 2:4].bitcast(F32R), key, part[0][:, 2:4], ALU.subtract).then_inc(built, 1)

            def copy_values(i, k):
                pool.wait_ge(q_rotated, 1)
                wait_from_one(pool, pv_done, G * (i - 1))
                pl.tensor_copy(v_ones[:, k % 2, :, :, 0:HD],
                               v_tok[:, bass.ds(i, 1)].rearrange("p i (n g c) -> p (i n) g c", n=2, g=G)) \
                  .then_inc(v_copied, 1)

            for i in range(SLOTS):
                build_group(i, i % SLOTS)
                if i >= 1:
                    copy_values(i - 1, (i - 1) % 2)
            with nc.gpsimd.Fori(1, NG // SLOTS) as m:
                for k in range(SLOTS):
                    build_group(SLOTS * m + k, k)
                    copy_values(SLOTS * m + k - 1, (k - 1) % 2)
            copy_values(NG - 1, 1)
            pl.tensor_tensor(x_tok[:], x_tok[:], out_b[:].unsqueeze(1).to_broadcast([P, NT, DM]), ALU.add) \
              .then_inc(bias_added, 1)
    return nc


def kernel(x, ctx_1024, fside_BxSx2_0, L0_xattn_in_proj_w, L0_xattn_conv_w, L0_xattn_conv_b, L0_xattn_x_proj_w,
           L0_xattn_dt_proj_w, L0_xattn_dt_proj_b, L0_xattn_A_log, L0_xattn_D, L0_ffn_router_w, L0_ffn_gate_w,
           L0_ffn_up_w, L0_ffn_down_w, L0_ffn_shared_gate_w, L0_ffn_shared_up_w, L0_ffn_shared_down_w,
           L1_xattn_Wq, L1_xattn_Wkv, L1_xattn_Wout, L1_xattn_bout, L1_ffn_A, L1_ffn_B, L1_ffn_Wr, L1_ffn_br):
    import numpy as np
    import concourse.bacc as bacc
    from concourse.bass_utils import run_bass_kernel_spmd

    cat = np.concatenate
    xp = np.asarray(L0_xattn_x_proj_w)
    bc = xp[DR:]
    small = np.zeros((P, 64 + G), np.float32)
    small[:, 64:] = np.arange(P)[:, None] // ROWS == np.arange(G)[None, :]
    small[:, 32:40] = np.arange(NE) - NE
    small[:, 40:48] = np.arange(NE) * P
    small[:, 48:48 + NS] = np.arange(NS)
    small[:, 0:32] = np.arange(32)[None, :] == (np.arange(P) % 32)[:, None]
    arrays = {
        "x": np.asarray(x),
        "ctxT": np.asarray(ctx_1024).reshape(TOK, DC).T,
        "in_w": np.asarray(L0_xattn_in_proj_w).T,
        "xp_w": cat([bc, bc, bc, xp[:DR]]).T,
        "dt_w": cat([np.zeros((96, DM), np.float32), np.asarray(L0_xattn_dt_proj_w).T]),
        "chan": cat([np.asarray(L0_xattn_conv_w)] + [np.asarray(a)[:, None] for a in
                    (L0_xattn_conv_b, L0_xattn_dt_proj_b, L0_xattn_D)] + [np.asarray(L0_xattn_A_log)], axis=1),
        "pos": np.asarray(fside_BxSx2_0),
        "q_w": np.asarray(L1_xattn_Wq), "kv_w": np.asarray(L1_xattn_Wkv), "out_w": np.asarray(L1_xattn_Wout),
        "out_b": np.asarray(L1_xattn_bout)[None],
        "wr_w": np.asarray(L1_ffn_Wr).T, "br": np.asarray(L1_ffn_br)[None],
        "a_w": np.asarray(L1_ffn_A).reshape(NE * RANK, DM).T,
        "b_w": np.asarray(L1_ffn_B).transpose(0, 2, 1).reshape(NE * RANK, DM),
        "router_w": np.asarray(L0_ffn_router_w),
        "gu_w": cat([cat([np.asarray(L0_ffn_gate_w), np.asarray(L0_ffn_shared_gate_w)[None]]),
                     cat([np.asarray(L0_ffn_up_w), np.asarray(L0_ffn_shared_up_w)[None]])], axis=2),
        "down_w": cat([np.asarray(L0_ffn_down_w), np.asarray(L0_ffn_shared_down_w)[None]]),
        "consts": cat([np.eye(P, dtype=np.float32), np.triu(np.ones((P, P), np.float32), 1), small], axis=1),
    }
    nc = bacc.Bacc("TRN2", target_bir_lowering=False, num_devices=1)
    arrays = {f"in_{k}": np.ascontiguousarray(a) for k, a in arrays.items()}
    handles = {k[3:]: nc.dram_tensor(k, a.shape, mybir.dt.from_np(a.dtype), kind="ExternalInput").ap()
               for k, a in arrays.items()}
    out = nc.dram_tensor("out", (NB, L, DM), F32, kind="ExternalOutput").ap()
    build(nc, handles, out)
    return run_bass_kernel_spmd(nc, [arrays], core_ids=[0]).results[0]["out"]
```

```python
import math
from contextlib import ExitStack

import concourse.bass as bass
from concourse import mybir

F32 = mybir.dt.float32
F32R = mybir.dt.float32r
BF16 = mybir.dt.bfloat16
I32 = mybir.dt.int32
ALU = mybir.AluOpType
ACT = mybir.ActivationFunctionType
AX = mybir.AxisListType

P = 128
NB, L, DM = 4, 256, 256
DC = 128
TOK = NB * L
NT = TOK // P
KT = DM // P
DS, TAPS, DR = 16, 4, 8
LN_EPS = 1e-5
HALF = 512
NE, F = 8, 256
NS = TOK // P + NE


NH, HD = 32, 8
G = 4
NG = NB * NH // G
ROWS = 32
SLOTS = 4
SPLIT = 3 * HD
RANK = 64
LOW_BANKS = (0, 1, 7)
TWO_PI_HI = 6.28125
TWO_PI_LO = 2 * math.pi - TWO_PI_HI
PI_BELOW = 3.1415925
ROUND = 1.5 * 2.0 ** 23


def wait_from_one(eng, sem, value):
    if not isinstance(value, int) or value > 0:
        eng.wait_ge(sem, value)


class Chain:

    def __init__(self, eng, sem):
        self.eng, self.sem, self.n = eng, sem, 0

    def then_wait(self, ins):
        self.n += 1
        ins.then_inc(self.sem, 1)
        self.eng.wait_ge(self.sem, self.n)


def build(nc, h, out):
    ctx = ExitStack()
    with ctx:
        def sb(name, shape, dt=F32):
            return ctx.enter_context(nc.sbuf_tensor(name, shape, dt))

        def sem(name):
            return ctx.enter_context(nc.semaphore(name))

        ps = ctx.enter_context(nc.psum_tensor("ps", [P, 8, HALF], F32))

        def banks(a, n):
            return ps[:, a:a + n, :].rearrange("p b c -> p (b c)")

        x_tok = sb("x_tok", [P, NT, DM])
        ctxT = sb("ctxT", [P, TOK])
        consts = sb("consts", [P, 2 * P + 64 + G])
        ident, upper = consts[:, 0:P], consts[:, P:2 * P]
        head_rows = consts[:, 2 * P + 64:]
        ident3f = consts[:, 2 * P:2 * P + 32]
        in_w = sb("in_w", [P, DM])
        xp_w = sb("xp_w", [P, KT, 104])
        dt_w = sb("dt_w", [104, DM])
        chan = sb("chan", [P, KT, TAPS + 3 + DS])
        tap_w, conv_b = chan[:, :, 0:TAPS], chan[:, :, TAPS:TAPS + 1]
        dt_b, d_skip = chan[:, :, TAPS + 1:TAPS + 2], chan[:, :, TAPS + 2:TAPS + 3]
        a_log = chan[:, :, TAPS + 3:]
        neg_a = sb("neg_a", [P, KT, DS])
        ident3 = sb("ident3", [96, 32], BF16)
        diag_d = sb("diag_d", [P, KT, P])
        u = sb("u", [P, KT, TOK])
        delta = sb("delta", [P, KT, TOK])
        du = sb("du", [P, KT, TOK])
        gate_z = sb("gate_z", [P, KT, TOK])
        xdbl_all = sb("xdbl", [P, TOK])
        xdbl = xdbl_all[0:104, :]
        bc3 = sb("bc3", [96, TOK], BF16)
        decay = sb("decay", [P, 2, TOK])
        drive = sb("drive", [P, 2, TOK])
        state = sb("state", [P, 2, TOK])
        read = sb("read", [P, 2, TOK])
        c_rows = sb("c_rows", [P, 2, TOK])
        stats = sb("stats", [P, NT, 6])
        mean_var = sb("mean_var", [P, NT, 2])
        ln_var = sb("ln_var", [P, NT])
        rstd = sb("rstd", [P, NT])
        shift = sb("shift", [P, NT])
        eps_col, one_col = sb("eps_col", [P, 1]), sb("one_col", [P, 1])

        col = consts[:, 2 * P + 32:]
        e_minus_8, j_times_128, tile_no = col[:, 0:NE], col[:, NE:2 * NE], col[:, 2 * NE:2 * NE + NS]
        router_w = sb("router_w", [P, KT, NE])
        gu_w = sb("gu_w", [P, NE + 1, KT, 2 * F])
        down_w = sb("down_w", [P, NE + 1, KT, DM])
        upper_bf, ones_bf = sb("upper_bf", [P, P], BF16), sb("ones_bf", [P, P], BF16)
        xn = delta[:].rearrange("p k (t d) -> p (k t) d", d=DM)
        xnT = du
        hidT = drive
        scaled = decay[:].rearrange("p k (t d) -> p (k t) d", d=DM)
        routed = read[:].rearrange("p k (t d) -> p (k t) d", d=DM)
        silu_g = state[:].rearrange("p k (b c) -> p (k b) c", c=HALF)
        zero_rows = c_rows[:].rearrange("p k c -> p (k c)")
        logitT = sb("logitT", [NE, TOK])
        logit = sb("logit", [P, NT, NE])
        top = sb("top", [P, NT])
        pick = sb("pick", [P, NT, NE])
        first_e = sb("first_e", [P, NT])
        onehot = sb("onehot", [P, NT, NE], BF16)
        score = sb("score", [P, NT])
        full_tile = sb("full_tile", [P, NE, NE])
        tiles_e, tiles_upto, zeros8 = sb("tiles_e", [P, NE]), sb("tiles_upto", [P, NE]), sb("zeros8", [P, NE])
        slot_f, slot = sb("slot_f", [P, NT]), sb("slot", [P, NT], I32)
        tile_e, tile_ei = sb("tile_e", [1, NS]), sb("tile_ei", [1, NS], I32)
        tile_cmp = sb("tile_cmp", [1, NS, NE])
        xg = xdbl_all[:, 0:2 * DM].rearrange("p (k d) -> p k d", k=2)
        xgT = xdbl_all[:, 2 * DM:].rearrange("p (k c t) -> p k c t", k=2, c=KT)
        sg = ctxT[:, 0:2 * F].rearrange("p (k f) -> p k f", k=2)
        hid = ctxT[:, 2 * F:].rearrange("p (k f) -> p k f", k=2)
        hT = sb("hT", [P, 2, KT, P])
        yo = sb("yo", [P, 2, DM])
        pos = sb("pos", [P, NT, 2])
        angle, turns = sb("angle", [P, 2, NT, 4]), sb("turns", [P, 2, NT, 4])
        cos8 = sb("cos8", [P, NT, HD])
        sin_pos, sin_neg = sb("sin_pos", [P, NT, 4]), sb("sin_neg", [P, NT, 4])
        q_w, kv_w, out_w = sb("q_w", [P, KT, DM]), sb("kv_w", [P, 2 * DM]), sb("out_w", [P, KT, DM])
        out_b = sb("out_b", [P, DM])
        k_tok = gate_z[:].rearrange("p k (t d) -> p (k t) d", d=DM)
        v_tok = c_rows[:].rearrange("p k (g c) -> p (k g) c", c=2 * G * HD)
        swapped = u[:].rearrange("p k (t d) -> p (k t) d", d=DM)
        q_cos = drive[:].rearrange("p k (t d) -> p (k t) d", d=DM)
        rot = sb("rot", [P, NG, 2, 2 * G * HD])
        stack = gu_w[:, 2:4].rearrange("p e c (m g r) -> p (e c) m g r", g=G, r=ROWS)
        rowsT = [sb(f"rowsT{k}", [P, L], F32R) for k in range(2)]
        keysT = [sb(f"keysT{k}", [P, G, L], F32R) for k in range(SLOTS)]
        queryT = [sb(f"queryT{k}", [P, L], F32R) for k in range(2)]
        current = gu_w[:, 0].rearrange("p c (k n) -> p (c k) n", n=4 * G * HD)
        row_max = sb("row_max", [P, 2, 2, G])
        v_ones = gu_w[:, 4, 0].rearrange("p (k j g r) -> p k j g r", k=2, j=2, g=G)
        prob = [b[:].rearrange("p k (c n) -> p (k c) n", n=HALF) for b in (drive, state)]
        o_sb = gu_w[:, 1].rearrange("p c (k n) -> p (c k) n", n=L)
        inv_sum = sb("inv_sum", [P, 2, G])
        attn = delta
        attnT = decay
        wr_w, br_row = sb("wr_w", [P, KT, NE]), sb("br_row", [P, NE])
        a_w = gate_z[:, 0, :].rearrange("p (k c) -> p k c", k=KT)
        b_w = gate_z[:, 1, :].rearrange("p (k c) -> p k c", k=4)
        weight, pick_w = sb("weight", [P, NT]), sb("pick_w", [P, NT, NE])
        low = drive[:].rearrange("p k (c n) -> p (k c) n", n=HALF)
        lowT = state[:].rearrange("p k (c n) -> p (k c) n", n=HALF)
        sorted_x = nc.dram_tensor("sorted_x", (NS * P, DM), F32, kind="Internal").ap()
        sorted_y = nc.dram_tensor("sorted_y", (NS * P, DM), F32, kind="Internal").ap()

        x_loaded = sem("x_loaded")
        ctx_loaded = sem("ctx_loaded")
        ssm_w_loaded = sem("ssm_w_loaded")
        consts_loaded = sem("consts_loaded")
        out_stored = sem("out_stored")
        dve_own, act_own, pool_own = sem("dve_own"), sem("act_own"), sem("pool_own")
        xin_done = sem("xin_done")
        tap0_done = sem("tap0_done")
        conv_done = sem("conv_done")
        cols_set = sem("cols_set")
        ln0_stats = sem("ln0_stats")
        ln0_rstd = sem("ln0_rstd")
        ln0_shift = sem("ln0_shift")
        u_done = sem("u_done")
        xdbl_done = sem("xdbl_done")
        xdbl_copied = sem("xdbl_copied")
        dt_done = sem("dt_done")
        expa_done = sem("expa_done")
        setup_done = sem("setup_done")
        log_done = sem("log_done")
        delta_done = sem("delta_done")
        bc3_done = sem("bc3_done")
        b_ready, c_ready = sem("b_ready"), sem("c_ready")
        decay_ready = [sem(f"decay_ready{e}") for e in range(KT)]
        drive_done = sem("drive_done")
        scan_done = [sem(f"scan_done{e}") for e in range(KT)]
        c_copied = sem("c_copied")
        read_done = [sem(f"read_done{e}") for e in range(KT)]
        y_added = [sem(f"y_added{e}") for e in range(KT)]
        y_gated = sem("y_gated")
        y_turned = sem("y_turned")
        x1_done = sem("x1_done")
        ffn_w_loaded = sem("ffn_w_loaded")
        zeros_set, sorted_cleared = sem("zeros_set"), sem("sorted_cleared")
        ln_stats, ln_rstd, xn_done = sem("ln_stats"), sem("ln_rstd"), sem("xn_done")
        xn_turned = sem("xn_turned")
        xnT_copied = [sem(f"xnT_copied{k}") for k in range(2)]
        bf_consts = sem("bf_consts")
        logitT_done, logitT_copied = sem("logitT_done"), sem("logitT_copied")
        logit_turned = sem("logit_turned")
        onehot_done, top_done, exp_top_done = sem("onehot_done"), sem("top_done"), sem("exp_top_done")
        rank_done = sem("rank_done")
        tile_e_done, slot_done, scaled_done = sem("tile_e_done"), sem("slot_done"), sem("scaled_done")
        scattered = sem("scattered")
        shared_gu, shared_silu, shared_hid = sem("shared_gu"), sem("shared_silu"), sem("shared_hid")
        shared_down, shared_added = sem("shared_down"), sem("shared_added")
        xg_loaded = [sem(f"xg_loaded{k}") for k in range(2)]
        xg_turned, xgT_ready = sem("xg_turned"), sem("xgT_ready")
        gu_done, sg_done, hid_done = sem("gu_done"), sem("sg_done"), sem("hid_done")
        hid_turned, hT_ready, down_done = sem("hid_turned"), sem("hT_ready"), sem("down_done")
        yo_ready = sem("yo_ready")
        yo_stored = [sem(f"yo_stored{k}") for k in range(2)]
        gathered = sem("gathered")
        x2_done = sem("x2_done")
        pos_loaded, att_w_loaded, last_w_loaded = sem("pos_loaded"), sem("att_w_loaded"), sem("last_w_loaded")
        angle_done, trig_done, trig_ready = sem("angle_done"), sem("trig_done"), sem("trig_ready")
        kv_done, kv_copied = sem("kv_done"), sem("kv_copied")
        k_rotated, q_done, q_rotated = sem("k_rotated"), sem("q_done"), sem("q_rotated")
        pads_set, built = sem("pads_set"), sem("built")
        stack_turned, rowsT_ready = sem("stack_turned"), sem("rowsT_ready")
        keysT_act, keysT_dve = sem("keysT_act"), sem("keysT_dve")
        rows_done, max_done, shift_done = sem("rows_done"), sem("max_done"), sem("shift_done")
        query_turned, queryT_ready = sem("query_turned"), sem("queryT_ready")
        cols_done, exp_done, pv_done = sem("cols_done"), sem("exp_done"), sem("pv_done")
        o_copied, o_turned, attn_done = sem("o_copied"), sem("o_turned"), sem("attn_done")
        v_copied = sem("v_copied")
        current_ready = sem("current_ready")
        hi_built = sem("hi_built")
        shift_hi, inv_done = sem("shift_hi"), sem("inv_done")
        bias_added = sem("bias_added")
        attn_turned, proj_done, x3_done = sem("attn_turned"), sem("proj_done"), sem("x3_done")
        attnT_copied = [sem(f"attnT_copied{k}") for k in range(2)]
        shifted_done, exp_logit_done, pick_w_done = sem("shifted_done"), sem("exp_logit_done"), sem("pick_w_done")
        onehot2_done = sem("onehot2_done")
        low_done, low_masked, low_turned, lowT_ready = (sem("low_done"), sem("low_masked"), sem("low_turned"),
                                                        sem("lowT_ready"))
        last_done, tile_done = sem("last_done"), sem("tile_done")

        xin_ps = [banks(0, 2), banks(2, 2)]
        xdbl_ps = banks(4, 2)[0:104, :]
        dt_ps = xin_ps
        b_ps, c_ps = banks(0, 2), banks(2, 2)
        y_ps = [banks(4, 2), banks(6, 2)]
        turned = banks(0, 4).rearrange("p (t d) -> p t d", t=NT)

        logitT_ps = banks(4, 2)[0:NE, :]
        logit_ps = banks(6, 1)[:, 0:NT * NE].rearrange("p (t e) -> p t e", e=NE)
        rank_ps = banks(7, 1)[:, 0:NT * NE].rearrange("p (t e) -> p t e", e=NE)
        count_ps = banks(7, 1)[:, NT * NE:NT * NE + NE]

        def rotate(eng, x, swap, tiles):
            n = tiles.stop - tiles.start
            pairs = x.rearrange("p t (h c two) -> p t h c two", two=2, c=4)
            outs = swap.rearrange("p t (h c two) -> p t h c two", two=2, c=4)
            for m, sine in ((0, sin_neg), (1, sin_pos)):
                ins = eng.tensor_tensor(outs[:, :, :, :, m], pairs[:, :, :, :, 1 - m],
                                  sine[:, tiles].unsqueeze(2).to_broadcast([P, n, NH, 4]), ALU.mult)
            return ins

        def add_rotated(eng, x_cos, swap, which, b):
            def view(x):
                return x[:, 2 * b:2 * b + 2].rearrange("p j (g c) -> p g j c", c=G * HD)
            groups = rot[:].rearrange("p (b g) w (j c) -> p b g w j c", b=NB, j=2)
            return eng.tensor_tensor(groups[:, b, :, which], view(x_cos), view(swap), ALU.add)

        def rows_of(g, n):
            return slice(g * ROWS, g * ROWS + n)

        def run_turns(eng, turn):
            lead, tail = 8, NG - SLOTS
            for i in range(-1, lead):
                turn(i, i % SLOTS, lambda n, i=i: 0 <= i + n < NG)
            with eng.Fori(lead // SLOTS, tail // SLOTS) as m:
                for k in range(SLOTS):
                    turn(SLOTS * m + k, k, lambda n: True)
            for i in range(tail, NG + 3):
                turn(i, i % SLOTS, lambda n, i=i: 0 <= i + n < NG)

        block = ctx.enter_context(nc.Block())

        @block.sync
        def _(sp):
            sp.dma_start(pos[:], h["pos"].rearrange("b (l p) c -> p (b l) c", p=P)).then_inc(pos_loaded, 16)
            sp.dma_start(ctxT[:], h["ctxT"]).then_inc(ctx_loaded, 16)
            sp.dma_start(in_w[:], h["in_w"]).then_inc(ctx_loaded, 16)
            sp.dma_start(chan[:], h["chan"].rearrange("(k p) c -> p k c", p=P)).then_inc(ssm_w_loaded, 16)
            sp.dma_start(x_tok[:], h["x"].rearrange("b (l p) d -> p (b l) d", p=P)).then_inc(x_loaded, 16)
            sp.dma_start(consts[:], h["consts"]).then_inc(consts_loaded, 16)
            sp.dma_start(xp_w[:], h["xp_w"].rearrange("(k p) c -> p k c", p=P)).then_inc(ssm_w_loaded, 16)
            sp.dma_start(dt_w[:], h["dt_w"]).then_inc(ssm_w_loaded, 16)
            sp.wait_ge(zeros_set, 1)
            sp.dma_start(sorted_x.rearrange("(p r) d -> p (r d)", p=P)[:, 0:NS // 2 * DM], zero_rows).then_inc(sorted_cleared, 16)
            sp.dma_start(sorted_x.rearrange("(p r) d -> p (r d)", p=P)[:, NS // 2 * DM:], zero_rows).then_inc(sorted_cleared, 16)
            sp.dma_start(router_w[:], h["router_w"].rearrange("(k p) e -> p k e", p=P)).then_inc(ffn_w_loaded, 16)
            sp.dma_start(gu_w[:, NE], h["gu_w"][NE].rearrange("(k p) f -> p k f", p=P)).then_inc(ffn_w_loaded, 16)
            sp.dma_start(down_w[:, NE], h["down_w"][NE].rearrange("(k p) f -> p k f", p=P)).then_inc(ffn_w_loaded, 16)
            for e in range(NE):
                sp.dma_start(gu_w[:, e], h["gu_w"][e].rearrange("(k p) f -> p k f", p=P)).then_inc(ffn_w_loaded, 16)
                sp.dma_start(down_w[:, e], h["down_w"][e].rearrange("(k p) f -> p k f", p=P)).then_inc(ffn_w_loaded, 16)

            sp.dma_start(q_w[:], h["q_w"].rearrange("(k p) c -> p k c", p=P)).then_inc(att_w_loaded, 16)
            sp.dma_start(kv_w[:], h["kv_w"]).then_inc(att_w_loaded, 16)
            sp.dma_start(out_w[:], h["out_w"].rearrange("(k p) c -> p k c", p=P)).then_inc(att_w_loaded, 16)
            sp.dma_start(out_b[:], h["out_b"].to_broadcast([P, DM])).then_inc(att_w_loaded, 16)
            sp.dma_start(wr_w[:], h["wr_w"].rearrange("(k p) c -> p k c", p=P)).then_inc(last_w_loaded, 16)
            sp.dma_start(br_row[:], h["br"].to_broadcast([P, NE])).then_inc(last_w_loaded, 16)

            def load_tile(s, k, first):
                if not first:
                    sp.wait_ge(xg_turned, s - 1)
                sp.dma_start(xg[:, k, :], sorted_x[bass.ds(s * P, P), :]).then_inc(xg_loaded[k], 16)

            sp.wait_ge(scattered, 16 * NT)
            for s in range(2):
                load_tile(s, s, first=True)
            with nc.sync.Fori(1, NS // 2) as i:
                for k in range(2):
                    load_tile(2 * i + k, k, first=False)

            sp.wait_ge(k_rotated, 1)
            sp.dma_start(a_w, h["a_w"].rearrange("(k p) c -> p k c", p=P)).then_inc(last_w_loaded, 16)
            sp.dma_start(b_w, h["b_w"].rearrange("(k p) c -> p k c", p=P)).then_inc(last_w_loaded, 16)
            for t in range(NT):
                sp.wait_ge(tile_done, t + 1)
                sp.dma_start(out.rearrange("b (l p) d -> p (b l) d", p=P)[:, t, :], x_tok[:, t, :]) \
                  .then_inc(out_stored, 16)
            sp.wait_ge(out_stored, 16 * NT)

        @block.tensor
        def _(pe):
            mm = nc.tensor.matmul

            pe.wait_ge(ctx_loaded, 32)
            for et in range(KT):
                for c in range(2):
                    ins = mm(xin_ps[et][:, c * HALF:(c + 1) * HALF], in_w[:, et * P:(et + 1) * P],
                             ctxT[:, c * HALF:(c + 1) * HALF], start=True, stop=True)
                ins.then_inc(xin_done, 1)
            pe.wait_ge(ssm_w_loaded, 48)
            for et in range(KT):
                pe.wait_ge(u_done, et + 1)
                for c in range(2):
                    ins = mm(xdbl_ps[:, c * HALF:(c + 1) * HALF], xp_w[:, et, :],
                             u[:, et, c * HALF:(c + 1) * HALF], start=(et == 0), stop=(et == 1))
            ins.then_inc(xdbl_done, 1)
            pe.wait_ge(xdbl_copied, 1)
            pe.wait_ge(conv_done, 2)
            for et in range(KT):
                for c in range(2):
                    ins = mm(dt_ps[et][:, c * HALF:(c + 1) * HALF], dt_w[:, et * P:(et + 1) * P],
                             xdbl[:, c * HALF:(c + 1) * HALF], start=True, stop=True)
                ins.then_inc(dt_done, 1)
            pe.wait_ge(setup_done, 1)
            pe.wait_ge(bc3_done, 1)
            for et in range(KT):
                for c in range(2):
                    mm(y_ps[et][:, c * HALF:(c + 1) * HALF], diag_d[:, et, :],
                       u[:, et, c * HALF:(c + 1) * HALF], start=True, stop=False, skip_group_check=True)

            def spread_b(n):
                for c in range(2):
                    ins = mm(b_ps[:, c * HALF:(c + 1) * HALF], ident3[:, bass.ds(n, 1)].to_broadcast([96, P]),
                             bc3[:, c * HALF:(c + 1) * HALF], start=True, stop=True)
                ins.then_inc(b_ready, 1)

            def spread_c(n):
                for c in range(2):
                    ins = mm(c_ps[:, c * HALF:(c + 1) * HALF],
                             ident3[:, bass.ds(n + DS, 1)].to_broadcast([96, P]),
                             bc3[:, c * HALF:(c + 1) * HALF], start=True, stop=True)
                ins.then_inc(c_ready, 1)

            def add_y(n, last=False):
                for et in range(KT):
                    pe.wait_ge(read_done[et], n + 1)
                    for c in range(2):
                        ins = mm(y_ps[et][:, c * HALF:(c + 1) * HALF], ident,
                                 read[:, et, c * HALF:(c + 1) * HALF], start=False, stop=last,
                                 skip_group_check=True)
                    ins.then_inc(y_added[et], 1)

            pe.wait_ge(delta_done, 2)
            spread_b(0)
            spread_c(0)
            with nc.tensor.Fori(0, DS - 1) as n:
                pe.wait_ge(drive_done, 2 * n + 2)
                spread_b(n + 1)
                pe.wait_ge(c_copied, n + 1)
                spread_c(n + 1)
                add_y(n)
            add_y(DS - 1, last=True)

            for b in range(NB):
                for et in range(KT):
                    pe.wait_ge(y_gated, et + 1)
                    for lt in range(2):
                        ins = nc.tensor.transpose(turned[:, 2 * b + lt, et * P:(et + 1) * P],
                                                  u[:, et, b * L + lt * P:b * L + (lt + 1) * P], ident)
                if b % 2 == 1:
                    ins.then_inc(y_turned, 1)

            def turn_xn(r, b):
                pe.wait_ge(xn_done, NB * r + b + 1)
                for k in range(KT):
                    for t in (2 * b, 2 * b + 1):
                        ins = nc.tensor.transpose(ps[:, b, k * L + (t % 2) * P:k * L + (t % 2 + 1) * P],
                                                  xn[:, t, k * P:(k + 1) * P], ident)
                ins.then_inc(xn_turned, 1)

            def wait_xnT(r, b):
                pe.wait_ge(xnT_copied[b % 2], 2 * r + b // 2 + 1)

            def router(r, weights, c):
                wait_xnT(r, 2 * c)
                wait_xnT(r, 2 * c + 1)
                for k in range(KT):
                    ins = mm(logitT_ps[:, c * HALF:(c + 1) * HALF], weights[:, k, :],
                             xnT[:, k, c * HALF:(c + 1) * HALF], start=(k == 0), stop=(k == 1))
                ins.then_inc(logitT_done, 1)

            def turn_logits(n):
                for t in range(NT):
                    if t % 4 == 0:
                        pe.wait_ge(logitT_copied, 2 * n - 1 + t // 4)
                    ins = nc.tensor.transpose(logit_ps[:, t, :], logitT[:, t * P:(t + 1) * P], ident[0:NE, 0:NE])
                ins.then_inc(logit_turned, 1)

            pe.wait_ge(att_w_loaded, 64)
            for t in range(NT):
                if t >= 4:
                    pe.wait_ge(kv_copied, t - 3)
                mm(ps[:, 4 + t % 4, :], ctxT[:, t * P:(t + 1) * P], kv_w[:], start=True, stop=True) \
                    .then_inc(kv_done, 1)

            pe.wait_ge(x1_done, 2)
            for b in range(NB):
                turn_xn(0, b)
            pe.wait_ge(ffn_w_loaded, 16 * (3 + 2 * NE))
            pe.wait_ge(kv_copied, NT)
            for c in range(2):
                router(0, router_w, c)

            def shared_half(j, g):
                c, ft = j // 2, j % 2
                if j >= 2 and g == 0:
                    pe.wait_ge(shared_hid, j - 1)
                for k in range(KT):
                    ins = mm(ps[:, 2 * (j % 2) + g, :], gu_w[:, NE, k, g * F + ft * P:g * F + (ft + 1) * P],
                             xnT[:, k, c * HALF:(c + 1) * HALF], start=(k == 0), stop=(k == 1))
                ins.then_inc(shared_gu, 1)

            shared_half(0, 0)
            turn_logits(1)
            shared_half(0, 1)
            pe.wait_ge(onehot_done, 1)
            pe.wait_ge(bf_consts, 1)
            mm(rank_ps, upper_bf[:], onehot[:], start=True, stop=False, skip_group_check=True)
            for t in range(NT - 1):
                mm(rank_ps[:, t + 1:, :], ones_bf[:], onehot[:, t:t + 1, :].to_broadcast([P, NT - 1 - t, NE]),
                   start=False, stop=True, skip_group_check=True)
            for t in range(NT):
                ins = mm(count_ps, ones_bf[:], onehot[:, t, :], start=False, stop=(t == NT - 1),
                         skip_group_check=True)
            ins.then_inc(rank_done, 1)
            for j in range(1, 4):
                for g in range(2):
                    shared_half(j, g)
            for j in range(4):
                pe.wait_ge(shared_hid, 2 * (j // 2) + 2)
                if j >= 2:
                    pe.wait_ge(shared_added, j - 1)
                for t in (2 * j, 2 * j + 1):
                    for ft in range(KT):
                        ins = mm(ps[:, 4 + j % 2, (t % 2) * DM:(t % 2 + 1) * DM], hidT[:, ft, t * P:(t + 1) * P],
                                 down_w[:, NE, ft, :], start=(ft == 0 and t % 2 == 0), stop=(ft == 1),
                                 skip_group_check=True)
                ins.then_inc(shared_down, 1)

            pe.wait_ge(shared_added, 4)
            pe.wait_ge(tile_e_done, 1)

            def turn_x(s, k, first, pair=None):
                pe.wait_ge(xg_loaded[k], 16 * ((s // 2 if pair is None else pair) + 1))
                if not first:
                    pe.wait_ge(xgT_ready, s - 1)
                for c in range(KT):
                    ins = nc.tensor.transpose(ps[:, k, c * P:(c + 1) * P], xg[:, k, c * P:(c + 1) * P], ident)
                ins.then_inc(xg_turned, 1)

            def expert(s):
                return pe.value_load(tile_ei[0:1, bass.ds(s, 1)], min_val=0, max_val=NE - 1)

            def gate_up(s, k, e, first):
                pe.wait_ge(xgT_ready, s + 1)
                if not first:
                    pe.wait_ge(hid_done, s - 1)
                for c in range(KT):
                    ins = mm(ps[:, 2 + k, :], xgT[:, k, c, :],
                             gu_w[:, bass.ds(e, 1), c, :].rearrange("p e f -> p (e f)"),
                             start=(c == 0), stop=(c == 1))
                ins.then_inc(gu_done, 1)

            def turn_hidden(s, k, first):
                pe.wait_ge(hid_done, s + 1)
                if not first:
                    pe.wait_ge(hT_ready, s - 1)
                for c in range(KT):
                    ins = nc.tensor.transpose(ps[:, 4 + k, c * P:(c + 1) * P], hid[:, k, c * P:(c + 1) * P], ident)
                ins.then_inc(hid_turned, 1)

            def down(s, k, e, first):
                pe.wait_ge(hT_ready, s + 1)
                if not first:
                    pe.wait_ge(yo_ready, s - 1)
                for c in range(KT):
                    ins = mm(ps[:, 6 + k, 0:DM], hT[:, k, c, :],
                             down_w[:, bass.ds(e, 1), c, :].rearrange("p e f -> p (e f)"),
                             start=(c == 0), stop=(c == 1))
                ins.then_inc(down_done, 1)

            def expert_turn(s, k, pair=None, ahead=True):
                early = isinstance(s, int) and s < 4
                e, e_before = expert(s), expert(s - 1)
                turn_hidden(s - 1, 1 - k, early and s < 3)
                gate_up(s, k, e, early and s < 2)
                down(s - 1, 1 - k, e_before, early and s < 3)
                if ahead:
                    turn_x(s + 2, k, False, pair)

            turn_x(0, 0, True)
            turn_x(1, 1, True)
            gate_up(0, 0, expert(0), True)
            turn_x(2, 0, False)
            for s in range(1, 4):
                expert_turn(s, s % 2)
            with nc.tensor.Fori(2, NS // 2 - 1) as i:
                for k in range(2):
                    expert_turn(2 * i + k, k, pair=i + 1)
            for s in (NS - 2, NS - 1):
                expert_turn(s, s % 2, ahead=False)
            e_last = expert(NS - 1)
            turn_hidden(NS - 1, 1, False)
            down(NS - 1, 1, e_last, False)

            pe.wait_ge(yo_ready, NS)

            def queries(b):
                wait_xnT(1, b)
                for t in (2 * b, 2 * b + 1):
                    for k in range(KT):
                        ins = mm(ps[:, 4 + b, (t % 2) * DM:(t % 2 + 1) * DM], xnT[:, k, t * P:(t + 1) * P],
                                 q_w[:, k, :], start=(k == 0 and t % 2 == 0), stop=(k == 1),
                                 skip_group_check=True)
                ins.then_inc(q_done, 1)

            turn_xn(1, 0)
            for b in range(NB):
                if b + 1 < NB:
                    turn_xn(1, b + 1)
                queries(b)

            def turn_stack(i, k):
                pe.wait_ge(built, i + 1)
                wait_from_one(pe, keysT_act, i)
                wait_from_one(pe, keysT_dve, i)
                for n in range(4):
                    ins = nc.tensor.transpose(ps[:, 0, n * P:(n + 1) * P],
                                              stack[:, k, n].rearrange("p g r -> p (g r)"), ident)
                ins.then_inc(stack_turned, 1)

            def logit_rows(i, k, n):
                if n == 0:
                    pe.wait_ge(keysT_act, i + 1)
                    pe.wait_ge(keysT_dve, i + 1)
                wait_from_one(pe, max_done, G * i + n - 1)
                heads, j = n // 2, n % 2
                mm(ps[:, 2 + n % 2, :], rowsT[k % 2][:, j * P:(j + 1) * P],
                   keysT[k][:, 2 * heads:2 * heads + 2, :].rearrange("p g n -> p (g n)")).then_inc(rows_done, 1)

            def turn_queries(i, k):
                pe.wait_ge(shift_done, i + 1)
                wait_from_one(pe, queryT_ready, i)
                for n in range(2):
                    ins = nc.tensor.transpose(ps[:, 1, n * P:(n + 1) * P],
                                              stack[:, k, n].rearrange("p g r -> p (g r)"), ident)
                ins.then_inc(query_turned, 1)

            def logit_cols(i, k, g):
                if g == 0:
                    pe.wait_ge(queryT_ready, i + 1)
                wait_from_one(pe, exp_done, G * i + g - 1)
                for j in range(2):
                    ins = mm(ps[:, 4 + g % 2, j * L:(j + 1) * L], keysT[k][:, g, j * P:(j + 1) * P],
                             queryT[k % 2][:], start=(j == 0), stop=True,
                             skip_group_check=True)
                ins.then_inc(cols_done, 1)

            def values(i, k, g):
                pe.wait_ge(exp_done, G * i + g + 1)
                if g == 0:
                    pe.wait_ge(v_copied, i + 1)
                    wait_from_one(pe, o_copied, i)
                for j in range(2):
                    ins = mm(ps[rows_of(g, ROWS), 6, 0:L], v_ones[:, k % 2, j, g, :],
                             prob[k % 2][:, g, j * L:(j + 1) * L], start=(j == 0), stop=(j == 1),
                             tile_position=(0, g * ROWS))
                ins.then_inc(pv_done, 1)

            def turn_values(i, k):
                pe.wait_ge(o_copied, i + 1)
                wait_from_one(pe, attn_done, i)
                for n in range(2):
                    ins = nc.tensor.transpose(ps[:, 7, n * P:(n + 1) * P], o_sb[:, k % 2, n * P:(n + 1) * P], ident)
                ins.then_inc(o_turned, 1)

            def attention_turn(i, k, live):
                if live(-2):
                    values(i - 2, (k + 2) % SLOTS, 0)
                if live(-3):
                    turn_values(i - 3, (k + 1) % SLOTS)
                if live(0):
                    logit_rows(i, k, 0)
                if live(-1):
                    turn_queries(i - 1, (k + 3) % SLOTS)
                if live(1):
                    turn_stack(i + 1, (k + 1) % SLOTS)
                if live(0):
                    logit_rows(i, k, 1)
                if live(-2):
                    values(i - 2, (k + 2) % SLOTS, 1)
                    values(i - 2, (k + 2) % SLOTS, 2)
                    values(i - 2, (k + 2) % SLOTS, 3)
                if live(-1):
                    logit_cols(i - 1, (k + 3) % SLOTS, 0)
                    logit_cols(i - 1, (k + 3) % SLOTS, 1)
                if live(0):
                    logit_rows(i, k, 2)
                    logit_rows(i, k, 3)
                if live(-1):
                    logit_cols(i - 1, (k + 3) % SLOTS, 2)
                    logit_cols(i - 1, (k + 3) % SLOTS, 3)

            run_turns(nc.tensor, attention_turn)

            def turn_attn(b):
                for f in range(KT):
                    for j in range(2):
                        ins = nc.tensor.transpose(ps[:, b, f * L + j * P:f * L + (j + 1) * P],
                                                  attn[:, j, b * DM + f * P:b * DM + (f + 1) * P], ident)
                ins.then_inc(attn_turned, 1)

            def project(b):
                pe.wait_ge(attnT_copied[b % 2], b // 2 + 1)
                for t in (2 * b, 2 * b + 1):
                    for k in range(KT):
                        ins = mm(ps[:, 4 + b, (t % 2) * DM:(t % 2 + 1) * DM], attnT[:, k, t * P:(t + 1) * P],
                                 out_w[:, k, :], start=(k == 0 and t % 2 == 0), stop=(k == 1),
                                 skip_group_check=True)
                ins.then_inc(proj_done, 1)

            pe.wait_ge(attn_done, NG)
            turn_attn(0)
            for b in range(NB):
                if b + 1 < NB:
                    turn_attn(b + 1)
                project(b)
                if b >= 2:
                    turn_xn(2, b - 2)

            pe.wait_ge(last_w_loaded, 64)
            turn_xn(2, 2)
            router(2, wr_w, 0)
            turn_xn(2, 3)
            router(2, wr_w, 1)

            def low_rank(t):
                if t >= 3:
                    pe.wait_ge(low_masked, t - 2)
                for k in range(KT):
                    ins = mm(ps[:, LOW_BANKS[t % 3], :], xnT[:, k, t * P:(t + 1) * P], a_w[:, k, :], start=(k == 0), stop=(k == 1))
                ins.then_inc(low_done, 1)

            def turn_low(t):
                pe.wait_ge(low_masked, t + 1)
                if t >= 2:
                    pe.wait_ge(lowT_ready, t - 1)
                for c in range(4):
                    ins = nc.tensor.transpose(ps[:, 2 + t % 2, c * P:(c + 1) * P], low[:, t % 2, c * P:(c + 1) * P],
                                              ident)
                ins.then_inc(low_turned, 1)

            def high(t):
                pe.wait_ge(lowT_ready, t + 1)
                if t >= 2:
                    pe.wait_ge(tile_done, t - 1)
                elif t == 0:
                    pe.wait_ge(logitT_copied, 4)
                for c in range(4):
                    ins = mm(ps[:, 4 + t % 2, 0:DM], lowT[:, t % 2, c * P:(c + 1) * P], b_w[:, c, :],
                             start=(c == 0), stop=(c == 3))
                ins.then_inc(last_done, 1)

            low_rank(0)
            turn_logits(2)
            low_rank(1)
            low_rank(2)
            for t in range(NT + 1):
                if t < NT:
                    turn_low(t)
                if t + 3 < NT:
                    low_rank(t + 3)
                if t >= 1:
                    high(t - 1)

        @block.scalar
        def _(act):
            own = Chain(act, act_own)
            nc.scalar.preload_act_table_set("natural_log_exp_and_others")
            act.wait_ge(ssm_w_loaded, 48)
            nc.scalar.activation(neg_a[:], a_log, ACT.Exp).then_inc(expa_done, 1)
            act.wait_ge(ln0_stats, 1)
            act.wait_ge(cols_set, 1)
            own.then_wait(nc.scalar.activation(ln_var[:], mean_var[:, :, 1], ACT.Ln, bias=eps_col[:]))
            nc.scalar.activation(rstd[:], ln_var[:], ACT.Exp, scale=-0.5).then_inc(ln0_rstd, 1)
            for et in range(KT):
                act.wait_ge(xin_done, et + 1)
                nc.scalar.activation(delta[:, et, :], xin_ps[et], ACT.Identity, bias=conv_b[:, et, :],
                                     scale=tap_w[:, et, TAPS - 1:TAPS]).then_inc(tap0_done, 1)
            nc.scalar.preload_act_table_set("silu_and_others")
            act.wait_ge(ln0_shift, 1)
            for b in range(NB):
                for et in range(KT):
                    t = 2 * b + et
                    nc.scalar.activation(gate_z[:, et, b * L:(b + 1) * L], x_tok[:, t, :], ACT.Silu,
                                         bias=shift[:, t:t + 1], scale=rstd[:, t:t + 1])
            act.wait_ge(angle_done, 1)
            nc.scalar.activation(angle[:], angle[:], ACT.Sin).then_inc(trig_done, 1)
            for et in range(KT):
                act.wait_ge(conv_done, et + 1)
                nc.scalar.activation(u[:, et, :], delta[:, et, :], ACT.Silu).then_inc(u_done, 1)
            nc.scalar.preload_act_table_set("natural_log_exp_and_others")
            act.wait_ge(xdbl_done, 1)
            nc.scalar.copy(xdbl[:], xdbl_ps).then_inc(xdbl_copied, 1)
            for et in range(KT):
                act.wait_ge(dt_done, et + 1)
                own.then_wait(nc.scalar.activation(state[:, et, :], dt_ps[et], ACT.Identity, bias=dt_b[:, et, :]))
                own.then_wait(nc.scalar.activation(read[:, et, :], state[:, et, :], ACT.Abs))
                own.then_wait(nc.scalar.activation(read[:, et, :], read[:, et, :], ACT.Exp, scale=-1.0))
                nc.scalar.activation(read[:, et, :], read[:, et, :], ACT.Ln, bias=one_col[:]).then_inc(log_done, 1)

            def decay_and_c(n, k, first):
                act.wait_ge(c_ready, n + 1)
                if not first:
                    act.wait_ge(read_done[1], n - 1)
                elif k == 0:
                    act.wait_ge(sorted_cleared, 32)
                nc.scalar.copy(c_rows[:, k, :], c_ps).then_inc(c_copied, 1)
                for et in range(KT):
                    act.wait_ge(delta_done, et + 1)
                    if not first or k > 0:
                        act.wait_ge(scan_done[et], n)
                    nc.scalar.activation(
                        decay[:, et, :].rearrange("p (b l) -> p b l", b=NB)[:, :, 1:],
                        delta[:, et, :].rearrange("p (b l) -> p b l", b=NB)[:, :, 1:],
                        ACT.Exp, scale=neg_a[:, et, bass.ds(n, 1)]).then_inc(decay_ready[et], 1)

            act.wait_ge(setup_done, 1)
            for k in range(2):
                decay_and_c(k, k, first=True)
            with nc.scalar.Fori(1, DS // 2) as i:
                for k in range(2):
                    decay_and_c(2 * i + k, k, first=False)

            def norm_rstd(r, b):
                act.wait_ge(ln_stats, NB * r + b + 1)
                own.then_wait(nc.scalar.activation(ln_var[:, 2 * b:2 * b + 2], mean_var[:, 2 * b:2 * b + 2, 1], ACT.Ln,
                                                   bias=eps_col[:]))
                nc.scalar.activation(rstd[:, 2 * b:2 * b + 2], ln_var[:, 2 * b:2 * b + 2], ACT.Exp, scale=-0.5) \
                    .then_inc(ln_rstd, 1)

            def copy_xnT(r, b):
                act.wait_ge(xn_turned, NB * r + b + 1)
                nc.scalar.copy(xnT[:, :, b * L:(b + 1) * L], ps[:, b, :].rearrange("p (k n) -> p k n", k=KT)) \
                    .then_inc(xnT_copied[0], 1)

            def copy_kv(t):
                b, j = t // 2, t % 2
                act.wait_ge(kv_done, t + 1)
                nc.scalar.copy(k_tok[:, t, :], ps[:, 4 + t % 4, 0:DM])
                nc.scalar.copy(v_tok[:, 8 * b:8 * b + 8, j * G * HD:(j + 1) * G * HD],
                               ps[:, 4 + t % 4, DM:2 * DM].rearrange("p (g c) -> p g c", c=G * HD)).then_inc(kv_copied, 1)

            for t in range(NT):
                copy_kv(t)
                if t >= 4:
                    norm_rstd(0, t - 4)
            copy_xnT(0, 0)
            copy_xnT(0, 2)
            for c in range(2):
                act.wait_ge(logitT_done, 1 + c)
                nc.scalar.copy(logitT[:, c * HALF:(c + 1) * HALF], logitT_ps[:, c * HALF:(c + 1) * HALF]) \
                    .then_inc(logitT_copied, 1)
            act.wait_ge(top_done, 1)
            nc.scalar.activation(score[:], top[:], ACT.Exp, scale=-1.0).then_inc(exp_top_done, 1)
            nc.scalar.preload_act_table_set("silu_and_others")
            for j in range(4):
                act.wait_ge(shared_gu, 2 * j + 1)
                nc.scalar.activation(silu_g[:, j, :], ps[:, 2 * (j % 2), :], ACT.Silu).then_inc(shared_silu, 1)

            def silu_tile(s, k, first):
                act.wait_ge(gu_done, s + 1)
                if not first:
                    act.wait_ge(hid_done, s - 1)
                nc.scalar.activation(sg[:, k, :], ps[:, 2 + k, 0:F], ACT.Silu).then_inc(sg_done, 1)

            def copy_hT(s, k, first):
                act.wait_ge(hid_turned, s + 1)
                if not first:
                    act.wait_ge(down_done, s - 1)
                nc.scalar.copy(hT[:, k].rearrange("p c t -> p (c t)"), ps[:, 4 + k, 0:F]).then_inc(hT_ready, 1)

            for s in range(2):
                silu_tile(s, s, True)
                copy_hT(s, s, True)
            with nc.scalar.Fori(1, NS // 2) as i:
                for k in range(2):
                    silu_tile(2 * i + k, k, False)
                    copy_hT(2 * i + k, k, False)

            nc.scalar.preload_act_table_set("natural_log_exp_and_others")
            for b in range(NB):
                norm_rstd(1, b)
                if b % 2 == 1:
                    copy_xnT(1, b - 1)

            def copy_rowsT(i, k):
                act.wait_ge(stack_turned, i + 1)
                wait_from_one(act, rows_done, G * (i - 1))
                nc.scalar.copy(rowsT[k % 2][:], ps[:, 0, 0:L]).then_inc(rowsT_ready, 1)

            def spread_keys(i, k):
                wait_from_one(act, cols_done, G * (i + 1 - SLOTS))
                for g in range(G // 2):
                    ins = nc.scalar.copy(keysT[k][rows_of(g, ROWS), g, :], ps[rows_of(g, ROWS), 0, L:2 * L])
                ins.then_inc(keysT_act, 1)

            def copy_queryT(i, k):
                act.wait_ge(query_turned, i + 1)
                wait_from_one(act, cols_done, G * (i - 1))
                nc.scalar.copy(queryT[k % 2][:], ps[:, 1, 0:L]).then_inc(queryT_ready, 1)

            def exponential(i, k, g):
                act.wait_ge(cols_done, G * i + g + 1)
                wait_from_one(act, pv_done, G * (i - 2) + g + 1)
                nc.scalar.activation(prob[k % 2][:, g, :], ps[:, 4 + g % 2, :], ACT.Exp, scale=HD ** -0.5) \
                    .then_inc(exp_done, 1)

            def copy_o(i, k):
                act.wait_ge(pv_done, G * i + G)
                wait_from_one(act, o_turned, i - 1)
                nc.scalar.copy(o_sb[:, k % 2, :], ps[:, 6, 0:L]).then_inc(o_copied, 1)

            def attention_turn(i, k, live):
                if live(-1):
                    copy_queryT(i - 1, (k + 3) % SLOTS)
                if live(1):
                    copy_rowsT(i + 1, (k + 1) % SLOTS)
                    spread_keys(i + 1, (k + 1) % SLOTS)
                if live(-1):
                    exponential(i - 1, (k + 3) % SLOTS, 0)
                    exponential(i - 1, (k + 3) % SLOTS, 1)
                if live(-2):
                    copy_o(i - 2, (k + 2) % SLOTS)
                if live(-1):
                    exponential(i - 1, (k + 3) % SLOTS, 2)
                    exponential(i - 1, (k + 3) % SLOTS, 3)

            run_turns(nc.scalar, attention_turn)

            for b in (0, 2):
                act.wait_ge(attn_turned, b + 1)
                nc.scalar.copy(attnT[:, :, b * L:(b + 1) * L], ps[:, b, :].rearrange("p (k n) -> p k n", k=KT)) \
                    .then_inc(attnT_copied[0], 1)
                if b == 2:
                    norm_rstd(2, 0)
            norm_rstd(2, 1)
            copy_xnT(2, 0)
            norm_rstd(2, 2)
            norm_rstd(2, 3)
            copy_xnT(2, 2)
            for c in range(2):
                act.wait_ge(logitT_done, 3 + c)
                nc.scalar.copy(logitT[:, c * HALF:(c + 1) * HALF], logitT_ps[:, c * HALF:(c + 1) * HALF]) \
                    .then_inc(logitT_copied, 1)
            act.wait_ge(shifted_done, 1)
            nc.scalar.activation(pick_w[:], pick_w[:], ACT.Exp).then_inc(exp_logit_done, 1)
            for t in range(NT):
                act.wait_ge(low_turned, t + 1)
                if t >= 2:
                    act.wait_ge(last_done, t - 1)
                nc.scalar.copy(lowT[:, t % 2, :], ps[:, 2 + t % 2, :]).then_inc(lowT_ready, 1)

        @block.vector
        def _(dve):
            own = Chain(dve, dve_own)
            vec = nc.vector

            def layer_norm_stats(done, tiles):
                for t in tiles:
                    ins = vec.bn_stats(stats[:, t, :], x_tok[:, t, :])
                own.then_wait(ins)
                for t in tiles:
                    ins = vec.bn_aggr(mean_var[:, t, :], stats[:, t, :])
                ins.then_inc(done, 1)

            dve.wait_ge(pos_loaded, 16)
            pos2 = pos[:].rearrange("p t c -> p (t c)")
            flat = [angle[:, c].rearrange("p t (c h) -> p (t c) h", h=2) for c in range(2)]
            for half in range(2):
                freq = 10000.0 ** (-half / 2)
                vec.tensor_scalar(flat[0][:, :, half], pos2, freq, None, ALU.mult)
                ins = vec.tensor_scalar(flat[1][:, :, half], pos2, freq, math.pi / 2, ALU.mult, ALU.add)
            own.then_wait(ins)
            own.then_wait(vec.tensor_scalar(turns[:], angle[:], 1 / (2 * math.pi), ROUND, ALU.mult, ALU.add))
            own.then_wait(vec.tensor_scalar(turns[:], turns[:], ROUND, None, ALU.subtract))
            for part in (TWO_PI_HI, TWO_PI_LO):
                own.then_wait(vec.scalar_tensor_tensor(out=angle[:], in0=turns[:], scalar=-part, in1=angle[:],
                                                       op0=ALU.mult, op1=ALU.add))
            vec.tensor_scalar(angle[:], angle[:], PI_BELOW, -PI_BELOW, ALU.min, ALU.max).then_inc(angle_done, 1)

            dve.wait_ge(x_loaded, 16)
            layer_norm_stats(ln0_stats, range(NT))
            dve.wait_ge(ln0_rstd, 1)
            vec.scalar_tensor_tensor(out=shift[:], in0=mean_var[:, :, 0], scalar=-1.0, in1=rstd[:],
                                     op0=ALU.mult, op1=ALU.mult).then_inc(ln0_shift, 1)
            for j in range(TAPS - 1):
                back = TAPS - 1 - j
                for et in range(KT):
                    if j == 0:
                        dve.wait_ge(tap0_done, et + 1)
                    acc = delta[:, et, :].rearrange("p (b l) -> p b l", b=NB)[:, :, back:]
                    xin = xin_ps[et].rearrange("p (b l) -> p b l", b=NB)[:, :, 0:L - back]
                    ins = vec.scalar_tensor_tensor(out=acc, in0=xin, scalar=tap_w[:, et, j:j + 1], in1=acc,
                                                   op0=ALU.mult, op1=ALU.add)
                    if j == TAPS - 2:
                        ins.then_inc(conv_done, 1)
                if j < TAPS - 2:
                    own.then_wait(ins)

            dve.wait_ge(xdbl_copied, 1)
            rest = drive[0:96, 0, :]
            own.then_wait(vec.tensor_copy(bc3[:], xdbl[0:96, :]))
            own.then_wait(vec.tensor_tensor(rest, xdbl[0:96, :], bc3[:], ALU.subtract))
            vec.tensor_copy(bc3[32:64, :], rest[32:64, :])
            own.then_wait(vec.tensor_copy(bc3[64:96, :], rest[64:96, :]))
            vec.tensor_tensor(bc3[64:96, :], rest[64:96, :], bc3[64:96, :], ALU.subtract).then_inc(bc3_done, 1)

            for et in range(KT):
                dve.wait_ge(log_done, et + 1)
                vec.scalar_tensor_tensor(out=delta[:, et, :], in0=state[:, et, :], scalar=0.0, in1=read[:, et, :],
                                         op0=ALU.max, op1=ALU.add).then_inc(delta_done, 1)
                dve.wait_ge(delta_done, et + 1)
                ins = vec.tensor_tensor(du[:, et, :], delta[:, et, :], u[:, et, :], ALU.mult)
            own.then_wait(ins)

            def scan_state(n, first):
                dve.wait_ge(b_ready, n + 1)
                for et in range(KT):
                    if not first:
                        dve.wait_ge(scan_done[et], n)
                    vec.tensor_tensor(drive[:, et, :], du[:, et, :], b_ps, ALU.mult).then_inc(drive_done, 1)
                for et in range(KT):
                    dve.wait_ge(decay_ready[et], n + 1)
                    dve.wait_ge(drive_done, 2 * n + et + 1)
                    if not first:
                        dve.wait_ge(read_done[et], n)
                    vec.tensor_tensor_scan(state[:, et, :], decay[:, et, :], drive[:, et, :], 0.0,
                                           ALU.mult, ALU.add).then_inc(scan_done[et], 1)

            scan_state(0, True)
            with nc.vector.Fori(1, DS) as n:
                scan_state(n, False)

            for et in range(KT):
                dve.wait_ge(y_added[et], DS)
                vec.tensor_tensor(u[:, et, :], y_ps[et], gate_z[:, et, :], ALU.mult).then_inc(y_gated, 1)
            for c in range(2):
                dve.wait_ge(y_turned, c + 1)
                vec.tensor_tensor(x_tok[:, 4 * c:4 * c + 4, :], x_tok[:, 4 * c:4 * c + 4, :],
                                  turned[:, 4 * c:4 * c + 4, :], ALU.add).then_inc(x1_done, 1)

            def batch_stats(b):
                layer_norm_stats(ln_stats, (2 * b, 2 * b + 1))

            def normalise(r, b):
                dve.wait_ge(ln_rstd, NB * r + b + 1)
                for t in (2 * b, 2 * b + 1):
                    ins = vec.tensor_scalar(xn[:, t, :], x_tok[:, t, :], mean_var[:, t, 0:1], rstd[:, t:t + 1],
                                            ALU.subtract, ALU.mult)
                ins.then_inc(xn_done, 1)

            def copy_xnT(r, b):
                dve.wait_ge(xn_turned, NB * r + b + 1)
                vec.tensor_copy(xnT[:, :, b * L:(b + 1) * L], ps[:, b, :].rearrange("p (k n) -> p k n", k=KT)) \
                   .then_inc(xnT_copied[1], 1)

            def first_of_top(done):
                vec.tensor_reduce(top[:], logit[:], AX.X, ALU.max).then_inc(top_done, 1)
                dve.wait_ge(top_done, 1 if done is onehot_done else 2)
                own.then_wait(vec.tensor_tensor(pick[:], logit[:], top[:].unsqueeze(2).to_broadcast([P, NT, NE]),
                                                ALU.is_equal))
                own.then_wait(vec.tensor_tensor(pick[:], pick[:], e_minus_8.unsqueeze(1).to_broadcast([P, NT, NE]),
                                                ALU.mult))
                own.then_wait(vec.tensor_reduce(first_e[:], pick[:], AX.X, ALU.min))
                vec.tensor_tensor(onehot[:], e_minus_8.unsqueeze(1).to_broadcast([P, NT, NE]),
                                  first_e[:].unsqueeze(2).to_broadcast([P, NT, NE]), ALU.is_equal) \
                   .then_inc(done, 1)

            dve.wait_ge(trig_done, 1)
            vec.tensor_copy(cos8[:].rearrange("p t (c h) -> p (t c) h", h=2),
                            angle[:, 1].rearrange("p t c -> p (t c)").unsqueeze(2).to_broadcast([P, NT * 4, 2]))
            vec.tensor_copy(sin_pos[:], angle[:, 0])
            vec.tensor_scalar(sin_neg[:], angle[:, 0], -1.0, None, ALU.mult).then_inc(trig_ready, 1)
            for b in range(NB):
                dve.wait_ge(x1_done, b // 2 + 1)
                batch_stats(b)
                if b >= 1:
                    normalise(0, b - 1)
            normalise(0, NB - 1)
            vec.memset(ones_bf[:], 1.0)
            vec.memset(zeros8[:], 0.0)
            vec.tensor_copy(upper_bf[:], upper).then_inc(bf_consts, 1)
            copy_xnT(0, 1)
            copy_xnT(0, 3)
            dve.wait_ge(logit_turned, 1)
            own.then_wait(vec.tensor_copy(logit[:], logit_ps))
            first_of_top(onehot_done)

            def multiply_shared(j):
                dve.wait_ge(shared_gu, 2 * j + 2)
                dve.wait_ge(shared_silu, j + 1)
                vec.tensor_tensor(hidT[:, j % 2, (j // 2) * HALF:(j // 2 + 1) * HALF], ps[:, 2 * (j % 2) + 1, :],
                                  silu_g[:, j, :], ALU.mult).then_inc(shared_hid, 1)

            multiply_shared(0)
            dve.wait_ge(onehot_done, 1)
            dve.wait_ge(rank_done, 1)
            own.then_wait(vec.tensor_copy(tiles_e[:], count_ps))
            own.then_wait(vec.tensor_tensor(full_tile[:], tiles_e[:].unsqueeze(2).to_broadcast([P, NE, NE]),
                                            j_times_128.unsqueeze(1).to_broadcast([P, NE, NE]), ALU.is_gt))
            own.then_wait(vec.tensor_reduce(tiles_e[:], full_tile[:], AX.X, ALU.add))
            own.then_wait(vec.tensor_tensor_scan(tiles_upto[:], tiles_e[:], zeros8[:], 0.0, ALU.add, ALU.add))
            own.then_wait(vec.tensor_tensor(tiles_e[:], tiles_upto[:], tiles_e[:], ALU.subtract))
            own.then_wait(vec.scalar_tensor_tensor(
                out=pick[:], in0=tiles_e[:].unsqueeze(1).to_broadcast([P, NT, NE]), scalar=float(P), in1=rank_ps,
                op0=ALU.mult, op1=ALU.add))
            own.then_wait(vec.tensor_tensor(pick[:], pick[:], onehot[:], ALU.mult))
            own.then_wait(vec.tensor_reduce(slot_f[:], pick[:], AX.X, ALU.add))
            vec.tensor_copy(slot[:], slot_f[:]).then_inc(slot_done, 1)
            own.then_wait(vec.tensor_tensor(tile_cmp[:], tiles_upto[0:1, :].unsqueeze(1).to_broadcast([1, NS, NE]),
                                            tile_no[0:1, :].unsqueeze(2).to_broadcast([1, NS, NE]), ALU.is_le))
            own.then_wait(vec.tensor_reduce(tile_e[:], tile_cmp[:], AX.X, ALU.add))
            vec.tensor_scalar(tile_ei[:], tile_e[:], float(NE - 1), None, ALU.min).then_inc(tile_e_done, 1)
            multiply_shared(1)
            dve.wait_ge(exp_top_done, 1)
            own.then_wait(vec.tensor_scalar(score[:], score[:], 1.0, None, ALU.add))
            own.then_wait(vec.reciprocal(score[:], score[:]))
            for t in range(NT):
                vec.tensor_scalar(scaled[:, t, :], xn[:, t, :], score[:, t:t + 1], None, ALU.mult) \
                   .then_inc(scaled_done, 1)

            for j in range(2, 4):
                multiply_shared(j)
            for j in range(4):
                dve.wait_ge(shared_down, j + 1)
                pair = x_tok[:, 2 * j:2 * j + 2, :].rearrange("p t d -> p (t d)")
                vec.tensor_tensor(pair, pair, ps[:, 4 + j % 2, :], ALU.add).then_inc(shared_added, 1)

            def copy_xgT(s, k, first):
                dve.wait_ge(xg_turned, s + 1)
                if not first:
                    dve.wait_ge(gu_done, s - 1)
                vec.tensor_copy(xgT[:, k].rearrange("p c t -> p (c t)"), ps[:, k, 0:DM]).then_inc(xgT_ready, 1)

            def multiply(s, k, first):
                dve.wait_ge(sg_done, s + 1)
                if not first:
                    dve.wait_ge(hid_turned, s - 1)
                vec.tensor_tensor(hid[:, k, :], ps[:, 2 + k, F:2 * F], sg[:, k, :], ALU.mult).then_inc(hid_done, 1)

            def copy_yo(s, k, first, pair=None):
                dve.wait_ge(down_done, s + 1)
                if not first:
                    dve.wait_ge(yo_stored[k], 16 * (s // 2 if pair is None else pair))
                vec.tensor_copy(yo[:, k, :], ps[:, 6 + k, 0:DM]).then_inc(yo_ready, 1)

            copy_xgT(0, 0, True)
            copy_xgT(1, 1, True)
            for s in range(4):
                multiply(s, s % 2, s < 2)
                if s >= 1:
                    copy_yo(s - 1, (s - 1) % 2, s < 3)
                copy_xgT(s + 2, s % 2, False)
            with nc.vector.Fori(2, NS // 2 - 1) as i:
                for k in range(2):
                    s = 2 * i + k
                    multiply(s, k, False)
                    copy_yo(s - 1, 1 - k, False, pair=i - 1 + k)
                    copy_xgT(s + 2, k, False)
            for k in range(2):
                s = NS - 2 + k
                multiply(s, k, False)
                copy_yo(s - 1, 1 - k, False)
            copy_yo(NS - 1, 1, False)

            q_ps = banks(4, 4).rearrange("p (t d) -> p t d", d=DM)

            def rotate_queries(b):
                dve.wait_ge(q_done, b + 1)
                tiles = slice(2 * b, 2 * b + 2)
                rotate(vec, q_ps[:, tiles], swapped[:, tiles], tiles)
                ins = vec.tensor_tensor(q_cos[:, tiles].rearrange("p t (h c) -> p t h c", c=HD),
                                        q_ps[:, tiles].rearrange("p t (h c) -> p t h c", c=HD),
                                        cos8[:, tiles].unsqueeze(2).to_broadcast([P, 2, NH, HD]), ALU.mult)
                own.then_wait(ins)
                add_rotated(vec, q_cos, swapped, 0, b).then_inc(q_rotated, 1)

            for b in range(NB):
                dve.wait_ge(gathered, 16 * NT)
                tiles = slice(2 * b, 2 * b + 2)
                vec.tensor_tensor(x_tok[:, tiles, :], x_tok[:, tiles, :], routed[:, tiles, :], ALU.add) \
                   .then_inc(x2_done, 1)
                dve.wait_ge(x2_done, b + 1)
                batch_stats(b)
                if b >= 1:
                    normalise(1, b - 1)
                if b == 2:
                    copy_xnT(1, 1)
            normalise(1, NB - 1)
            dve.wait_ge(k_rotated, 1)
            rotate_queries(0)
            copy_xnT(1, 3)
            for b in range(1, NB):
                rotate_queries(b)

            def spread_keys(i, k):
                dve.wait_ge(rowsT_ready, i + 1)
                wait_from_one(dve, cols_done, G * (i + 1 - SLOTS))
                for g in range(G // 2, G):
                    ins = vec.tensor_copy(keysT[k][rows_of(g, ROWS), g, :], ps[rows_of(g, ROWS), 0, L:2 * L])
                ins.then_inc(keysT_dve, 1)

            def row_maximum(i, k, n):
                dve.wait_ge(rows_done, G * i + n + 1)
                heads = slice(n // 2 * 2, n // 2 * 2 + 2)
                vec.tensor_reduce(row_max[:, k % 2, n % 2, heads], ps[:, 2 + n % 2, :].rearrange("p (g n) -> p g n", n=L),
                                  AX.X, ALU.max).then_inc(max_done, 1)

            def write_shift(i, k):
                dve.wait_ge(max_done, G * i + G)
                dve.wait_ge(stack_turned, i + 1)
                wait_from_one(dve, query_turned, i + 1 - SLOTS)
                hi, lo = stack[:, k, 0:2, :, SPLIT], stack[:, k, 0:2, :, SPLIT + 1]
                vec.tensor_scalar(hi.bitcast(F32R), row_max[:, k % 2], -1.0, None, ALU.mult).then_inc(shift_hi, 1)
                dve.wait_ge(shift_hi, i + 1)
                vec.scalar_tensor_tensor(out=lo.bitcast(F32R), in0=row_max[:, k % 2], scalar=-1.0, in1=hi,
                                         op0=ALU.mult, op1=ALU.subtract).then_inc(shift_done, 1)

            def divide(i, k):
                dve.wait_ge(o_turned, i + 1)
                heads = ps[:, 7, 0:2 * P].rearrange("p (j g r) -> p j g r", j=2, g=G)
                wait_from_one(dve, attn_done, i)
                vec.reciprocal(inv_sum[:], heads[:, :, :, HD]).then_inc(inv_done, 1)
                dve.wait_ge(inv_done, i + 1)
                vec.tensor_tensor(attn[:, :, bass.ds(i * (G * HD), G * HD)].rearrange("p j (g c) -> p j g c", g=G),
                                  heads[:, :, :, 0:HD], inv_sum[:].unsqueeze(3).to_broadcast([P, 2, G, HD]),
                                  ALU.mult).then_inc(attn_done, 1)

            def attention_turn(i, k, live):
                if live(-3):
                    divide(i - 3, (k + 1) % SLOTS)
                if live(0):
                    row_maximum(i, k, 0)
                    row_maximum(i, k, 1)
                if live(1):
                    spread_keys(i + 1, (k + 1) % SLOTS)
                if live(0):
                    row_maximum(i, k, 2)
                    row_maximum(i, k, 3)
                    write_shift(i, k)

            run_turns(nc.vector, attention_turn)

            def add_projected(b):
                dve.wait_ge(proj_done, b + 1)
                pair = x_tok[:, 2 * b:2 * b + 2, :].rearrange("p t d -> p (t d)")
                vec.tensor_tensor(pair, pair, ps[:, 4 + b, :], ALU.add).then_inc(x3_done, 1)
                dve.wait_ge(x3_done, b + 1)
                batch_stats(b)


            for b in range(NB):
                if b % 2 == 1:
                    dve.wait_ge(attn_turned, b + 1)
                    vec.tensor_copy(attnT[:, :, b * L:(b + 1) * L], ps[:, b, :].rearrange("p (k n) -> p k n", k=KT)) \
                       .then_inc(attnT_copied[1], 1)
                if b == 0:
                    dve.wait_ge(bias_added, 1)
                if b >= 1:
                    add_projected(b - 1)
                if b >= 2:
                    normalise(2, b - 2)
            add_projected(NB - 1)
            normalise(2, NB - 2)
            copy_xnT(2, 1)
            normalise(2, NB - 1)
            copy_xnT(2, 3)
            dve.wait_ge(logit_turned, 2)
            own.then_wait(vec.tensor_tensor(logit[:], logit_ps, br_row[:].unsqueeze(1).to_broadcast([P, NT, NE]), ALU.add))
            first_of_top(onehot2_done)
            vec.tensor_tensor(pick_w[:], logit[:], top[:].unsqueeze(2).to_broadcast([P, NT, NE]), ALU.subtract) \
               .then_inc(shifted_done, 1)
            dve.wait_ge(exp_logit_done, 1)
            own.then_wait(vec.tensor_reduce(weight[:], pick_w[:], AX.X, ALU.add))
            own.then_wait(vec.reciprocal(weight[:], weight[:]))
            own.then_wait(vec.tensor_scalar(weight[:], weight[:], 1.0 / RANK, None, ALU.mult))
            dve.wait_ge(onehot2_done, 1)
            own.then_wait(vec.tensor_tensor(pick_w[:], onehot[:], weight[:].unsqueeze(2).to_broadcast([P, NT, NE]),
                                            ALU.mult))
            for t in range(NT + 2):
                if t < NT:
                    dve.wait_ge(low_done, t + 1)
                    if t >= 2:
                        dve.wait_ge(low_turned, t - 1)
                    vec.tensor_tensor(low[:, t % 2, :].rearrange("p (e r) -> p e r", r=RANK),
                                      ps[:, LOW_BANKS[t % 3], :].rearrange("p (e r) -> p e r", r=RANK),
                                      pick_w[:, t, :].unsqueeze(2).to_broadcast([P, NE, RANK]), ALU.mult) \
                       .then_inc(low_masked, 1)
                if t >= 2:
                    dve.wait_ge(last_done, t - 1)
                    vec.tensor_tensor(x_tok[:, t - 2, :], x_tok[:, t - 2, :], ps[:, 4 + t % 2, 0:DM], ALU.add) \
                       .then_inc(tile_done, 1)

        @block.gpsimd
        def _(pool):
            own = Chain(pool, pool_own)
            pl = nc.gpsimd
            pl.memset(eps_col[:], LN_EPS)
            pl.memset(one_col[:], 1.0)
            pl.memset(zero_rows, 0.0).then_inc(zeros_set, 1)
            pl.memset(decay[:].rearrange("p e (b l) -> p e b l", b=NB)[:, :, :, 0:1], 0.0).then_inc(cols_set, 1)
            pool.wait_ge(zeros_set, 1)
            for k in range(SLOTS):
                pl.tensor_scalar(keysT[k][:].rearrange("p g n -> p (g n)"), zero_rows[:, 0:G * L], 1.0, 1.0, ALU.mult, ALU.mult)
            pool.wait_ge(consts_loaded, 16)
            pool.wait_ge(ssm_w_loaded, 48)
            pl.tensor_copy(ident3[:], ident3f[0:96, :])
            for et in range(KT):
                pl.tensor_scalar(diag_d[:, et, :], ident, d_skip[:, et, :], 1.0, ALU.mult, ALU.mult)
            pool.wait_ge(expa_done, 1)
            pl.tensor_scalar(neg_a[:], neg_a[:], -1.0, 1.0, ALU.mult, ALU.mult).then_inc(setup_done, 1)

            def read_state(n, k, first):
                for et in range(KT):
                    pool.wait_ge(scan_done[et], n + 1)
                    pool.wait_ge(c_copied, n + 1)
                    if not first:
                        pool.wait_ge(y_added[et], n)
                    pl.tensor_tensor(read[:, et, :], state[:, et, :], c_rows[:, k, :], ALU.mult) \
                      .then_inc(read_done[et], 1)

            for k in range(2):
                read_state(k, k, first=(k == 0))
            with nc.gpsimd.Fori(1, DS // 2) as i:
                for k in range(2):
                    read_state(2 * i + k, k, first=False)

            for t in range(NT):
                pool.wait_ge(scaled_done, t + 1)
                if t == 0:
                    pool.wait_ge(slot_done, 1)
                    pool.wait_ge(sorted_cleared, 32)
                pl.indirect_dma_start(sorted_x, bass.IndirectOffsetOnAxis(ap=slot[:, t:t + 1], axis=0),
                                      scaled[:, t, :], None).then_inc(scattered, 16)
            pool.wait_ge(trig_ready, 1)
            pool.wait_ge(kv_copied, NT)
            pool.wait_ge(y_turned, 2)
            own.then_wait(rotate(pl, k_tok, swapped, slice(0, NT)))
            own.then_wait(pl.tensor_tensor(k_tok.rearrange("p t (h c) -> p t h c", c=HD),
                                           k_tok.rearrange("p t (h c) -> p t h c", c=HD),
                                           cos8[:].unsqueeze(2).to_broadcast([P, NT, NH, HD]), ALU.mult))
            for b in range(NB):
                ins = add_rotated(pl, k_tok, swapped, 1, b)
            ins.then_inc(k_rotated, 1)

            with nc.gpsimd.Fori(0, NS // 2) as i:
                for k in range(2):
                    pool.wait_ge(yo_ready, 2 * i + k + 1)
                    pl.dma_start(sorted_y[bass.ds((2 * i + k) * P, P), :], yo[:, k, :]).then_inc(yo_stored[k], 16)
            pool.wait_ge(yo_stored[0], 8 * NS)
            pool.wait_ge(yo_stored[1], 8 * NS)
            for t in range(NT):
                pl.indirect_dma_start(routed[:, t, :], None, sorted_y,
                                      bass.IndirectOffsetOnAxis(ap=slot[:, t:t + 1], axis=0)) \
                  .then_inc(gathered, 16)

            pl.memset(stack[:], 0.0)
            pl.memset(v_ones[:], 0.0).then_inc(pads_set, 1)
            pool.wait_ge(pads_set, 1)
            pl.memset(stack[:, :, 2:4, :, SPLIT:SPLIT + 2], 1.0)
            pl.memset(v_ones[:, :, :, :, HD:HD + 1], 1.0)

            def build_group(i, k):
                wait_from_one(pool, query_turned, i + 1 - SLOTS)
                wait_from_one(pool, built, i - 1)
                pl.tensor_copy(current[:, k % 2:k % 2 + 1], rot[:, bass.ds(i, 1)].rearrange("p i w c -> p i (w c)")) \
                  .then_inc(current_ready, 1)
                pool.wait_ge(current_ready, i + 1)
                both = current[:, k % 2].rearrange("p (n g c) -> p n g c", n=4, g=G)
                q, key = both[:, 0:2], both[:, 2:4]
                part = [stack[:, k, :, :, n * HD:(n + 1) * HD] for n in range(3)]
                pl.tensor_tensor(part[0].bitcast(F32R), both, one_col[:].unsqueeze(1).unsqueeze(2).to_broadcast([P, 4, G, HD]),
                                 ALU.mult)
                pl.tensor_scalar(part[1][:, 0:2].bitcast(F32R), q, 1.0, 1.0, ALU.mult, ALU.mult)
                pl.tensor_scalar(part[2][:, 2:4].bitcast(F32R), key, 1.0, 1.0, ALU.mult, ALU.mult).then_inc(hi_built, 1)
                pool.wait_ge(hi_built, i + 1)
                pl.tensor_tensor(part[2][:, 0:2].bitcast(F32R), q, part[0][:, 0:2], ALU.subtract)
                pl.tensor_tensor(part[1][:, 2:4].bitcast(F32R), key, part[0][:, 2:4], ALU.subtract).then_inc(built, 1)

            def copy_values(i, k):
                wait_from_one(pool, pv_done, G * (i - 1))
                pl.tensor_copy(v_ones[:, k % 2, :, :, 0:HD],
                               v_tok[:, bass.ds(i, 1)].rearrange("p i (n g c) -> p (i n) g c", n=2, g=G)) \
                  .then_inc(v_copied, 1)

            pool.wait_ge(q_rotated, 1)
            for i in range(SLOTS):
                build_group(i, i % SLOTS)
                if i >= 1:
                    copy_values(i - 1, (i - 1) % 2)
            pool.wait_ge(q_rotated, NB)
            with nc.gpsimd.Fori(1, NG // SLOTS) as m:
                for k in range(SLOTS):
                    build_group(SLOTS * m + k, k)
                    copy_values(SLOTS * m + k - 1, (k - 1) % 2)
            copy_values(NG - 1, 1)
            pl.tensor_tensor(x_tok[:], x_tok[:], out_b[:].unsqueeze(1).to_broadcast([P, NT, DM]), ALU.add) \
              .then_inc(bias_added, 1)
    return nc


def kernel(x, ctx_1024, fside_BxSx2_0, L0_xattn_in_proj_w, L0_xattn_conv_w, L0_xattn_conv_b, L0_xattn_x_proj_w,
           L0_xattn_dt_proj_w, L0_xattn_dt_proj_b, L0_xattn_A_log, L0_xattn_D, L0_ffn_router_w, L0_ffn_gate_w,
           L0_ffn_up_w, L0_ffn_down_w, L0_ffn_shared_gate_w, L0_ffn_shared_up_w, L0_ffn_shared_down_w,
           L1_xattn_Wq, L1_xattn_Wkv, L1_xattn_Wout, L1_xattn_bout, L1_ffn_A, L1_ffn_B, L1_ffn_Wr, L1_ffn_br):
    import numpy as np
    import concourse.bacc as bacc
    from concourse.bass_utils import run_bass_kernel_spmd

    cat = np.concatenate
    xp = np.asarray(L0_xattn_x_proj_w)
    bc = xp[DR:]
    small = np.zeros((P, 64 + G), np.float32)
    small[:, 64:] = np.arange(P)[:, None] // ROWS == np.arange(G)[None, :]
    small[:, 32:40] = np.arange(NE) - NE
    small[:, 40:48] = np.arange(NE) * P
    small[:, 48:48 + NS] = np.arange(NS)
    small[:, 0:32] = np.arange(32)[None, :] == (np.arange(P) % 32)[:, None]
    arrays = {
        "x": np.asarray(x),
        "ctxT": np.asarray(ctx_1024).reshape(TOK, DC).T,
        "in_w": np.asarray(L0_xattn_in_proj_w).T,
        "xp_w": cat([bc, bc, bc, xp[:DR]]).T,
        "dt_w": cat([np.zeros((96, DM), np.float32), np.asarray(L0_xattn_dt_proj_w).T]),
        "chan": cat([np.asarray(L0_xattn_conv_w)] + [np.asarray(a)[:, None] for a in
                    (L0_xattn_conv_b, L0_xattn_dt_proj_b, L0_xattn_D)] + [np.asarray(L0_xattn_A_log)], axis=1),
        "pos": np.asarray(fside_BxSx2_0),
        "q_w": np.asarray(L1_xattn_Wq), "kv_w": np.asarray(L1_xattn_Wkv), "out_w": np.asarray(L1_xattn_Wout),
        "out_b": np.asarray(L1_xattn_bout)[None],
        "wr_w": np.asarray(L1_ffn_Wr).T, "br": np.asarray(L1_ffn_br)[None],
        "a_w": np.asarray(L1_ffn_A).reshape(NE * RANK, DM).T,
        "b_w": np.asarray(L1_ffn_B).transpose(0, 2, 1).reshape(NE * RANK, DM),
        "router_w": np.asarray(L0_ffn_router_w),
        "gu_w": cat([cat([np.asarray(L0_ffn_gate_w), np.asarray(L0_ffn_shared_gate_w)[None]]),
                     cat([np.asarray(L0_ffn_up_w), np.asarray(L0_ffn_shared_up_w)[None]])], axis=2),
        "down_w": cat([np.asarray(L0_ffn_down_w), np.asarray(L0_ffn_shared_down_w)[None]]),
        "consts": cat([np.eye(P, dtype=np.float32), np.triu(np.ones((P, P), np.float32), 1), small], axis=1),
    }
    nc = bacc.Bacc("TRN2", target_bir_lowering=False, num_devices=1)
    arrays = {f"in_{k}": np.ascontiguousarray(a) for k, a in arrays.items()}
    handles = {k[3:]: nc.dram_tensor(k, a.shape, mybir.dt.from_np(a.dtype), kind="ExternalInput").ap()
               for k, a in arrays.items()}
    out = nc.dram_tensor("out", (NB, L, DM), F32, kind="ExternalOutput").ap()
    build(nc, handles, out)
    return run_bass_kernel_spmd(nc, [arrays], core_ids=[0]).results[0]["out"]
```

```python
import math
from contextlib import ExitStack

import concourse.bass as bass
from concourse import mybir

F32 = mybir.dt.float32
F32R = mybir.dt.float32r
BF16 = mybir.dt.bfloat16
I32 = mybir.dt.int32
ALU = mybir.AluOpType
ACT = mybir.ActivationFunctionType
AX = mybir.AxisListType

P = 128
NB, L, DM = 4, 256, 256
DC = 128
TOK = NB * L
NT = TOK // P
KT = DM // P
DS, TAPS, DR = 16, 4, 8
LN_EPS = 1e-5
HALF = 512
NE, F = 8, 256
NS = TOK // P + NE
LAG = 6

NH, HD = 32, 8
G = 4
NG = NB * NH // G
ROWS = 32
SLOTS = 4
SPLIT = 3 * HD
RANK = 64
OUT_BANKS = (0, 2, 3, 1)
LOW_BANKS, TURN_BANKS = (7, 0, 2, 1), (3, 6)
TWO_PI_HI = 6.28125
TWO_PI_LO = 2 * math.pi - TWO_PI_HI
PI_BELOW = 3.1415925
ROUND = 1.5 * 2.0 ** 23


def wait_from_one(eng, sem, value):
    if not isinstance(value, int) or value > 0:
        eng.wait_ge(sem, value)


class Chain:

    def __init__(self, eng, sem):
        self.eng, self.sem, self.n = eng, sem, 0

    def then_wait(self, ins):
        self.n += 1
        ins.then_inc(self.sem, 1)
        self.eng.wait_ge(self.sem, self.n)


def build(nc, h, out):
    ctx = ExitStack()
    with ctx:
        def sb(name, shape, dt=F32):
            return ctx.enter_context(nc.sbuf_tensor(name, shape, dt))

        def sem(name):
            return ctx.enter_context(nc.semaphore(name))

        ps = ctx.enter_context(nc.psum_tensor("ps", [P, 8, HALF], F32))

        def banks(a, n):
            return ps[:, a:a + n, :].rearrange("p b c -> p (b c)")

        x_tok = sb("x_tok", [P, NT, DM])
        ctxT = sb("ctxT", [P, TOK])
        consts = sb("consts", [P, 2 * P + 64])
        ident, upper = consts[:, 0:P], consts[:, P:2 * P]
        ident3f = consts[:, 2 * P:2 * P + 32]
        in_w = sb("in_w", [P, DM])
        xp_w = sb("xp_w", [P, KT, 104])
        dt_w = sb("dt_w", [104, DM])
        chan = sb("chan", [P, KT, TAPS + 3 + DS])
        tap_w, conv_b = chan[:, :, 0:TAPS], chan[:, :, TAPS:TAPS + 1]
        dt_b, d_skip = chan[:, :, TAPS + 1:TAPS + 2], chan[:, :, TAPS + 2:TAPS + 3]
        a_log = chan[:, :, TAPS + 3:]
        neg_a = sb("neg_a", [P, KT, DS])
        ident3 = sb("ident3", [96, 32], BF16)
        diag_d = sb("diag_d", [P, KT, P])
        u = sb("u", [P, KT, TOK])
        delta = sb("delta", [P, KT, TOK])
        du = sb("du", [P, KT, TOK])
        gate_z = sb("gate_z", [P, KT, TOK])
        xdbl_all = sb("xdbl", [P, TOK])
        xdbl = xdbl_all[0:104, :]
        bc3 = sb("bc3", [96, TOK], BF16)
        decay = sb("decay", [P, 2, TOK])
        drive = sb("drive", [P, 2, TOK])
        state = sb("state", [P, 2, TOK])
        rot = sb("rot", [P, NG, 2, 2 * G * HD])
        read = sb("read", [P, 2, TOK])
        products = [read, rot[:, 0:NG // 2].rearrange("p (e g) w c -> p e (g w c)", e=KT)]
        c_rows = sb("c_rows", [P, 2, TOK])
        stats = sb("stats", [P, NT, 6])
        mean_var = sb("mean_var", [P, NT, 2])
        ln_var = sb("ln_var", [P, NT])
        rstd = sb("rstd", [P, NT])
        shift = sb("shift", [P, NT])
        eps_col, one_col = sb("eps_col", [P, 1]), sb("one_col", [P, 1])

        col = consts[:, 2 * P + 32:]
        e_minus_8, j_times_128, tile_no = col[:, 0:NE], col[:, NE:2 * NE], col[:, 2 * NE:2 * NE + NS]
        router_w = sb("router_w", [P, KT, NE])
        gu_w = sb("gu_w", [P, NE + 1, KT, 2 * F])
        down_w = sb("down_w", [P, NE + 1, KT, DM])
        upper_bf, ones_bf = sb("upper_bf", [P, P], BF16), sb("ones_bf", [P, P], BF16)
        xn = delta[:].rearrange("p k (t d) -> p (k t) d", d=DM)
        xnT = du
        hidT = drive
        scaled = decay[:].rearrange("p k (t d) -> p (k t) d", d=DM)
        routed = read[:].rearrange("p k (t d) -> p (k t) d", d=DM)
        silu_g = state[:].rearrange("p k (b c) -> p (k b) c", c=HALF)
        zero_rows = c_rows[:].rearrange("p k c -> p (k c)")
        logitT = sb("logitT", [NE, TOK])
        logit = sb("logit", [P, NT, NE])
        top = sb("top", [P, NT])
        pick = sb("pick", [P, NT, NE])
        first_e = sb("first_e", [P, NT])
        onehot = sb("onehot", [P, NT, NE], BF16)
        score = sb("score", [P, NT])
        full_tile = sb("full_tile", [P, NE, NE])
        tiles_e, tiles_upto, zeros8 = sb("tiles_e", [P, NE]), sb("tiles_upto", [P, NE]), sb("zeros8", [P, NE])
        slot_f, slot = sb("slot_f", [P, NT]), sb("slot", [P, NT], I32)
        tile_e, tile_ei = sb("tile_e", [1, NS]), sb("tile_ei", [1, NS], I32)
        tile_cmp = sb("tile_cmp", [1, NS, NE])
        xg = xdbl_all[:, 0:2 * DM].rearrange("p (k d) -> p k d", k=2)
        xgT = xdbl_all[:, 2 * DM:].rearrange("p (k c t) -> p k c t", k=2, c=KT)
        sg = ctxT[:, 0:2 * F].rearrange("p (k f) -> p k f", k=2)
        hid = ctxT[:, 2 * F:].rearrange("p (k f) -> p k f", k=2)
        hT = sb("hT", [P, 2, KT, P])
        yo = sb("yo", [P, 2, DM])
        pos = sb("pos", [P, NT, 2])
        angle, turns = sb("angle", [P, 2, NT, 4]), sb("turns", [P, 2, NT, 4])
        cos8 = sb("cos8", [P, NT, HD])
        sin_pos, sin_neg = sb("sin_pos", [P, NT, 4]), sb("sin_neg", [P, NT, 4])
        q_w, kv_w, out_w = sb("q_w", [P, KT, DM]), sb("kv_w", [P, 2 * DM]), sb("out_w", [P, KT, DM])
        out_b = sb("out_b", [P, DM])
        k_tok = gate_z[:].rearrange("p k (t d) -> p (k t) d", d=DM)
        v_tok = c_rows[:].rearrange("p k (g c) -> p (k g) c", c=2 * G * HD)
        swapped = u[:].rearrange("p k (t d) -> p (k t) d", d=DM)
        q_cos = drive[:].rearrange("p k (t d) -> p (k t) d", d=DM)
        stack = gu_w[:, 2:4].rearrange("p e c (m g r) -> p (e c) m g r", g=G, r=ROWS)
        rowsT = [sb(f"rowsT{k}", [P, L], F32R) for k in range(2)]
        keysT = [sb(f"keysT{k}", [P, G, L], F32R) for k in range(SLOTS)]
        queryT = [sb(f"queryT{k}", [P, L], F32R) for k in range(2)]
        current = gu_w[:, 0].rearrange("p c (k n) -> p (c k) n", n=4 * G * HD)
        row_max = sb("row_max", [P, 2, 2, G])
        v_ones = gu_w[:, 4, 0].rearrange("p (k j g r) -> p k j g r", k=2, j=2, g=G)
        prob = [b[:].rearrange("p k (c n) -> p (k c) n", n=HALF) for b in (drive, state)]
        o_sb = gu_w[:, 1].rearrange("p c (k n) -> p (c k) n", n=L)
        inv_sum = sb("inv_sum", [P, 2, G])
        attn = delta
        attnT = decay
        wr_w, br_row = sb("wr_w", [P, KT, NE]), sb("br_row", [P, NE])
        a_w = gate_z[:, 0, :].rearrange("p (k c) -> p k c", k=KT)
        b_w = gate_z[:, 1, :].rearrange("p (k c) -> p k c", k=4)
        weight, pick_w = sb("weight", [P, NT]), sb("pick_w", [P, NT, NE])
        low = drive[:].rearrange("p k (c n) -> p (k c) n", n=HALF)
        b_hi, b_lo = keysT[0], keysT[1]
        low_hiT, low_loT = [k[:].rearrange("p (s g) n -> p s (g n)", s=2) for k in keysT[2:4]]
        sorted_x = nc.dram_tensor("sorted_x", (NS * P, DM), F32, kind="Internal").ap()
        sorted_y = nc.dram_tensor("sorted_y", (NS * P, DM), F32, kind="Internal").ap()

        x_loaded = sem("x_loaded")
        ctx_loaded = sem("ctx_loaded")
        ssm_w_loaded = sem("ssm_w_loaded")
        consts_loaded = sem("consts_loaded")
        out_stored = sem("out_stored")
        dve_own, act_own, pool_own = sem("dve_own"), sem("act_own"), sem("pool_own")
        xin_done = sem("xin_done")
        tap0_done = sem("tap0_done")
        conv_done = sem("conv_done")
        cols_set = sem("cols_set")
        ln0_stats = sem("ln0_stats")
        ln0_rstd = sem("ln0_rstd")
        ln0_shift = sem("ln0_shift")
        u_done = sem("u_done")
        xdbl_done = sem("xdbl_done")
        xdbl_copied = sem("xdbl_copied")
        dt_done = sem("dt_done")
        expa_done = sem("expa_done")
        setup_done = sem("setup_done")
        abs_done, relu_done, log_done = sem("abs_done"), sem("relu_done"), sem("log_done")
        delta_done = sem("delta_done")
        bc3_done = sem("bc3_done")
        b_ready, c_ready = sem("b_ready"), sem("c_ready")
        decay_ready = [sem(f"decay_ready{e}") for e in range(KT)]
        drive_done = sem("drive_done")
        scan_done = [sem(f"scan_done{e}") for e in range(KT)]
        c_copied = sem("c_copied")
        read_done = [sem(f"read_done{e}") for e in range(KT)]
        y_added = [sem(f"y_added{e}") for e in range(KT)]
        last_read_done = sem("last_read_done")
        y_gated = sem("y_gated")
        y_turned = sem("y_turned")
        x1_done = sem("x1_done")
        ffn_w_loaded = sem("ffn_w_loaded")
        zeros_set, sorted_cleared = sem("zeros_set"), sem("sorted_cleared")
        ln_stats, ln_rstd, xn_done = sem("ln_stats"), sem("ln_rstd"), sem("xn_done")
        xn_turned = sem("xn_turned")
        xnT_copied = [sem(f"xnT_copied{k}") for k in range(2)]
        bf_consts = sem("bf_consts")
        logitT_done, logitT_copied = sem("logitT_done"), sem("logitT_copied")
        logit_turned = sem("logit_turned")
        onehot_done, top_done, exp_top_done = sem("onehot_done"), sem("top_done"), sem("exp_top_done")
        rank_done = sem("rank_done")
        tile_e_done, halfdone, scaled_done = sem("tile_e_done"), sem("halfdone"), sem("scaled_done")
        scattered = sem("scattered")
        shared_gu, shared_silu, shared_hid = sem("shared_gu"), sem("shared_silu"), sem("shared_hid")
        shared_down, shared_added = sem("shared_down"), sem("shared_added")
        xg_loaded = [sem(f"xg_loaded{k}") for k in range(2)]
        xg_turned, xgT_ready = sem("xg_turned"), sem("xgT_ready")
        gu_done, sg_done, hid_done = sem("gu_done"), sem("sg_done"), sem("hid_done")
        hid_turned, hT_ready, down_done = sem("hid_turned"), sem("hT_ready"), sem("down_done")
        yo_ready = sem("yo_ready")
        yo_stored = [sem(f"yo_stored{k}") for k in range(2)]
        gathered = [sem(f"gathered{b}") for b in range(NB)]
        x2_done = sem("x2_done")
        pos_loaded, att_w_loaded, last_w_loaded = sem("pos_loaded"), sem("att_w_loaded"), sem("last_w_loaded")
        angle_done, trig_done, trig_ready = sem("angle_done"), sem("trig_done"), sem("trig_ready")
        kv_done, kv_copied = sem("kv_done"), sem("kv_copied")
        k_rotated, q_done, q_rotated = sem("k_rotated"), sem("q_done"), sem("q_rotated")
        pads_set, built = sem("pads_set"), sem("built")
        stack_turned, rowsT_ready = sem("stack_turned"), sem("rowsT_ready")
        keysT_act, keysT_dve = sem("keysT_act"), sem("keysT_dve")
        rows_done, max_done, shift_done = sem("rows_done"), sem("max_done"), sem("shift_done")
        query_turned, queryT_ready = sem("query_turned"), sem("queryT_ready")
        cols_done, exp_done, pv_done = sem("cols_done"), sem("exp_done"), sem("pv_done")
        o_copied, o_turned, attn_done = sem("o_copied"), sem("o_turned"), sem("attn_done")
        v_copied = sem("v_copied")
        current_ready = sem("current_ready")
        hi_built = sem("hi_built")
        shift_hi, inv_done = sem("shift_hi"), sem("inv_done")
        bias_added = sem("bias_added")
        attn_turned, proj_done, x3_done = sem("attn_turned"), sem("proj_done"), sem("x3_done")
        attnT_copied = sem("attnT_copied")
        shifted_done, exp_logit_done = sem("shifted_done"), sem("exp_logit_done")
        onehot2_done = sem("onehot2_done")
        low_done, low_masked, low_turned = sem("low_done"), sem("low_masked"), sem("low_turned")
        low_hi_ready, low_lo_ready, b_split = sem("low_hi_ready"), sem("low_lo_ready"), sem("b_split")
        last_done, tile_done = sem("last_done"), sem("tile_done")

        xin_ps = [banks(0, 2), banks(2, 2)]
        xdbl_ps = banks(4, 2)[0:104, :]
        dt_ps = xin_ps
        b_ps, c_ps = banks(0, 2), banks(2, 2)
        y_ps = [banks(4, 2), banks(6, 2)]
        turned = banks(0, 4).rearrange("p (t d) -> p t d", t=NT)

        logitT_ps = banks(4, 2)[0:NE, :]
        logit_ps = banks(6, 1)[:, 0:NT * NE].rearrange("p (t e) -> p t e", e=NE)
        rank_ps = banks(7, 1)[:, 0:NT * NE].rearrange("p (t e) -> p t e", e=NE)
        count_ps = banks(7, 1)[:, NT * NE:NT * NE + NE]

        def rotate(eng, x, swap, tiles):
            n = tiles.stop - tiles.start
            pairs = x.rearrange("p t (h c two) -> p t h c two", two=2, c=4)
            outs = swap.rearrange("p t (h c two) -> p t h c two", two=2, c=4)
            for m, sine in ((0, sin_neg), (1, sin_pos)):
                ins = eng.tensor_tensor(outs[:, :, :, :, m], pairs[:, :, :, :, 1 - m],
                                  sine[:, tiles].unsqueeze(2).to_broadcast([P, n, NH, 4]), ALU.mult)
            return ins

        def add_rotated(eng, x_cos, swap, which, b):
            def view(x):
                return x[:, 2 * b:2 * b + 2].rearrange("p j (g c) -> p g j c", c=G * HD)
            groups = rot[:].rearrange("p (b g) w (j c) -> p b g w j c", b=NB, j=2)
            return eng.tensor_tensor(groups[:, b, :, which], view(x_cos), view(swap), ALU.add)

        def rows_of(g, n):
            return slice(g * ROWS, g * ROWS + n)

        def run_turns(eng, turn, after):
            lead, tail = 8, NG - SLOTS
            for i in range(-1, lead):
                turn(i, i % SLOTS, lambda n, i=i: 0 <= i + n < NG)
            with eng.Fori(lead // SLOTS, tail // SLOTS) as m:
                for k in range(SLOTS):
                    turn(SLOTS * m + k, k, lambda n: True)
            for i in range(tail, NG + 4):
                turn(i, i % SLOTS, lambda n, i=i: 0 <= i + n < NG)
                after(i)

        block = ctx.enter_context(nc.Block())

        @block.sync
        def _(sp):
            sp.dma_start(pos[:], h["pos"].rearrange("b (l p) c -> p (b l) c", p=P)).then_inc(pos_loaded, 16)
            sp.dma_start(ctxT[:], h["ctxT"]).then_inc(ctx_loaded, 16)
            sp.dma_start(in_w[:], h["in_w"]).then_inc(ctx_loaded, 16)
            sp.dma_start(chan[:], h["chan"].rearrange("(k p) c -> p k c", p=P)).then_inc(ssm_w_loaded, 16)
            sp.dma_start(x_tok[:], h["x"].rearrange("b (l p) d -> p (b l) d", p=P)).then_inc(x_loaded, 16)
            sp.dma_start(consts[:], h["consts"]).then_inc(consts_loaded, 16)
            sp.dma_start(xp_w[:], h["xp_w"].rearrange("(k p) c -> p k c", p=P)).then_inc(ssm_w_loaded, 16)
            sp.dma_start(dt_w[:], h["dt_w"]).then_inc(ssm_w_loaded, 16)
            sp.wait_ge(zeros_set, 1)
            for half in range(2):
                sp.dma_start(sorted_x.rearrange("(p r) d -> p (r d)", p=P)[:, half * (NS // 2) * DM:(half + 1) * (NS // 2) * DM],
                             zero_rows).then_inc(sorted_cleared, 16)
            sp.dma_start(router_w[:], h["router_w"].rearrange("(k p) e -> p k e", p=P)).then_inc(ffn_w_loaded, 16)
            sp.dma_start(gu_w[:, NE], h["gu_w"][NE].rearrange("(k p) f -> p k f", p=P)).then_inc(ffn_w_loaded, 16)
            sp.dma_start(down_w[:, NE], h["down_w"][NE].rearrange("(k p) f -> p k f", p=P)).then_inc(ffn_w_loaded, 16)
            for e in range(NE):
                sp.dma_start(gu_w[:, e], h["gu_w"][e].rearrange("(k p) f -> p k f", p=P)).then_inc(ffn_w_loaded, 16)
                sp.dma_start(down_w[:, e], h["down_w"][e].rearrange("(k p) f -> p k f", p=P)).then_inc(ffn_w_loaded, 16)

            sp.dma_start(q_w[:], h["q_w"].rearrange("(k p) c -> p k c", p=P)).then_inc(att_w_loaded, 16)
            sp.dma_start(kv_w[:], h["kv_w"]).then_inc(att_w_loaded, 16)
            sp.dma_start(out_w[:], h["out_w"].rearrange("(k p) c -> p k c", p=P)).then_inc(att_w_loaded, 16)
            sp.dma_start(out_b[:], h["out_b"].to_broadcast([P, DM])).then_inc(att_w_loaded, 16)
            sp.dma_start(wr_w[:], h["wr_w"].rearrange("(k p) c -> p k c", p=P)).then_inc(last_w_loaded, 16)
            sp.dma_start(br_row[:], h["br"].to_broadcast([P, NE])).then_inc(last_w_loaded, 16)

            def load_tile(s, k, first):
                if not first:
                    sp.wait_ge(xg_turned, s - 1)
                sp.dma_start(xg[:, k, :], sorted_x[bass.ds(s * P, P), :]).then_inc(xg_loaded[k], 16)

            def store_tile(s, k):
                sp.wait_ge(yo_ready, s + 1)
                sp.dma_start(sorted_y[bass.ds(s * P, P), :], yo[:, k, :]).then_inc(yo_stored[k], 16)

            sp.wait_ge(scattered, 16 * NT)
            for s in range(2):
                load_tile(s, s, first=True)
            for s in range(2, LAG):
                load_tile(s, s % 2, first=False)
            with nc.sync.Fori(LAG // 2, NS // 2) as i:
                for k in range(2):
                    load_tile(2 * i + k, k, first=False)
                    store_tile(2 * i + k - LAG, k)
            for s in range(NS - LAG, NS):
                store_tile(s, s % 2)

            sp.wait_ge(k_rotated, 1)
            sp.dma_start(a_w, h["a_w"].rearrange("(k p) c -> p k c", p=P)).then_inc(last_w_loaded, 16)
            sp.dma_start(b_w, h["b_w"].rearrange("(k p) c -> p k c", p=P)).then_inc(last_w_loaded, 16)
            for t in range(NT):
                sp.wait_ge(tile_done, t + 1)
                sp.dma_start(out.rearrange("b (l p) d -> p (b l) d", p=P)[:, t, :], x_tok[:, t, :]) \
                  .then_inc(out_stored, 16)
            sp.wait_ge(out_stored, 16 * NT)

        @block.tensor
        def _(pe):
            mm = nc.tensor.matmul

            pe.wait_ge(ctx_loaded, 32)
            for et in range(KT):
                for c in range(2):
                    ins = mm(xin_ps[et][:, c * HALF:(c + 1) * HALF], in_w[:, et * P:(et + 1) * P],
                             ctxT[:, c * HALF:(c + 1) * HALF], start=True, stop=True)
                ins.then_inc(xin_done, 1)
            pe.wait_ge(ssm_w_loaded, 48)
            for et in range(KT):
                pe.wait_ge(u_done, et + 1)
                for c in range(2):
                    ins = mm(xdbl_ps[:, c * HALF:(c + 1) * HALF], xp_w[:, et, :],
                             u[:, et, c * HALF:(c + 1) * HALF], start=(et == 0), stop=(et == 1))
                    if et == 1:
                        ins.then_inc(xdbl_done, 1)
            pe.wait_ge(conv_done, 2)
            for et in range(KT):
                for c in range(2):
                    pe.wait_ge(xdbl_copied, c + 1)
                    ins = mm(dt_ps[et][:, c * HALF:(c + 1) * HALF], dt_w[:, et * P:(et + 1) * P],
                             xdbl[:, c * HALF:(c + 1) * HALF], start=True, stop=True)
                ins.then_inc(dt_done, 1)
            pe.wait_ge(setup_done, 1)
            pe.wait_ge(bc3_done, 1)
            for et in range(KT):
                for c in range(2):
                    mm(y_ps[et][:, c * HALF:(c + 1) * HALF], diag_d[:, et, :],
                       u[:, et, c * HALF:(c + 1) * HALF], start=True, stop=False, skip_group_check=True)

            def spread_b(n):
                for c in range(2):
                    ins = mm(b_ps[:, c * HALF:(c + 1) * HALF], ident3[:, bass.ds(n, 1)].to_broadcast([96, P]),
                             bc3[:, c * HALF:(c + 1) * HALF], start=True, stop=True)
                ins.then_inc(b_ready, 1)

            def spread_c(n):
                for c in range(2):
                    ins = mm(c_ps[:, c * HALF:(c + 1) * HALF],
                             ident3[:, bass.ds(n + DS, 1)].to_broadcast([96, P]),
                             bc3[:, c * HALF:(c + 1) * HALF], start=True, stop=True)
                ins.then_inc(c_ready, 1)

            def add_y(n, k, last=False):
                for et in range(KT):
                    if last and et == 1:
                        pe.wait_ge(last_read_done, 1)
                    else:
                        pe.wait_ge(read_done[et], n + 1)
                    for c in range(2):
                        ins = mm(y_ps[et][:, c * HALF:(c + 1) * HALF], ident,
                                 products[k][:, et, c * HALF:(c + 1) * HALF], start=False, stop=last,
                                 skip_group_check=True)
                    ins.then_inc(y_added[et], 1)

            def spread(n):
                pe.wait_ge(drive_done, 2 * n)
                spread_b(n)
                pe.wait_ge(c_copied, n)
                spread_c(n)

            pe.wait_ge(relu_done, 2)
            spread_b(0)
            spread_c(0)
            spread(1)
            with nc.tensor.Fori(0, DS // 2 - 1) as i:
                for k in range(2):
                    spread(2 * i + k + 2)
                    add_y(2 * i + k, k)
            add_y(DS - 2, 0)
            add_y(DS - 1, 1, last=True)

            for b in range(NB):
                for et in range(KT):
                    pe.wait_ge(y_gated, et + 1)
                    for lt in range(2):
                        ins = nc.tensor.transpose(turned[:, 2 * b + lt, et * P:(et + 1) * P],
                                                  u[:, et, b * L + lt * P:b * L + (lt + 1) * P], ident)
                if b % 2 == 1:
                    ins.then_inc(y_turned, 1)

            def turn_xn(r, b):
                bank = OUT_BANKS[b] if r == 2 else b
                pe.wait_ge(xn_done, NB * r + b + 1)
                for k in range(KT):
                    for t in (2 * b, 2 * b + 1):
                        ins = nc.tensor.transpose(ps[:, bank, k * L + (t % 2) * P:k * L + (t % 2 + 1) * P],
                                                  xn[:, t, k * P:(k + 1) * P], ident)
                ins.then_inc(xn_turned, 1)

            def wait_xnT(r, b):
                if r == 0:
                    pe.wait_ge(xnT_copied[b % 2], b // 2 + 1)
                else:
                    pe.wait_ge(xnT_copied[0], 2 + NB * (r - 1) + b + 1)

            def router(r, weights, c):
                wait_xnT(r, 2 * c)
                wait_xnT(r, 2 * c + 1)
                for k in range(KT):
                    ins = mm(logitT_ps[:, c * HALF:(c + 1) * HALF], weights[:, k, :],
                             xnT[:, k, c * HALF:(c + 1) * HALF], start=(k == 0), stop=(k == 1))
                ins.then_inc(logitT_done, 1)

            def turn_logits(n):
                for t in range(NT):
                    if t % 4 == 0:
                        pe.wait_ge(logitT_copied, 2 * n - 1 + t // 4)
                    ins = nc.tensor.transpose(logit_ps[:, t, :], logitT[:, t * P:(t + 1) * P], ident[0:NE, 0:NE])
                ins.then_inc(logit_turned, 1)

            pe.wait_ge(att_w_loaded, 64)
            for t in range(NT):
                if t == 6:
                    pe.wait_ge(x1_done, 2)
                    turn_xn(0, 0)
                if t >= 4:
                    pe.wait_ge(kv_copied, t - 3)
                mm(ps[:, 4 + t % 4, :], ctxT[:, t * P:(t + 1) * P], kv_w[:], start=True, stop=True) \
                    .then_inc(kv_done, 1)

            for b in range(1, NB):
                turn_xn(0, b)
            pe.wait_ge(ffn_w_loaded, 16 * (3 + 2 * NE))
            pe.wait_ge(kv_copied, NT)
            for c in range(2):
                router(0, router_w, c)

            def shared_half(j, g):
                c, ft = j // 2, j % 2
                if j >= 2 and g == 0:
                    pe.wait_ge(shared_hid, j - 1)
                for k in range(KT):
                    ins = mm(ps[:, 2 * (j % 2) + g, :], gu_w[:, NE, k, g * F + ft * P:g * F + (ft + 1) * P],
                             xnT[:, k, c * HALF:(c + 1) * HALF], start=(k == 0), stop=(k == 1))
                ins.then_inc(shared_gu, 1)

            shared_half(0, 0)
            turn_logits(1)
            shared_half(0, 1)
            pe.wait_ge(onehot_done, 1)
            pe.wait_ge(bf_consts, 1)
            mm(rank_ps, upper_bf[:], onehot[:], start=True, stop=False, skip_group_check=True)
            for t in range(NT - 1):
                mm(rank_ps[:, t + 1:, :], ones_bf[:], onehot[:, t:t + 1, :].to_broadcast([P, NT - 1 - t, NE]),
                   start=False, stop=True, skip_group_check=True)
            for t in range(NT):
                ins = mm(count_ps, ones_bf[:], onehot[:, t, :], start=False, stop=(t == NT - 1),
                         skip_group_check=True)
            ins.then_inc(rank_done, 1)
            for j in range(1, 4):
                for g in range(2):
                    shared_half(j, g)
            for j in range(4):
                pe.wait_ge(shared_hid, 2 * (j // 2) + 2)
                if j >= 2:
                    pe.wait_ge(shared_added, j - 1)
                for t in (2 * j, 2 * j + 1):
                    for ft in range(KT):
                        ins = mm(ps[:, 4 + j % 2, (t % 2) * DM:(t % 2 + 1) * DM], hidT[:, ft, t * P:(t + 1) * P],
                                 down_w[:, NE, ft, :], start=(ft == 0 and t % 2 == 0), stop=(ft == 1),
                                 skip_group_check=True)
                ins.then_inc(shared_down, 1)

            pe.wait_ge(shared_added, 4)
            pe.wait_ge(tile_e_done, 1)

            def turn_x(s, k, first, pair=None):
                pe.wait_ge(xg_loaded[k], 16 * ((s // 2 if pair is None else pair) + 1))
                if not first:
                    pe.wait_ge(xgT_ready, s - 1)
                for c in range(KT):
                    ins = nc.tensor.transpose(ps[:, k, c * P:(c + 1) * P], xg[:, k, c * P:(c + 1) * P], ident)
                ins.then_inc(xg_turned, 1)

            def expert(s):
                return pe.value_load(tile_ei[0:1, bass.ds(s, 1)], min_val=0, max_val=NE - 1)

            def gate_up(s, k, e, first):
                pe.wait_ge(xgT_ready, s + 1)
                if not first:
                    pe.wait_ge(hid_done, s - 1)
                for c in range(KT):
                    ins = mm(ps[:, 2 + k, :], xgT[:, k, c, :],
                             gu_w[:, bass.ds(e, 1), c, :].rearrange("p e f -> p (e f)"),
                             start=(c == 0), stop=(c == 1))
                ins.then_inc(gu_done, 1)

            def turn_hidden(s, k, first):
                pe.wait_ge(hid_done, s + 1)
                if not first:
                    pe.wait_ge(hT_ready, s - 1)
                for c in range(KT):
                    ins = nc.tensor.transpose(ps[:, 4 + k, c * P:(c + 1) * P], hid[:, k, c * P:(c + 1) * P], ident)
                ins.then_inc(hid_turned, 1)

            def down(s, k, e, first):
                pe.wait_ge(hT_ready, s + 1)
                if not first:
                    pe.wait_ge(yo_ready, s - 1)
                for c in range(KT):
                    ins = mm(ps[:, 6 + k, 0:DM], hT[:, k, c, :],
                             down_w[:, bass.ds(e, 1), c, :].rearrange("p e f -> p (e f)"),
                             start=(c == 0), stop=(c == 1))
                ins.then_inc(down_done, 1)

            def expert_turn(s, k, pair=None, ahead=True):
                early = isinstance(s, int) and s < 4
                e, e_before = expert(s), expert(s - 1)
                turn_hidden(s - 1, 1 - k, early and s < 3)
                gate_up(s, k, e, early and s < 2)
                down(s - 1, 1 - k, e_before, early and s < 3)
                if ahead:
                    turn_x(s + 2, k, False, pair)

            turn_x(0, 0, True)
            turn_x(1, 1, True)
            gate_up(0, 0, expert(0), True)
            turn_x(2, 0, False)
            for s in range(1, 4):
                expert_turn(s, s % 2)
            with nc.tensor.Fori(2, NS // 2 - 1) as i:
                for k in range(2):
                    expert_turn(2 * i + k, k, pair=i + 1)
            for s in (NS - 2, NS - 1):
                expert_turn(s, s % 2, ahead=False)
            e_last = expert(NS - 1)
            turn_hidden(NS - 1, 1, False)
            down(NS - 1, 1, e_last, False)

            pe.wait_ge(yo_ready, NS)

            def queries(b):
                wait_xnT(1, b)
                for t in (2 * b, 2 * b + 1):
                    for k in range(KT):
                        ins = mm(ps[:, 4 + b, (t % 2) * DM:(t % 2 + 1) * DM], xnT[:, k, t * P:(t + 1) * P],
                                 q_w[:, k, :], start=(k == 0 and t % 2 == 0), stop=(k == 1),
                                 skip_group_check=True)
                ins.then_inc(q_done, 1)

            turn_xn(1, 0)
            for b in range(NB):
                if b + 1 < NB:
                    turn_xn(1, b + 1)
                queries(b)

            def turn_stack(i, k):
                pe.wait_ge(built, i + 1)
                wait_from_one(pe, keysT_act, i)
                wait_from_one(pe, keysT_dve, i)
                for n in range(4):
                    ins = nc.tensor.transpose(ps[:, 0, n * P:(n + 1) * P],
                                              stack[:, k, n].rearrange("p g r -> p (g r)"), ident)
                ins.then_inc(stack_turned, 1)

            def logit_rows(i, k, n):
                if n == 0:
                    pe.wait_ge(keysT_act, i + 1)
                    pe.wait_ge(keysT_dve, i + 1)
                wait_from_one(pe, max_done, G * i + n - 1)
                heads, j = n // 2, n % 2
                mm(ps[:, 2 + n % 2, :], rowsT[k % 2][:, j * P:(j + 1) * P],
                   keysT[k][:, 2 * heads:2 * heads + 2, :].rearrange("p g n -> p (g n)")).then_inc(rows_done, 1)

            def turn_queries(i, k):
                pe.wait_ge(shift_done, i + 1)
                wait_from_one(pe, queryT_ready, i)
                for n in range(2):
                    ins = nc.tensor.transpose(ps[:, 1, n * P:(n + 1) * P],
                                              stack[:, k, n].rearrange("p g r -> p (g r)"), ident)
                ins.then_inc(query_turned, 1)

            def logit_cols(i, k, g):
                if g == 0:
                    pe.wait_ge(queryT_ready, i + 1)
                wait_from_one(pe, exp_done, G * i + g - 1)
                for j in range(2):
                    ins = mm(ps[:, 4 + g % 2, j * L:(j + 1) * L], keysT[k][:, g, j * P:(j + 1) * P],
                             queryT[k % 2][:], start=(j == 0), stop=True,
                             skip_group_check=True)
                ins.then_inc(cols_done, 1)

            def values(i, k, g):
                pe.wait_ge(exp_done, G * i + g + 1)
                if g == 0:
                    pe.wait_ge(v_copied, i + 1)
                    wait_from_one(pe, o_copied, i)
                for j in range(2):
                    ins = mm(ps[rows_of(g, ROWS), 6, 0:L], v_ones[:, k % 2, j, g, :],
                             prob[k % 2][:, g, j * L:(j + 1) * L], start=(j == 0), stop=(j == 1),
                             tile_position=(0, g * ROWS))
                ins.then_inc(pv_done, 1)

            def turn_values(i, k):
                pe.wait_ge(o_copied, i + 1)
                wait_from_one(pe, attn_done, i)
                for n in range(2):
                    ins = nc.tensor.transpose(ps[:, 7, n * P:(n + 1) * P], o_sb[:, k % 2, n * P:(n + 1) * P], ident)
                ins.then_inc(o_turned, 1)

            def attention_turn(i, k, live):
                if live(1):
                    turn_stack(i + 1, (k + 1) % SLOTS)
                if live(0):
                    logit_rows(i, k, 0)
                if live(-2):
                    logit_cols(i - 2, (k + 2) % SLOTS, 0)
                    logit_cols(i - 2, (k + 2) % SLOTS, 1)
                if live(0):
                    logit_rows(i, k, 1)
                if live(-3):
                    values(i - 3, (k + 1) % SLOTS, 0)
                if live(-1):
                    turn_queries(i - 1, (k + 3) % SLOTS)
                if live(0):
                    logit_rows(i, k, 2)
                if live(-3):
                    values(i - 3, (k + 1) % SLOTS, 1)
                    values(i - 3, (k + 1) % SLOTS, 2)
                    values(i - 3, (k + 1) % SLOTS, 3)
                if live(-2):
                    logit_cols(i - 2, (k + 2) % SLOTS, 2)
                if live(0):
                    logit_rows(i, k, 3)
                if live(-2):
                    logit_cols(i - 2, (k + 2) % SLOTS, 3)
                if live(-4):
                    turn_values(i - 4, k)

            def turn_attn(b):
                pe.wait_ge(attn_done, NG // NB * (b + 1))
                if b in (1, 2):
                    pe.wait_ge(max_done, G * NG)
                elif b == 3:
                    pe.wait_ge(queryT_ready, NG)
                for f in range(KT):
                    for j in range(2):
                        ins = nc.tensor.transpose(ps[:, OUT_BANKS[b], f * L + j * P:f * L + (j + 1) * P],
                                                  attn[:, j, b * DM + f * P:b * DM + (f + 1) * P], ident)
                ins.then_inc(attn_turned, 1)

            def project(b):
                pe.wait_ge(attnT_copied, b + 1)
                for t in (2 * b, 2 * b + 1):
                    for k in range(KT):
                        ins = mm(ps[:, OUT_BANKS[b], (t % 2) * DM:(t % 2 + 1) * DM], attnT[:, k, t * P:(t + 1) * P],
                                 out_w[:, k, :], start=(k == 0 and t % 2 == 0), stop=(k == 1),
                                 skip_group_check=True)
                ins.then_inc(proj_done, 1)

            def after_turn(i):
                if i == NG:
                    turn_attn(0)
                elif i == NG + 1:
                    turn_attn(1)
                    turn_attn(2)
                elif i == NG + 2:
                    project(0)

            run_turns(nc.tensor, attention_turn, after_turn)
            project(1)
            turn_attn(3)
            project(2)
            turn_xn(2, 0)
            project(3)
            turn_xn(2, 1)


            pe.wait_ge(last_w_loaded, 64)

            def low_rank(t):
                if t >= len(LOW_BANKS):
                    pe.wait_ge(low_masked, t + 1 - len(LOW_BANKS))
                wait_xnT(2, t // 2)
                if t == 3:
                    wait_xnT(2, 3)
                for k in range(KT):
                    ins = mm(ps[:, LOW_BANKS[t % len(LOW_BANKS)], :], xnT[:, k, t * P:(t + 1) * P], a_w[:, k, :],
                             start=(k == 0), stop=(k == 1))
                ins.then_inc(low_done, 1)

            def turn_low(t):
                pe.wait_ge(low_masked, t + 1)
                if t >= 2:
                    pe.wait_ge(low_lo_ready, t - 1)
                for c in range(4):
                    ins = nc.tensor.transpose(ps[:, TURN_BANKS[t % 2], c * P:(c + 1) * P],
                                              low[:, t % 2, c * P:(c + 1) * P], ident)
                ins.then_inc(low_turned, 1)

            def high(t):
                pe.wait_ge(low_lo_ready, t + 1)
                if t >= 2:
                    pe.wait_ge(tile_done, t - 1)
                elif t == 0:
                    pe.wait_ge(logitT_copied, 4)
                    pe.wait_ge(b_split, 1)
                for c in range(4):
                    hi, lo = [part[:, t % 2, c * P:(c + 1) * P] for part in (low_hiT, low_loT)]
                    for n, (rows, weights) in enumerate(((hi, b_hi), (hi, b_lo), (lo, b_hi))):
                        ins = mm(ps[:, 4 + t % 2, 0:DM], rows, weights[:, c, :],
                                 start=(c == 0 and n == 0), stop=(c == 3 and n == 2))
                ins.then_inc(last_done, 1)

            low_rank(0)
            turn_xn(2, 2)
            turn_xn(2, 3)
            router(2, wr_w, 0)
            router(2, wr_w, 1)
            turn_logits(2)
            for t in range(1, len(LOW_BANKS)):
                low_rank(t)
            for t in range(NT + 1):
                if t < NT:
                    turn_low(t)
                if t + 4 < NT:
                    low_rank(t + 4)
                if t >= 1:
                    high(t - 1)

        @block.scalar
        def _(act):
            own = Chain(act, act_own)
            nc.scalar.preload_act_table_set("natural_log_exp_and_others")
            act.wait_ge(ssm_w_loaded, 48)
            for et in range(KT):
                act.wait_ge(xin_done, et + 1)
                nc.scalar.activation(delta[:, et, :], xin_ps[et], ACT.Identity, bias=conv_b[:, et, :],
                                     scale=tap_w[:, et, TAPS - 1:TAPS]).then_inc(tap0_done, 1)
            nc.scalar.activation(neg_a[:], a_log, ACT.Exp).then_inc(expa_done, 1)
            act.wait_ge(ln0_stats, 1)
            act.wait_ge(cols_set, 1)
            own.then_wait(nc.scalar.activation(ln_var[:], mean_var[:, :, 1], ACT.Ln, bias=eps_col[:]))
            nc.scalar.activation(rstd[:], ln_var[:], ACT.Exp, scale=-0.5).then_inc(ln0_rstd, 1)
            nc.scalar.preload_act_table_set("silu_and_others")
            act.wait_ge(ln0_shift, 1)
            for b in range(NB):
                for et in range(KT):
                    t = 2 * b + et
                    nc.scalar.activation(gate_z[:, et, b * L:(b + 1) * L], x_tok[:, t, :], ACT.Silu,
                                         bias=shift[:, t:t + 1], scale=rstd[:, t:t + 1])
            act.wait_ge(angle_done, 1)
            nc.scalar.activation(angle[:], angle[:], ACT.Sin).then_inc(trig_done, 1)
            for et in range(KT):
                act.wait_ge(conv_done, et + 1)
                nc.scalar.activation(u[:, et, :], delta[:, et, :], ACT.Silu).then_inc(u_done, 1)
            nc.scalar.preload_act_table_set("natural_log_exp_and_others")
            for c in range(2):
                act.wait_ge(xdbl_done, c + 1)
                nc.scalar.copy(xdbl[:, c * HALF:(c + 1) * HALF], xdbl_ps[:, c * HALF:(c + 1) * HALF]) \
                    .then_inc(xdbl_copied, 1)
            for et in range(KT):
                act.wait_ge(dt_done, et + 1)
                nc.scalar.activation(read[:, et, :], dt_ps[et], ACT.Abs, bias=dt_b[:, et, :]).then_inc(abs_done, 1)
                act.wait_ge(abs_done, et + 1)
                own.then_wait(nc.scalar.activation(read[:, et, :], read[:, et, :], ACT.Exp, scale=-1.0))
                nc.scalar.activation(read[:, et, :], read[:, et, :], ACT.Ln, bias=one_col[:]).then_inc(log_done, 1)

            def decay_and_c(n, k, first):
                act.wait_ge(c_ready, n + 1)
                if not first:
                    act.wait_ge(read_done[1], n - 1)
                elif k == 0:
                    act.wait_ge(sorted_cleared, 32)
                nc.scalar.copy(c_rows[:, k, :], c_ps).then_inc(c_copied, 1)
                for et in range(KT):
                    act.wait_ge(delta_done, et + 1)
                    if not first or k > 0:
                        act.wait_ge(scan_done[et], n)
                    nc.scalar.activation(
                        decay[:, et, :].rearrange("p (b l) -> p b l", b=NB)[:, :, 1:],
                        delta[:, et, :].rearrange("p (b l) -> p b l", b=NB)[:, :, 1:],
                        ACT.Exp, scale=neg_a[:, et, bass.ds(n, 1)]).then_inc(decay_ready[et], 1)

            act.wait_ge(setup_done, 1)
            for k in range(2):
                decay_and_c(k, k, first=True)
            with nc.scalar.Fori(1, DS // 2) as i:
                for k in range(2):
                    decay_and_c(2 * i + k, k, first=False)

            def norm_rstd(r, b):
                act.wait_ge(ln_stats, NB * r + b + 1)
                own.then_wait(nc.scalar.activation(ln_var[:, 2 * b:2 * b + 2], mean_var[:, 2 * b:2 * b + 2, 1], ACT.Ln,
                                                   bias=eps_col[:]))
                nc.scalar.activation(rstd[:, 2 * b:2 * b + 2], ln_var[:, 2 * b:2 * b + 2], ACT.Exp, scale=-0.5) \
                    .then_inc(ln_rstd, 1)

            def copy_xnT(r, b):
                act.wait_ge(xn_turned, NB * r + b + 1)
                bank = OUT_BANKS[b] if r == 2 else b
                nc.scalar.copy(xnT[:, :, b * L:(b + 1) * L], ps[:, bank, :].rearrange("p (k n) -> p k n", k=KT)) \
                    .then_inc(xnT_copied[0], 1)

            def copy_kv(t):
                b, j = t // 2, t % 2
                act.wait_ge(kv_done, t + 1)
                nc.scalar.copy(k_tok[:, t, :], ps[:, 4 + t % 4, 0:DM])
                nc.scalar.copy(v_tok[:, 8 * b:8 * b + 8, j * G * HD:(j + 1) * G * HD],
                               ps[:, 4 + t % 4, DM:2 * DM].rearrange("p (g c) -> p g c", c=G * HD)) \
                    .then_inc(kv_copied, 1)

            for t in range(NT):
                copy_kv(t)
                if 1 <= t < 5:
                    norm_rstd(0, t - 1)
                if t == 5:
                    copy_xnT(0, 0)
            copy_xnT(0, 2)
            for c in range(2):
                act.wait_ge(logitT_done, 1 + c)
                nc.scalar.copy(logitT[:, c * HALF:(c + 1) * HALF], logitT_ps[:, c * HALF:(c + 1) * HALF]) \
                    .then_inc(logitT_copied, 1)
            act.wait_ge(top_done, 1)
            nc.scalar.activation(score[:], top[:], ACT.Exp, scale=-1.0).then_inc(exp_top_done, 1)
            nc.scalar.preload_act_table_set("silu_and_others")
            for j in range(4):
                act.wait_ge(shared_gu, 2 * j + 1)
                nc.scalar.activation(silu_g[:, j, :], ps[:, 2 * (j % 2), :], ACT.Silu).then_inc(shared_silu, 1)

            def silu_tile(s, k, first):
                act.wait_ge(gu_done, s + 1)
                if not first:
                    act.wait_ge(hid_done, s - 1)
                nc.scalar.activation(sg[:, k, :], ps[:, 2 + k, 0:F], ACT.Silu).then_inc(sg_done, 1)

            def copy_hT(s, k, first):
                act.wait_ge(hid_turned, s + 1)
                if not first:
                    act.wait_ge(down_done, s - 1)
                nc.scalar.copy(hT[:, k].rearrange("p c t -> p (c t)"), ps[:, 4 + k, 0:F]).then_inc(hT_ready, 1)

            for s in range(2):
                silu_tile(s, s, True)
                copy_hT(s, s, True)
            with nc.scalar.Fori(1, NS // 2) as i:
                for k in range(2):
                    silu_tile(2 * i + k, k, False)
                    copy_hT(2 * i + k, k, False)

            nc.scalar.preload_act_table_set("natural_log_exp_and_others")
            for b in range(NB):
                norm_rstd(1, b)
                if b == 1:
                    copy_xnT(1, 0)
            for b in range(1, NB):
                copy_xnT(1, b)

            def copy_rowsT(i, k):
                act.wait_ge(stack_turned, i + 1)
                wait_from_one(act, rows_done, G * (i - 1))
                nc.scalar.copy(rowsT[k % 2][:], ps[:, 0, 0:L]).then_inc(rowsT_ready, 1)

            def spread_keys(i, k):
                wait_from_one(act, cols_done, G * (i + 1 - SLOTS))
                for g in range(G // 2):
                    ins = nc.scalar.copy(keysT[k][rows_of(g, ROWS), g, :], ps[rows_of(g, ROWS), 0, L:2 * L])
                ins.then_inc(keysT_act, 1)

            def copy_queryT(i, k):
                act.wait_ge(query_turned, i + 1)
                wait_from_one(act, cols_done, G * (i - 1))
                nc.scalar.copy(queryT[k % 2][:], ps[:, 1, 0:L]).then_inc(queryT_ready, 1)

            def exponential(i, k, g):
                act.wait_ge(cols_done, G * i + g + 1)
                wait_from_one(act, pv_done, G * (i - 2) + g + 1)
                nc.scalar.activation(prob[k % 2][:, g, :], ps[:, 4 + g % 2, :], ACT.Exp, scale=HD ** -0.5) \
                    .then_inc(exp_done, 1)

            def copy_o(i, k):
                act.wait_ge(pv_done, G * i + G)
                wait_from_one(act, o_turned, i - 1)
                nc.scalar.copy(o_sb[:, k % 2, :], ps[:, 6, 0:L]).then_inc(o_copied, 1)

            def attention_turn(i, k, live):
                if live(1):
                    copy_rowsT(i + 1, (k + 1) % SLOTS)
                if live(-2):
                    exponential(i - 2, (k + 2) % SLOTS, 0)
                    exponential(i - 2, (k + 2) % SLOTS, 1)
                if live(1):
                    spread_keys(i + 1, (k + 1) % SLOTS)
                if live(-1):
                    copy_queryT(i - 1, (k + 3) % SLOTS)
                if live(-3):
                    copy_o(i - 3, (k + 1) % SLOTS)
                if live(-2):
                    exponential(i - 2, (k + 2) % SLOTS, 2)
                    exponential(i - 2, (k + 2) % SLOTS, 3)

            def copy_attnT(b):
                act.wait_ge(attn_turned, b + 1)
                nc.scalar.copy(attnT[:, :, b * L:(b + 1) * L],
                               ps[:, OUT_BANKS[b], :].rearrange("p (k n) -> p k n", k=KT)) \
                    .then_inc(attnT_copied, 1)

            def after_turn(i):
                if i == NG:
                    copy_attnT(0)
                elif i == NG + 1:
                    copy_attnT(1)
                    copy_attnT(2)

            run_turns(nc.scalar, attention_turn, after_turn)

            norm_rstd(2, 0)
            copy_attnT(3)
            norm_rstd(2, 1)
            norm_rstd(2, 2)
            copy_xnT(2, 0)
            copy_xnT(2, 1)
            norm_rstd(2, 3)
            copy_xnT(2, 2)
            copy_xnT(2, 3)
            for c in range(2):
                act.wait_ge(logitT_done, 3 + c)
                nc.scalar.copy(logitT[:, c * HALF:(c + 1) * HALF], logitT_ps[:, c * HALF:(c + 1) * HALF]) \
                    .then_inc(logitT_copied, 1)
            act.wait_ge(shifted_done, 1)
            nc.scalar.activation(pick_w[:], pick_w[:], ACT.Exp).then_inc(exp_logit_done, 1)
            for t in range(NT):
                act.wait_ge(low_turned, t + 1)
                if t >= 2:
                    act.wait_ge(last_done, t - 1)
                nc.scalar.copy(low_hiT[:, t % 2, :], ps[:, TURN_BANKS[t % 2], :]).then_inc(low_hi_ready, 1)

        @block.vector
        def _(dve):
            own = Chain(dve, dve_own)
            vec = nc.vector

            def layer_norm_stats(done, tiles):
                for t in tiles:
                    ins = vec.bn_stats(stats[:, t, :], x_tok[:, t, :])
                own.then_wait(ins)
                for t in tiles:
                    ins = vec.bn_aggr(mean_var[:, t, :], stats[:, t, :])
                ins.then_inc(done, 1)

            dve.wait_ge(pos_loaded, 16)
            pos2 = pos[:].rearrange("p t c -> p (t c)")
            flat = [angle[:, c].rearrange("p t (c h) -> p (t c) h", h=2) for c in range(2)]
            for half in range(2):
                freq = 10000.0 ** (-half / 2)
                vec.tensor_scalar(flat[0][:, :, half], pos2, freq, None, ALU.mult)
                ins = vec.tensor_scalar(flat[1][:, :, half], pos2, freq, math.pi / 2, ALU.mult, ALU.add)
            own.then_wait(ins)
            own.then_wait(vec.tensor_scalar(turns[:], angle[:], 1 / (2 * math.pi), ROUND, ALU.mult, ALU.add))
            own.then_wait(vec.tensor_scalar(turns[:], turns[:], ROUND, None, ALU.subtract))
            for part in (TWO_PI_HI, TWO_PI_LO):
                own.then_wait(vec.scalar_tensor_tensor(out=angle[:], in0=turns[:], scalar=-part, in1=angle[:],
                                                       op0=ALU.mult, op1=ALU.add))
            vec.tensor_scalar(angle[:], angle[:], PI_BELOW, -PI_BELOW, ALU.min, ALU.max).then_inc(angle_done, 1)

            vec.memset(ones_bf[:], 1.0)
            vec.memset(zeros8[:], 0.0)
            dve.wait_ge(consts_loaded, 16)
            vec.tensor_copy(upper_bf[:], upper).then_inc(bf_consts, 1)
            dve.wait_ge(x_loaded, 16)
            layer_norm_stats(ln0_stats, range(NT))
            for j in range(TAPS - 1):
                back = TAPS - 1 - j
                for et in range(KT):
                    if j == 0:
                        dve.wait_ge(tap0_done, et + 1)
                    acc = delta[:, et, :].rearrange("p (b l) -> p b l", b=NB)[:, :, back:]
                    xin = xin_ps[et].rearrange("p (b l) -> p b l", b=NB)[:, :, 0:L - back]
                    ins = vec.scalar_tensor_tensor(out=acc, in0=xin, scalar=tap_w[:, et, j:j + 1], in1=acc,
                                                   op0=ALU.mult, op1=ALU.add)
                    if j == TAPS - 2:
                        ins.then_inc(conv_done, 1)
                if j < TAPS - 2:
                    own.then_wait(ins)
                if j == 0:
                    dve.wait_ge(ln0_rstd, 1)
                    vec.scalar_tensor_tensor(out=shift[:], in0=mean_var[:, :, 0], scalar=-1.0, in1=rstd[:],
                                             op0=ALU.mult, op1=ALU.mult).then_inc(ln0_shift, 1)

            dve.wait_ge(xdbl_copied, 2)
            rest = drive[0:96, 0, :]
            own.then_wait(vec.tensor_copy(bc3[:], xdbl[0:96, :]))
            own.then_wait(vec.tensor_tensor(rest, xdbl[0:96, :], bc3[:], ALU.subtract))
            vec.tensor_copy(bc3[32:64, :], rest[32:64, :])
            own.then_wait(vec.tensor_copy(bc3[64:96, :], rest[64:96, :]))
            vec.tensor_tensor(bc3[64:96, :], rest[64:96, :], bc3[64:96, :], ALU.subtract).then_inc(bc3_done, 1)

            for et in range(KT):
                dve.wait_ge(abs_done, et + 1)
                vec.tensor_scalar(state[:, et, :], dt_ps[et], dt_b[:, et, :], 0.0, ALU.add, ALU.max) \
                   .then_inc(relu_done, 1)
            for et in range(KT):
                dve.wait_ge(log_done, et + 1)
                dve.wait_ge(relu_done, et + 1)
                vec.tensor_tensor(delta[:, et, :], state[:, et, :], read[:, et, :], ALU.add).then_inc(delta_done, 1)
                dve.wait_ge(delta_done, et + 1)
                ins = vec.tensor_tensor(du[:, et, :], delta[:, et, :], u[:, et, :], ALU.mult)
            own.then_wait(ins)

            def scan_state(n, first):
                dve.wait_ge(b_ready, n + 1)
                for et in range(KT):
                    if not first:
                        dve.wait_ge(scan_done[et], n)
                    vec.tensor_tensor(drive[:, et, :], du[:, et, :], b_ps, ALU.mult).then_inc(drive_done, 1)
                for et in range(KT):
                    dve.wait_ge(decay_ready[et], n + 1)
                    dve.wait_ge(drive_done, 2 * n + et + 1)
                    if not first:
                        dve.wait_ge(read_done[et], n)
                    vec.tensor_tensor_scan(state[:, et, :], decay[:, et, :], drive[:, et, :], 0.0,
                                           ALU.mult, ALU.add).then_inc(scan_done[et], 1)

            scan_state(0, True)
            with nc.vector.Fori(1, DS) as n:
                scan_state(n, False)
            dve.wait_ge(scan_done[1], DS)
            dve.wait_ge(c_copied, DS)
            dve.wait_ge(y_added[1], DS - 2)
            vec.tensor_tensor(products[1][:, 1, :], state[:, 1, :], c_rows[:, 1, :], ALU.mult) \
               .then_inc(last_read_done, 1)

            for et in range(KT):
                dve.wait_ge(y_added[et], DS)
                vec.tensor_tensor(u[:, et, :], y_ps[et], gate_z[:, et, :], ALU.mult).then_inc(y_gated, 1)
            for c in range(2):
                dve.wait_ge(y_turned, c + 1)
                vec.tensor_tensor(x_tok[:, 4 * c:4 * c + 4, :], x_tok[:, 4 * c:4 * c + 4, :],
                                  turned[:, 4 * c:4 * c + 4, :], ALU.add).then_inc(x1_done, 1)

            def batch_stats(b):
                layer_norm_stats(ln_stats, (2 * b, 2 * b + 1))

            def normalise(r, b):
                dve.wait_ge(ln_rstd, NB * r + b + 1)
                for t in (2 * b, 2 * b + 1):
                    ins = vec.tensor_scalar(xn[:, t, :], x_tok[:, t, :], mean_var[:, t, 0:1], rstd[:, t:t + 1],
                                            ALU.subtract, ALU.mult)
                ins.then_inc(xn_done, 1)

            def copy_xnT(r, b):
                dve.wait_ge(xn_turned, NB * r + b + 1)
                vec.tensor_copy(xnT[:, :, b * L:(b + 1) * L], ps[:, b, :].rearrange("p (k n) -> p k n", k=KT)) \
                   .then_inc(xnT_copied[1], 1)

            def first_of_top(done):
                vec.tensor_reduce(top[:], logit[:], AX.X, ALU.max).then_inc(top_done, 1)
                dve.wait_ge(top_done, 1 if done is onehot_done else 2)
                own.then_wait(vec.tensor_tensor(pick[:], logit[:], top[:].unsqueeze(2).to_broadcast([P, NT, NE]),
                                                ALU.is_equal))
                own.then_wait(vec.tensor_tensor(pick[:], pick[:], e_minus_8.unsqueeze(1).to_broadcast([P, NT, NE]),
                                                ALU.mult))
                own.then_wait(vec.tensor_reduce(first_e[:], pick[:], AX.X, ALU.min))
                vec.tensor_tensor(onehot[:], e_minus_8.unsqueeze(1).to_broadcast([P, NT, NE]),
                                  first_e[:].unsqueeze(2).to_broadcast([P, NT, NE]), ALU.is_equal) \
                   .then_inc(done, 1)

            dve.wait_ge(trig_done, 1)
            vec.tensor_copy(cos8[:].rearrange("p t (c h) -> p (t c) h", h=2),
                            angle[:, 1].rearrange("p t c -> p (t c)").unsqueeze(2).to_broadcast([P, NT * 4, 2]))
            vec.tensor_copy(sin_pos[:], angle[:, 0])
            vec.tensor_scalar(sin_neg[:], angle[:, 0], -1.0, None, ALU.mult).then_inc(trig_ready, 1)
            for b in range(NB):
                dve.wait_ge(x1_done, b // 2 + 1)
                batch_stats(b)
                if b >= 1:
                    normalise(0, b - 1)
            normalise(0, NB - 1)
            copy_xnT(0, 1)
            copy_xnT(0, 3)
            dve.wait_ge(logit_turned, 1)
            own.then_wait(vec.tensor_copy(logit[:], logit_ps))
            first_of_top(onehot_done)

            def multiply_shared(j):
                dve.wait_ge(shared_gu, 2 * j + 2)
                dve.wait_ge(shared_silu, j + 1)
                vec.tensor_tensor(hidT[:, j % 2, (j // 2) * HALF:(j // 2 + 1) * HALF], ps[:, 2 * (j % 2) + 1, :],
                                  silu_g[:, j, :], ALU.mult).then_inc(shared_hid, 1)

            multiply_shared(0)
            dve.wait_ge(onehot_done, 1)
            dve.wait_ge(rank_done, 1)
            own.then_wait(vec.tensor_copy(tiles_e[:], count_ps))
            own.then_wait(vec.tensor_tensor(full_tile[:], tiles_e[:].unsqueeze(2).to_broadcast([P, NE, NE]),
                                            j_times_128.unsqueeze(1).to_broadcast([P, NE, NE]), ALU.is_gt))
            own.then_wait(vec.tensor_reduce(tiles_e[:], full_tile[:], AX.X, ALU.add))
            own.then_wait(vec.tensor_tensor_scan(tiles_upto[:], tiles_e[:], zeros8[:], 0.0, ALU.add, ALU.add))
            own.then_wait(vec.tensor_tensor(tiles_e[:], tiles_upto[:], tiles_e[:], ALU.subtract))
            own.then_wait(vec.scalar_tensor_tensor(
                out=pick[:], in0=tiles_e[:].unsqueeze(1).to_broadcast([P, NT, NE]), scalar=float(P), in1=rank_ps,
                op0=ALU.mult, op1=ALU.add))
            own.then_wait(vec.tensor_tensor(pick[:], pick[:], onehot[:], ALU.mult))
            own.then_wait(vec.tensor_reduce(slot_f[:], pick[:], AX.X, ALU.add))
            vec.tensor_copy(slot[:], slot_f[:]).then_inc(halfdone, 1)
            own.then_wait(vec.tensor_tensor(tile_cmp[:], tiles_upto[0:1, :].unsqueeze(1).to_broadcast([1, NS, NE]),
                                            tile_no[0:1, :].unsqueeze(2).to_broadcast([1, NS, NE]), ALU.is_le))
            own.then_wait(vec.tensor_reduce(tile_e[:], tile_cmp[:], AX.X, ALU.add))
            vec.tensor_scalar(tile_ei[:], tile_e[:], float(NE - 1), None, ALU.min).then_inc(tile_e_done, 1)
            multiply_shared(1)
            dve.wait_ge(exp_top_done, 1)
            own.then_wait(vec.tensor_scalar(score[:], score[:], 1.0, None, ALU.add))
            own.then_wait(vec.reciprocal(score[:], score[:]))
            for t in range(NT):
                vec.tensor_scalar(scaled[:, t, :], xn[:, t, :], score[:, t:t + 1], None, ALU.mult) \
                   .then_inc(scaled_done, 1)

            for j in range(2, 4):
                multiply_shared(j)
            for j in range(4):
                dve.wait_ge(shared_down, j + 1)
                pair = x_tok[:, 2 * j:2 * j + 2, :].rearrange("p t d -> p (t d)")
                vec.tensor_tensor(pair, pair, ps[:, 4 + j % 2, :], ALU.add).then_inc(shared_added, 1)

            def copy_xgT(s, k, first):
                dve.wait_ge(xg_turned, s + 1)
                if not first:
                    dve.wait_ge(gu_done, s - 1)
                vec.tensor_copy(xgT[:, k].rearrange("p c t -> p (c t)"), ps[:, k, 0:DM]).then_inc(xgT_ready, 1)

            def multiply(s, k, first):
                dve.wait_ge(sg_done, s + 1)
                if not first:
                    dve.wait_ge(hid_turned, s - 1)
                vec.tensor_tensor(hid[:, k, :], ps[:, 2 + k, F:2 * F], sg[:, k, :], ALU.mult).then_inc(hid_done, 1)

            def copy_yo(s, k, first, pair=None):
                dve.wait_ge(down_done, s + 1)
                if not first:
                    dve.wait_ge(yo_stored[k], 16 * (s // 2 if pair is None else pair))
                vec.tensor_copy(yo[:, k, :], ps[:, 6 + k, 0:DM]).then_inc(yo_ready, 1)

            copy_xgT(0, 0, True)
            copy_xgT(1, 1, True)
            for s in range(4):
                multiply(s, s % 2, s < 2)
                if s >= 1:
                    copy_yo(s - 1, (s - 1) % 2, s < 3)
                copy_xgT(s + 2, s % 2, False)
            with nc.vector.Fori(2, NS // 2 - 1) as i:
                for k in range(2):
                    s = 2 * i + k
                    multiply(s, k, False)
                    copy_yo(s - 1, 1 - k, False, pair=i - 1 + k)
                    copy_xgT(s + 2, k, False)
            for k in range(2):
                s = NS - 2 + k
                multiply(s, k, False)
                copy_yo(s - 1, 1 - k, False)
            copy_yo(NS - 1, 1, False)

            q_ps = banks(4, 4).rearrange("p (t d) -> p t d", d=DM)

            def rotate_queries(b):
                dve.wait_ge(q_done, b + 1)
                tiles = slice(2 * b, 2 * b + 2)
                rotate(vec, q_ps[:, tiles], swapped[:, tiles], tiles)
                ins = vec.tensor_tensor(q_cos[:, tiles].rearrange("p t (h c) -> p t h c", c=HD),
                                        q_ps[:, tiles].rearrange("p t (h c) -> p t h c", c=HD),
                                        cos8[:, tiles].unsqueeze(2).to_broadcast([P, 2, NH, HD]), ALU.mult)
                own.then_wait(ins)
                add_rotated(vec, q_cos, swapped, 0, b).then_inc(q_rotated, 1)

            for b in range(NB):
                dve.wait_ge(gathered[b], 32)
                tiles = slice(2 * b, 2 * b + 2)
                vec.tensor_tensor(x_tok[:, tiles, :], x_tok[:, tiles, :], routed[:, tiles, :], ALU.add) \
                   .then_inc(x2_done, 1)
                dve.wait_ge(x2_done, b + 1)
                batch_stats(b)
                if b >= 1:
                    normalise(1, b - 1)
            dve.wait_ge(k_rotated, 1)
            normalise(1, NB - 1)
            rotate_queries(0)
            for b in range(1, NB):
                rotate_queries(b)

            def spread_keys(i, k):
                dve.wait_ge(rowsT_ready, i + 1)
                wait_from_one(dve, cols_done, G * (i + 1 - SLOTS))
                for g in range(G // 2, G):
                    ins = vec.tensor_copy(keysT[k][rows_of(g, ROWS), g, :], ps[rows_of(g, ROWS), 0, L:2 * L])
                ins.then_inc(keysT_dve, 1)

            def row_maximum(i, k, n):
                dve.wait_ge(rows_done, G * i + n + 1)
                heads = slice(n // 2 * 2, n // 2 * 2 + 2)
                vec.tensor_reduce(row_max[:, k % 2, n % 2, heads],
                                  ps[:, 2 + n % 2, :].rearrange("p (g n) -> p g n", n=L),
                                  AX.X, ALU.max).then_inc(max_done, 1)

            def write_shift(i, k):
                dve.wait_ge(max_done, G * i + G)
                dve.wait_ge(stack_turned, i + 1)
                wait_from_one(dve, query_turned, i + 1 - SLOTS)
                hi, lo = stack[:, k, 0:2, :, SPLIT], stack[:, k, 0:2, :, SPLIT + 1]
                vec.tensor_scalar(hi.bitcast(F32R), row_max[:, k % 2], -1.0, None, ALU.mult).then_inc(shift_hi, 1)
                dve.wait_ge(shift_hi, i + 1)
                vec.scalar_tensor_tensor(out=lo.bitcast(F32R), in0=row_max[:, k % 2], scalar=-1.0, in1=hi,
                                         op0=ALU.mult, op1=ALU.subtract).then_inc(shift_done, 1)

            def divide(i, k):
                dve.wait_ge(o_turned, i + 1)
                heads = ps[:, 7, 0:2 * P].rearrange("p (j g r) -> p j g r", j=2, g=G)
                wait_from_one(dve, attn_done, i)
                vec.reciprocal(inv_sum[:], heads[:, :, :, HD]).then_inc(inv_done, 1)
                dve.wait_ge(inv_done, i + 1)
                vec.tensor_tensor(attn[:, :, bass.ds(i * (G * HD), G * HD)].rearrange("p j (g c) -> p j g c", g=G),
                                  heads[:, :, :, 0:HD], inv_sum[:].unsqueeze(3).to_broadcast([P, 2, G, HD]),
                                  ALU.mult).then_inc(attn_done, 1)

            def attention_turn(i, k, live):
                if live(0):
                    row_maximum(i, k, 0)
                    row_maximum(i, k, 1)
                if live(1):
                    spread_keys(i + 1, (k + 1) % SLOTS)
                if live(0):
                    row_maximum(i, k, 2)
                    row_maximum(i, k, 3)
                if live(-4):
                    divide(i - 4, k)
                if live(0):
                    write_shift(i, k)

            def add_projected(b):
                dve.wait_ge(proj_done, b + 1)
                pair = x_tok[:, 2 * b:2 * b + 2, :].rearrange("p t d -> p (t d)")
                vec.tensor_tensor(pair, pair, ps[:, OUT_BANKS[b], :], ALU.add).then_inc(x3_done, 1)
                dve.wait_ge(x3_done, b + 1)
                batch_stats(b)

            def after_turn(i):
                if i == NG + 2:
                    dve.wait_ge(bias_added, NB)
                    add_projected(0)

            run_turns(nc.vector, attention_turn, after_turn)
            add_projected(1)
            normalise(2, 0)
            add_projected(2)
            normalise(2, 1)
            add_projected(3)
            normalise(2, 2)
            normalise(2, 3)
            dve.wait_ge(logit_turned, 2)
            own.then_wait(vec.tensor_tensor(logit[:], logit_ps, br_row[:].unsqueeze(1).to_broadcast([P, NT, NE]),
                                            ALU.add))
            first_of_top(onehot2_done)
            vec.tensor_tensor(pick_w[:], logit[:], top[:].unsqueeze(2).to_broadcast([P, NT, NE]), ALU.subtract) \
               .then_inc(shifted_done, 1)
            dve.wait_ge(exp_logit_done, 1)
            own.then_wait(vec.tensor_reduce(weight[:], pick_w[:], AX.X, ALU.add))
            own.then_wait(vec.reciprocal(weight[:], weight[:]))
            own.then_wait(vec.tensor_scalar(weight[:], weight[:], 1.0 / RANK, None, ALU.mult))
            dve.wait_ge(onehot2_done, 1)
            own.then_wait(vec.tensor_tensor(pick_w[:], onehot[:], weight[:].unsqueeze(2).to_broadcast([P, NT, NE]),
                                            ALU.mult))
            for t in range(NT + 2):
                if t < NT:
                    dve.wait_ge(low_done, t + 1)
                    if t >= 2:
                        dve.wait_ge(low_turned, t - 1)
                    vec.tensor_tensor(low[:, t % 2, :].rearrange("p (e r) -> p e r", r=RANK),
                                      ps[:, LOW_BANKS[t % len(LOW_BANKS)], :].rearrange("p (e r) -> p e r", r=RANK),
                                      pick_w[:, t, :].unsqueeze(2).to_broadcast([P, NE, RANK]), ALU.mult) \
                       .then_inc(low_masked, 1)
                if 1 <= t <= NT:
                    dve.wait_ge(low_hi_ready, t)
                    if t >= 3:
                        dve.wait_ge(last_done, t - 2)
                    half = (t - 1) % 2
                    vec.tensor_tensor(low_loT[:, half, :], ps[:, TURN_BANKS[half], :], low_hiT[:, half, :],
                                      ALU.subtract).then_inc(low_lo_ready, 1)
                if t >= 2:
                    dve.wait_ge(last_done, t - 1)
                    vec.tensor_tensor(x_tok[:, t - 2, :], x_tok[:, t - 2, :], ps[:, 4 + t % 2, 0:DM], ALU.add) \
                       .then_inc(tile_done, 1)

        @block.gpsimd
        def _(pool):
            own = Chain(pool, pool_own)
            pl = nc.gpsimd
            pl.memset(eps_col[:], LN_EPS)
            pl.memset(one_col[:], 1.0)
            pl.memset(zero_rows, 0.0).then_inc(zeros_set, 1)
            pl.memset(decay[:].rearrange("p e (b l) -> p e b l", b=NB)[:, :, :, 0:1], 0.0).then_inc(cols_set, 1)
            pool.wait_ge(zeros_set, 1)
            for k in range(SLOTS):
                pl.tensor_scalar(keysT[k][:].rearrange("p g n -> p (g n)"), zero_rows[:, 0:G * L], 1.0, 1.0,
                                 ALU.mult, ALU.mult)
            pool.wait_ge(consts_loaded, 16)
            pool.wait_ge(ssm_w_loaded, 48)
            pl.tensor_copy(ident3[:], ident3f[0:96, :])
            for et in range(KT):
                pl.tensor_scalar(diag_d[:, et, :], ident, d_skip[:, et, :], 1.0, ALU.mult, ALU.mult)
            pool.wait_ge(expa_done, 1)
            pl.tensor_scalar(neg_a[:], neg_a[:], -1.0, 1.0, ALU.mult, ALU.mult).then_inc(setup_done, 1)

            def read_state(n, k, first, tiles=range(KT)):
                for et in tiles:
                    pool.wait_ge(scan_done[et], n + 1)
                    pool.wait_ge(c_copied, n + 1)
                    if not first:
                        pool.wait_ge(y_added[et], n - 1)
                    pl.tensor_tensor(products[k][:, et, :], state[:, et, :], c_rows[:, k, :], ALU.mult) \
                      .then_inc(read_done[et], 1)

            for k in range(2):
                read_state(k, k, first=True)
            with nc.gpsimd.Fori(1, DS // 2 - 1) as i:
                for k in range(2):
                    read_state(2 * i + k, k, first=False)
            read_state(DS - 2, 0, first=False)
            read_state(DS - 1, 1, first=False, tiles=(0,))

            for t in range(NT):
                pool.wait_ge(scaled_done, t + 1)
                if t == 0:
                    pool.wait_ge(halfdone, 1)
                    pool.wait_ge(sorted_cleared, 32)
                pl.indirect_dma_start(sorted_x, bass.IndirectOffsetOnAxis(ap=slot[:, t:t + 1], axis=0),
                                      scaled[:, t, :], None).then_inc(scattered, 16)
            pool.wait_ge(trig_ready, 1)
            pool.wait_ge(kv_copied, NT)
            pool.wait_ge(y_turned, 2)
            own.then_wait(rotate(pl, k_tok, swapped, slice(0, NT)))
            own.then_wait(pl.tensor_tensor(k_tok.rearrange("p t (h c) -> p t h c", c=HD),
                                           k_tok.rearrange("p t (h c) -> p t h c", c=HD),
                                           cos8[:].unsqueeze(2).to_broadcast([P, NT, NH, HD]), ALU.mult))
            for b in range(NB):
                ins = add_rotated(pl, k_tok, swapped, 1, b)
            ins.then_inc(k_rotated, 1)

            pool.wait_ge(yo_ready, NS)
            pl.memset(stack[:], 0.0)
            pool.wait_ge(yo_stored[0], 8 * NS)
            pool.wait_ge(yo_stored[1], 8 * NS)
            for t in range(NT):
                pl.indirect_dma_start(routed[:, t, :], None, sorted_y,
                                      bass.IndirectOffsetOnAxis(ap=slot[:, t:t + 1], axis=0)) \
                  .then_inc(gathered[t // 2], 16)

            pl.memset(v_ones[:], 0.0).then_inc(pads_set, 1)
            pool.wait_ge(pads_set, 1)
            pl.memset(stack[:, :, 2:4, :, SPLIT:SPLIT + 2], 1.0)
            pl.memset(v_ones[:, :, :, :, HD:HD + 1], 1.0)

            def build_group(i, k):
                wait_from_one(pool, query_turned, i + 1 - SLOTS)
                wait_from_one(pool, built, i - 1)
                pl.tensor_copy(current[:, k % 2:k % 2 + 1], rot[:, bass.ds(i, 1)].rearrange("p i w c -> p i (w c)")) \
                  .then_inc(current_ready, 1)
                pool.wait_ge(current_ready, i + 1)
                both = current[:, k % 2].rearrange("p (n g c) -> p n g c", n=4, g=G)
                q, key = both[:, 0:2], both[:, 2:4]
                part = [stack[:, k, :, :, n * HD:(n + 1) * HD] for n in range(3)]
                pl.tensor_tensor(part[0].bitcast(F32R), both,
                                 one_col[:].unsqueeze(1).unsqueeze(2).to_broadcast([P, 4, G, HD]),
                                 ALU.mult)
                pl.tensor_scalar(part[1][:, 0:2].bitcast(F32R), q, 1.0, 1.0, ALU.mult, ALU.mult)
                pl.tensor_scalar(part[2][:, 2:4].bitcast(F32R), key, 1.0, 1.0, ALU.mult, ALU.mult).then_inc(hi_built, 1)
                pool.wait_ge(hi_built, i + 1)
                pl.tensor_tensor(part[2][:, 0:2].bitcast(F32R), q, part[0][:, 0:2], ALU.subtract)
                pl.tensor_tensor(part[1][:, 2:4].bitcast(F32R), key, part[0][:, 2:4], ALU.subtract).then_inc(built, 1)

            def copy_values(i, k):
                wait_from_one(pool, pv_done, G * (i - 1))
                pl.tensor_copy(v_ones[:, k % 2, :, :, 0:HD],
                               v_tok[:, bass.ds(i, 1)].rearrange("p i (n g c) -> p (i n) g c", n=2, g=G)) \
                  .then_inc(v_copied, 1)

            pool.wait_ge(q_rotated, 1)
            for i in range(SLOTS):
                build_group(i, i % SLOTS)
                if i >= 3:
                    copy_values(i - 3, (i - 3) % 2)
            pool.wait_ge(q_rotated, NB)
            for i in range(SLOTS, 2 * SLOTS):
                build_group(i, i % SLOTS)
                copy_values(i - 3, (i - 3) % 2)
                tiles = slice(2 * (i - SLOTS), 2 * (i - SLOTS) + 2)
                pl.tensor_tensor(x_tok[:, tiles], x_tok[:, tiles],
                                 out_b[:].unsqueeze(1).to_broadcast([P, 2, DM]), ALU.add) \
                  .then_inc(bias_added, 1)
            with nc.gpsimd.Fori(2, NG // SLOTS) as m:
                for k in range(SLOTS):
                    build_group(SLOTS * m + k, k)
                    copy_values(SLOTS * m + k - 3, (k - 3) % 2)
            for i in range(NG - 3, NG):
                copy_values(i, i % 2)
            pool.wait_ge(cols_done, G * NG)
            pool.wait_ge(last_w_loaded, 64)
            own.then_wait(pl.tensor_scalar(b_hi[:], b_w, 1.0, 1.0, ALU.mult, ALU.mult))
            pl.tensor_tensor(b_lo[:], b_w, b_hi[:], ALU.subtract).then_inc(b_split, 1)
    return nc


def kernel(x, ctx_1024, fside_BxSx2_0, L0_xattn_in_proj_w, L0_xattn_conv_w, L0_xattn_conv_b, L0_xattn_x_proj_w,
           L0_xattn_dt_proj_w, L0_xattn_dt_proj_b, L0_xattn_A_log, L0_xattn_D, L0_ffn_router_w, L0_ffn_gate_w,
           L0_ffn_up_w, L0_ffn_down_w, L0_ffn_shared_gate_w, L0_ffn_shared_up_w, L0_ffn_shared_down_w,
           L1_xattn_Wq, L1_xattn_Wkv, L1_xattn_Wout, L1_xattn_bout, L1_ffn_A, L1_ffn_B, L1_ffn_Wr, L1_ffn_br):
    import numpy as np
    import concourse.bacc as bacc
    from concourse.bass_utils import run_bass_kernel_spmd

    cat = np.concatenate
    xp = np.asarray(L0_xattn_x_proj_w)
    bc = xp[DR:]
    small = np.zeros((P, 64), np.float32)
    small[:, 32:40] = np.arange(NE) - NE
    small[:, 40:48] = np.arange(NE) * P
    small[:, 48:48 + NS] = np.arange(NS)
    small[:, 0:32] = np.arange(32)[None, :] == (np.arange(P) % 32)[:, None]
    arrays = {
        "x": np.asarray(x),
        "ctxT": np.asarray(ctx_1024).reshape(TOK, DC).T,
        "in_w": np.asarray(L0_xattn_in_proj_w).T,
        "xp_w": cat([bc, bc, bc, xp[:DR]]).T,
        "dt_w": cat([np.zeros((96, DM), np.float32), np.asarray(L0_xattn_dt_proj_w).T]),
        "chan": cat([np.asarray(L0_xattn_conv_w)] + [np.asarray(a)[:, None] for a in
                    (L0_xattn_conv_b, L0_xattn_dt_proj_b, L0_xattn_D)] + [np.asarray(L0_xattn_A_log)], axis=1),
        "pos": np.asarray(fside_BxSx2_0),
        "q_w": np.asarray(L1_xattn_Wq), "kv_w": np.asarray(L1_xattn_Wkv), "out_w": np.asarray(L1_xattn_Wout),
        "out_b": np.asarray(L1_xattn_bout)[None],
        "wr_w": np.asarray(L1_ffn_Wr).T, "br": np.asarray(L1_ffn_br)[None],
        "a_w": np.asarray(L1_ffn_A).reshape(NE * RANK, DM).T,
        "b_w": np.asarray(L1_ffn_B).transpose(0, 2, 1).reshape(NE * RANK, DM),
        "router_w": np.asarray(L0_ffn_router_w),
        "gu_w": cat([cat([np.asarray(L0_ffn_gate_w), np.asarray(L0_ffn_shared_gate_w)[None]]),
                     cat([np.asarray(L0_ffn_up_w), np.asarray(L0_ffn_shared_up_w)[None]])], axis=2),
        "down_w": cat([np.asarray(L0_ffn_down_w), np.asarray(L0_ffn_shared_down_w)[None]]),
        "consts": cat([np.eye(P, dtype=np.float32), np.triu(np.ones((P, P), np.float32), 1), small], axis=1),
    }
    nc = bacc.Bacc("TRN2", target_bir_lowering=False, num_devices=1)
    arrays = {f"in_{k}": np.ascontiguousarray(a) for k, a in arrays.items()}
    handles = {k[3:]: nc.dram_tensor(k, a.shape, mybir.dt.from_np(a.dtype), kind="ExternalInput").ap()
               for k, a in arrays.items()}
    out = nc.dram_tensor("out", (NB, L, DM), F32, kind="ExternalOutput").ap()
    build(nc, handles, out)
    return run_bass_kernel_spmd(nc, [arrays], core_ids=[0]).results[0]["out"]
```
